# Optimizing a Trainium2 kernel written in Bass

```python
import numpy as np
import jax
import jax.numpy as jnp

def _softmax(x, axis=-1):
    return jax.nn.softmax(x, axis=axis)

def _gelu(x):
    return jax.nn.gelu(x, approximate=True)

def _silu(x):
    return jax.nn.silu(x)

def _sigmoid(x):
    return jax.nn.sigmoid(x)

def _layernorm(x, axis=-1, eps=1e-05):
    m = jnp.mean(x, axis=axis, keepdims=True)
    v = jnp.var(x, axis=axis, keepdims=True)
    return (x - m) / jnp.sqrt(v + eps)

def _scatter_add(tgt, idx, src, axis=0):
    return tgt.at[idx].add(src)

def _segment_sum(src, seg, n):
    return jax.ops.segment_sum(src, seg, n)
kernel_name = 'mk_gps_d2_gnn_r8_40cd40'

def setup_inputs(seed: int=0):
    np.random.seed(seed)
    _w = jnp.asarray

    def _rec_inputs():
        import jax
        import jax.numpy as jnp
        _gk = jax.random.key(seed)
        x = -6.415e-05 + 1 * jax.random.normal(jax.random.fold_in(_gk, 1), (1250, 512), jnp.float32)
        src = jax.random.randint(jax.random.fold_in(_gk, 2), (40000,), 0, 1250, jnp.int32)
        dst = jnp.minimum((1250 * jax.random.uniform(jax.random.fold_in(_gk, 3), (40000,)) ** 2.0).astype(jnp.int32), 9999)
        _o = jnp.argsort(dst, stable=True)
        src = src[_o]
        dst = dst[_o]
        edge_attr_8 = 0.000735704 + 1.0001 * jax.random.normal(jax.random.fold_in(_gk, 11), (40000, 8), jnp.float32)
        return (x, src, dst, edge_attr_8)
    x, src, dst, edge_attr_8 = _rec_inputs()

    def _L0_gnn_setup():
        import jax, jax.numpy as jnp
        import numpy as np
        L, E = (2500, 40000)
        C, HID, H = (512, 1024, 8)
        D = C // H
        EPS = 1e-05

        def _layernorm(x, g, b):
            mu = jnp.mean(x, axis=-1, keepdims=True)
            var = jnp.mean(jnp.square(x - mu), axis=-1, keepdims=True)
            return (x - mu) * jax.lax.rsqrt(var + EPS) * g + b
        key = jax.random.key(seed)
        ks = jax.random.split(key, 12)
        s_c = 1.0 / np.sqrt(C)
        s_h = 1.0 / np.sqrt(HID)
        inp = {'x': jax.random.normal(ks[0], (L, C), jnp.float32), 'edge_index': jax.random.randint(ks[1], (2, E), 0, L, jnp.int64), 'att_bias': jax.random.normal(ks[2], (E, H), jnp.float32), 'Wq': jax.random.normal(ks[3], (C, C), jnp.float32) * s_c, 'bq': jnp.zeros((C,), jnp.float32), 'Wk': jax.random.normal(ks[4], (C, C), jnp.float32) * s_c, 'bk': jnp.zeros((C,), jnp.float32), 'Wv': jax.random.normal(ks[5], (C, C), jnp.float32) * s_c, 'bv': jnp.zeros((C,), jnp.float32), 'Wo': jax.random.normal(ks[6], (C, C), jnp.float32) * s_c, 'bo': jnp.zeros((C,), jnp.float32), 'ln_att_g': jnp.ones((C,), jnp.float32), 'ln_att_b': jnp.zeros((C,), jnp.float32), 'ln_ff_g': jnp.ones((C,), jnp.float32), 'ln_ff_b': jnp.zeros((C,), jnp.float32), 'W1': jax.random.normal(ks[7], (HID, C), jnp.float32) * s_c, 'b1': jnp.zeros((HID,), jnp.float32), 'W2': jax.random.normal(ks[8], (C, HID), jnp.float32) * s_h, 'b2': jnp.zeros((C,), jnp.float32)}
        return inp
    _L0_gnn_all = _L0_gnn_setup()
    _L0_gnn_in = {k: v for k, v in _L0_gnn_all.items() if k in ('Wq', 'bq', 'Wk', 'bk', 'Wv', 'bv', 'Wo', 'bo', 'ln_att_g', 'ln_att_b', 'ln_ff_g', 'ln_ff_b', 'W1', 'b1', 'W2', 'b2')}
    del _L0_gnn_all

    def _L0_mix_setup():
        import jax, jax.numpy as jnp
        import numpy as np
        B, L, HID, H, FF = (32, 1024, 512, 8, 256)
        DH = HID // H
        KEPS = 0.001
        LN_EPS = 1e-06

        def _layernorm(x, scale, bias):
            mu = jnp.mean(x, axis=-1, keepdims=True)
            var = jnp.mean(jnp.square(x - mu), axis=-1, keepdims=True)
            return (x - mu) * jax.lax.rsqrt(var + LN_EPS) * scale + bias

        def _favor_bidirectional(q, k, v):
            qp = jax.nn.relu(q) + KEPS
            kp = jax.nn.relu(k) + KEPS
            kv = jnp.einsum('blhm,blhd->bhmd', kp, v)
            num = jnp.einsum('blhm,bhmd->blhd', qp, kv)
            den = jnp.einsum('blhm,bhm->blh', qp, kp.sum(axis=1))
            return num / den[..., None]
        key = jax.random.key(seed)
        ks = jax.random.split(key, 12)
        sa = 1.0 / np.sqrt(HID)
        sf = 1.0 / np.sqrt(FF)
        return {'x': jax.random.normal(ks[0], (B, L, HID), jnp.float32), 'Wq': jax.random.normal(ks[1], (HID, H, DH), jnp.float32) * sa, 'bq': jnp.zeros((H, DH), jnp.float32), 'Wk': jax.random.normal(ks[2], (HID, H, DH), jnp.float32) * sa, 'bk': jnp.zeros((H, DH), jnp.float32), 'Wv': jax.random.normal(ks[3], (HID, H, DH), jnp.float32) * sa, 'bv': jnp.zeros((H, DH), jnp.float32), 'Wo': jax.random.normal(ks[4], (H, DH, HID), jnp.float32) * sa, 'bo': jnp.zeros((HID,), jnp.float32), 'ln1_scale': jnp.ones((HID,), jnp.float32), 'ln1_bias': jnp.zeros((HID,), jnp.float32), 'W1': jax.random.normal(ks[5], (HID, FF), jnp.float32) * sa, 'b1': jnp.zeros((FF,), jnp.float32), 'W2': jax.random.normal(ks[6], (FF, HID), jnp.float32) * sf, 'b2': jnp.zeros((HID,), jnp.float32), 'ln2_scale': jnp.ones((HID,), jnp.float32), 'ln2_bias': jnp.zeros((HID,), jnp.float32)}
    _L0_mix_all = _L0_mix_setup()
    _L0_mix_in = {k: v for k, v in _L0_mix_all.items() if k in ('Wq', 'bq', 'Wk', 'bk', 'Wv', 'bv', 'Wo', 'bo', 'ln1_scale', 'ln1_bias', 'W1', 'b1', 'W2', 'b2', 'ln2_scale', 'ln2_bias')}
    del _L0_mix_all

    def _L0_ffn_setup():
        import jax, jax.numpy as jnp
        import numpy as np
        B, N, DIM = (1, 256, 512)
        DH, H = (64, 8)
        E, FF = (8, 256)

        def _layernorm(x, g, b, eps=1e-05):
            mu = jnp.mean(x, axis=-1, keepdims=True)
            var = jnp.mean(jnp.square(x - mu), axis=-1, keepdims=True)
            return (x - mu) * jax.lax.rsqrt(var + eps) * g + b

        def _l2norm(x, eps=1e-12):
            return x / jnp.sqrt(jnp.sum(jnp.square(x), axis=-1, keepdims=True) + eps)
        key = jax.random.key(seed)
        ks = jax.random.split(key, 12)
        g = lambda k, shape: jax.random.normal(k, shape, jnp.float32) * 0.02
        return {'x': jax.random.normal(ks[0], (B, N, DIM), jnp.float32), 'ln_g': jnp.ones((DIM,), jnp.float32), 'ln_b': jnp.zeros((DIM,), jnp.float32), 'Wq': g(ks[1], (DIM, DIM)), 'Wk': g(ks[2], (DIM, DIM)), 'Wv': g(ks[3], (DIM, DIM)), 'Wo': g(ks[4], (DIM, DIM)), 'qn_g': jnp.ones((DH,), jnp.float32), 'kn_g': jnp.ones((DH,), jnp.float32), 'gate_W': g(ks[5], (DIM, E)), 'gate_b': jnp.zeros((E,), jnp.float32), 'W1': g(ks[6], (E, DIM, FF)), 'b1': jnp.zeros((E, FF), jnp.float32), 'W2': g(ks[7], (E, FF, DIM)), 'b2': jnp.zeros((E, DIM), jnp.float32)}
    _L0_ffn_all = _L0_ffn_setup()
    _L0_ffn_in = {k: v for k, v in _L0_ffn_all.items() if k in ('ln_g', 'ln_b', 'Wq', 'Wk', 'Wv', 'Wo', 'qn_g', 'kn_g', 'gate_W', 'gate_b', 'W1', 'b1', 'W2', 'b2')}
    del _L0_ffn_all

    def _L1_gnn_setup():
        import jax, jax.numpy as jnp
        import numpy as np
        N_NODES = 12500
        N_EDGES = 100000
        DIM = 512
        key = jax.random.key(seed)
        k1, k2, k3, k4 = jax.random.split(key, 4)
        scale = 1.0 / np.sqrt(DIM)
        embedding = jax.random.normal(k1, (N_NODES, DIM), dtype=jnp.float32)
        edge_index = jax.random.randint(k2, (2, N_EDGES), 0, N_NODES, dtype=jnp.int64)
        W_gcn = jax.random.normal(k3, (DIM, DIM), dtype=jnp.float32) * scale
        b_gcn = jnp.zeros((DIM,), dtype=jnp.float32)
        W_dense = jax.random.normal(k4, (DIM, DIM), dtype=jnp.float32) * scale
        b_dense = jnp.zeros((DIM,), dtype=jnp.float32)
        return {'embedding': embedding, 'edge_index': edge_index, 'W_gcn': W_gcn, 'b_gcn': b_gcn, 'W_dense': W_dense, 'b_dense': b_dense}
    _L1_gnn_all = _L1_gnn_setup()
    _L1_gnn_in = {k: v for k, v in _L1_gnn_all.items() if k in ('W_gcn', 'b_gcn', 'W_dense', 'b_dense')}
    del _L1_gnn_all

    def _L1_mix_setup():
        import jax, jax.numpy as jnp
        import numpy as np
        B, N, C = (8, 512, 512)
        H = 8
        HD = C // H
        SCALE = HD ** (-0.5)
        key = jax.random.key(seed)
        ks = jax.random.split(key, 6)
        x = jax.random.normal(ks[0], (B, N, C), dtype=jnp.float32)
        w_qkv = jax.random.normal(ks[1], (3 * C, C), dtype=jnp.float32) * C ** (-0.5)
        w_proj = jax.random.normal(ks[2], (C, C), dtype=jnp.float32) * C ** (-0.5)
        b_proj = jnp.zeros((C,), dtype=jnp.float32)
        w_q = jax.random.normal(ks[3], (H, HD), dtype=jnp.float32)
        w_k = jax.random.normal(ks[4], (H, HD), dtype=jnp.float32)
        return {'x': x, 'w_qkv': w_qkv, 'w_proj': w_proj, 'b_proj': b_proj, 'w_q': w_q, 'w_k': w_k}
    _L1_mix_all = _L1_mix_setup()
    _L1_mix_in = {k: v for k, v in _L1_mix_all.items() if k in ('w_qkv', 'w_proj', 'b_proj', 'w_q', 'w_k')}
    del _L1_mix_all

    def _L1_ffn_setup():
        import jax, jax.numpy as jnp
        import numpy as np
        DIM = 512
        HEADS = 8
        DIM_KEY = 32
        NUM_EXPERTS = 8192
        NUM_KEYS = 256
        TOPK = 16
        BN_EPS = 1e-05

        def peer_forward(x, w_q, keys, weight_down_embed, weight_up_embed):
            b, n, _ = x.shape
            q = x @ w_q * (1.0 / np.sqrt(1.0 + BN_EPS))
            queries = q.reshape(b, n, 2, HEADS, DIM_KEY).transpose(2, 0, 1, 3, 4)
            sim = jnp.einsum('pbnhd,hkpd->pbnhk', queries, keys)
            v0, i0 = jax.lax.top_k(sim[0], TOPK)
            v1, i1 = jax.lax.top_k(sim[1], TOPK)
            all_scores = v0[..., :, None] + i0[..., None, :].astype(v0.dtype)
            all_scores = all_scores.reshape(*all_scores.shape[:-2], -1)
            scores, pk_indices = jax.lax.top_k(all_scores, TOPK)
            weights_down = jnp.take(weight_down_embed, pk_indices, axis=0)
            weights_up = jnp.take(weight_up_embed, pk_indices, axis=0)
            h = jnp.einsum('bnd,bnhkd->bnhk', q, weights_down)
            h = jax.nn.gelu(h)
            h = h * jax.nn.softmax(scores, axis=-1)
            out = jnp.einsum('bnhk,bnhkd->bnd', h, weights_up)
            return out
        key = jax.random.key(seed)
        k1, k2, k3, k4, k5 = jax.random.split(key, 5)
        b, n = (2, 512)
        x = jax.random.normal(k1, (b, n, DIM), dtype=jnp.float32)
        w_q = jax.random.normal(k2, (DIM, DIM_KEY * HEADS * 2), dtype=jnp.float32) / np.sqrt(DIM)
        keys = jax.random.normal(k3, (HEADS, NUM_KEYS, 2, DIM_KEY), dtype=jnp.float32) * 0.01
        weight_down_embed = jax.random.normal(k4, (NUM_EXPERTS, DIM), dtype=jnp.float32) * 0.01
        weight_up_embed = jax.random.normal(k5, (NUM_EXPERTS, DIM), dtype=jnp.float32) * 0.01
        return {'x': x, 'w_q': w_q, 'keys': keys, 'weight_down_embed': weight_down_embed, 'weight_up_embed': weight_up_embed}
    _L1_ffn_all = _L1_ffn_setup()
    _L1_ffn_in = {k: v for k, v in _L1_ffn_all.items() if k in ('w_q', 'keys', 'weight_down_embed', 'weight_up_embed')}
    del _L1_ffn_all
    return {'x': x, 'src': src, 'dst': dst, 'edge_attr_8': edge_attr_8, 'L0_gnn_Wq': _L0_gnn_in['Wq'], 'L0_gnn_bq': _L0_gnn_in['bq'], 'L0_gnn_Wk': _L0_gnn_in['Wk'], 'L0_gnn_bk': _L0_gnn_in['bk'], 'L0_gnn_Wv': _L0_gnn_in['Wv'], 'L0_gnn_bv': _L0_gnn_in['bv'], 'L0_gnn_Wo': _L0_gnn_in['Wo'], 'L0_gnn_bo': _L0_gnn_in['bo'], 'L0_gnn_ln_att_g': _L0_gnn_in['ln_att_g'], 'L0_gnn_ln_att_b': _L0_gnn_in['ln_att_b'], 'L0_gnn_ln_ff_g': _L0_gnn_in['ln_ff_g'], 'L0_gnn_ln_ff_b': _L0_gnn_in['ln_ff_b'], 'L0_gnn_W1': _L0_gnn_in['W1'], 'L0_gnn_b1': _L0_gnn_in['b1'], 'L0_gnn_W2': _L0_gnn_in['W2'], 'L0_gnn_b2': _L0_gnn_in['b2'], 'L0_mix_Wq': _L0_mix_in['Wq'], 'L0_mix_bq': _L0_mix_in['bq'], 'L0_mix_Wk': _L0_mix_in['Wk'], 'L0_mix_bk': _L0_mix_in['bk'], 'L0_mix_Wv': _L0_mix_in['Wv'], 'L0_mix_bv': _L0_mix_in['bv'], 'L0_mix_Wo': _L0_mix_in['Wo'], 'L0_mix_bo': _L0_mix_in['bo'], 'L0_mix_ln1_scale': _L0_mix_in['ln1_scale'], 'L0_mix_ln1_bias': _L0_mix_in['ln1_bias'], 'L0_mix_W1': _L0_mix_in['W1'], 'L0_mix_b1': _L0_mix_in['b1'], 'L0_mix_W2': _L0_mix_in['W2'], 'L0_mix_b2': _L0_mix_in['b2'], 'L0_mix_ln2_scale': _L0_mix_in['ln2_scale'], 'L0_mix_ln2_bias': _L0_mix_in['ln2_bias'], 'L0_ffn_ln_g': _L0_ffn_in['ln_g'], 'L0_ffn_ln_b': _L0_ffn_in['ln_b'], 'L0_ffn_Wq': _L0_ffn_in['Wq'], 'L0_ffn_Wk': _L0_ffn_in['Wk'], 'L0_ffn_Wv': _L0_ffn_in['Wv'], 'L0_ffn_Wo': _L0_ffn_in['Wo'], 'L0_ffn_qn_g': _L0_ffn_in['qn_g'], 'L0_ffn_kn_g': _L0_ffn_in['kn_g'], 'L0_ffn_gate_W': _L0_ffn_in['gate_W'], 'L0_ffn_gate_b': _L0_ffn_in['gate_b'], 'L0_ffn_W1': _L0_ffn_in['W1'], 'L0_ffn_b1': _L0_ffn_in['b1'], 'L0_ffn_W2': _L0_ffn_in['W2'], 'L0_ffn_b2': _L0_ffn_in['b2'], 'L1_gnn_W_gcn': _L1_gnn_in['W_gcn'], 'L1_gnn_b_gcn': _L1_gnn_in['b_gcn'], 'L1_gnn_W_dense': _L1_gnn_in['W_dense'], 'L1_gnn_b_dense': _L1_gnn_in['b_dense'], 'L1_mix_w_qkv': _L1_mix_in['w_qkv'], 'L1_mix_w_proj': _L1_mix_in['w_proj'], 'L1_mix_b_proj': _L1_mix_in['b_proj'], 'L1_mix_w_q': _L1_mix_in['w_q'], 'L1_mix_w_k': _L1_mix_in['w_k'], 'L1_ffn_w_q': _L1_ffn_in['w_q'], 'L1_ffn_keys': _L1_ffn_in['keys'], 'L1_ffn_weight_down_embed': _L1_ffn_in['weight_down_embed'], 'L1_ffn_weight_up_embed': _L1_ffn_in['weight_up_embed']}

def reference(x, src, dst, edge_attr_8, L0_gnn_Wq, L0_gnn_bq, L0_gnn_Wk, L0_gnn_bk, L0_gnn_Wv, L0_gnn_bv, L0_gnn_Wo, L0_gnn_bo, L0_gnn_ln_att_g, L0_gnn_ln_att_b, L0_gnn_ln_ff_g, L0_gnn_ln_ff_b, L0_gnn_W1, L0_gnn_b1, L0_gnn_W2, L0_gnn_b2, L0_mix_Wq, L0_mix_bq, L0_mix_Wk, L0_mix_bk, L0_mix_Wv, L0_mix_bv, L0_mix_Wo, L0_mix_bo, L0_mix_ln1_scale, L0_mix_ln1_bias, L0_mix_W1, L0_mix_b1, L0_mix_W2, L0_mix_b2, L0_mix_ln2_scale, L0_mix_ln2_bias, L0_ffn_ln_g, L0_ffn_ln_b, L0_ffn_Wq, L0_ffn_Wk, L0_ffn_Wv, L0_ffn_Wo, L0_ffn_qn_g, L0_ffn_kn_g, L0_ffn_gate_W, L0_ffn_gate_b, L0_ffn_W1, L0_ffn_b1, L0_ffn_W2, L0_ffn_b2, L1_gnn_W_gcn, L1_gnn_b_gcn, L1_gnn_W_dense, L1_gnn_b_dense, L1_mix_w_qkv, L1_mix_w_proj, L1_mix_b_proj, L1_mix_w_q, L1_mix_w_k, L1_ffn_w_q, L1_ffn_keys, L1_ffn_weight_down_embed, L1_ffn_weight_up_embed):
    import jax
    import jax.numpy as jnp

    def _L0_gnn_ref(x, edge_index, att_bias, Wq, bq, Wk, bk, Wv, bv, Wo, bo, ln_att_g, ln_att_b, ln_ff_g, ln_ff_b, W1, b1, W2, b2):
        import jax, jax.numpy as jnp
        import numpy as np
        L, E = (2500, 40000)
        C, HID, H = (512, 1024, 8)
        D = C // H
        EPS = 1e-05

        def _layernorm(x, g, b):
            mu = jnp.mean(x, axis=-1, keepdims=True)
            var = jnp.mean(jnp.square(x - mu), axis=-1, keepdims=True)
            return (x - mu) * jax.lax.rsqrt(var + EPS) * g + b
        n = x.shape[0]
        src = edge_index[0]
        dst = edge_index[1]
        z = _layernorm(x, ln_att_g, ln_att_b)
        q = (z @ Wq.T + bq).reshape(n, H, D)
        k = (z @ Wk.T + bk).reshape(n, H, D)
        v = (z @ Wv.T + bv).reshape(n, H, D)
        s = jnp.einsum('ehd,ehd->eh', q[src], k[dst]) / np.sqrt(D) + att_bias
        m = jax.ops.segment_max(s, src, num_segments=n)
        p = jnp.exp(s - m[src])
        denom = jax.ops.segment_sum(p, src, num_segments=n)
        alpha = p / jnp.where(denom[src] == 0, 1.0, denom[src])
        agg = jax.ops.segment_sum(alpha[:, :, None] * v[dst], src, num_segments=n)
        att = agg.reshape(n, C) @ Wo.T + bo
        x = x + att
        z = _layernorm(x, ln_ff_g, ln_ff_b)
        h = jax.nn.silu(z @ W1.T + b1)
        ff = h @ W2.T + b2
        return x + ff

    def _L0_mix_ref(x, Wq, bq, Wk, bk, Wv, bv, Wo, bo, ln1_scale, ln1_bias, W1, b1, W2, b2, ln2_scale, ln2_bias):
        import jax, jax.numpy as jnp
        import numpy as np
        B, L, HID, H, FF = (32, 1024, 512, 8, 256)
        DH = HID // H
        KEPS = 0.001
        LN_EPS = 1e-06

        def _layernorm(x, scale, bias):
            mu = jnp.mean(x, axis=-1, keepdims=True)
            var = jnp.mean(jnp.square(x - mu), axis=-1, keepdims=True)
            return (x - mu) * jax.lax.rsqrt(var + LN_EPS) * scale + bias

        def _favor_bidirectional(q, k, v):
            qp = jax.nn.relu(q) + KEPS
            kp = jax.nn.relu(k) + KEPS
            kv = jnp.einsum('blhm,blhd->bhmd', kp, v)
            num = jnp.einsum('blhm,bhmd->blhd', qp, kv)
            den = jnp.einsum('blhm,bhm->blh', qp, kp.sum(axis=1))
            return num / den[..., None]
        q = jnp.einsum('blc,chd->blhd', x, Wq) + bq
        k = jnp.einsum('blc,chd->blhd', x, Wk) + bk
        v = jnp.einsum('blc,chd->blhd', x, Wv) + bv
        attn = _favor_bidirectional(q, k, v)
        attended = jnp.einsum('blhd,hdc->blc', attn, Wo) + bo
        h = _layernorm(attended + x, ln1_scale, ln1_bias)
        ff = jax.nn.relu(h @ W1 + b1) @ W2 + b2
        return _layernorm(ff + h, ln2_scale, ln2_bias)

    def _L0_ffn_ref(x, ln_g, ln_b, Wq, Wk, Wv, Wo, qn_g, kn_g, gate_W, gate_b, W1, b1, W2, b2):
        import jax, jax.numpy as jnp
        import numpy as np
        B, N, DIM = (1, 256, 512)
        DH, H = (64, 8)
        E, FF = (8, 256)

        def _layernorm(x, g, b, eps=1e-05):
            mu = jnp.mean(x, axis=-1, keepdims=True)
            var = jnp.mean(jnp.square(x - mu), axis=-1, keepdims=True)
            return (x - mu) * jax.lax.rsqrt(var + eps) * g + b

        def _l2norm(x, eps=1e-12):
            return x / jnp.sqrt(jnp.sum(jnp.square(x), axis=-1, keepdims=True) + eps)
        b, n, d = x.shape
        dh = qn_g.shape[0]
        h = d // dh
        hx = _layernorm(x, ln_g, ln_b)
        q = (hx @ Wq).reshape(b, n, h, dh).transpose(0, 2, 1, 3)
        k = (hx @ Wk).reshape(b, n, h, dh).transpose(0, 2, 1, 3)
        v = (hx @ Wv).reshape(b, n, h, dh).transpose(0, 2, 1, 3)
        scale = jnp.sqrt(jnp.float32(dh))
        q = _l2norm(q) * scale * qn_g
        k = _l2norm(k) * scale * kn_g
        scores = jnp.einsum('bhqd,bhkd->bhqk', q, k) * dh ** (-0.5)
        causal = jnp.tril(jnp.ones((n, n), bool))
        scores = jnp.where(causal, scores, jnp.finfo(scores.dtype).min)
        attn = jax.nn.softmax(scores, axis=-1)
        o = jnp.einsum('bhqk,bhkd->bhqd', attn, v)
        y = o.transpose(0, 2, 1, 3).reshape(b, n, d) @ Wo
        gate = jax.nn.softmax(y @ gate_W + gate_b, axis=-1)
        hid = jax.nn.gelu(jnp.einsum('bnd,edf->bnef', y, W1) + b1)
        eo = jnp.einsum('bnef,efd->bned', hid, W2) + b2
        out = jnp.einsum('bned,bne->bnd', eo, gate)
        return out

    def _L1_gnn_ref(embedding, edge_index, W_gcn, b_gcn, W_dense, b_dense):
        import jax, jax.numpy as jnp
        import numpy as np
        N_NODES = 12500
        N_EDGES = 100000
        DIM = 512
        N = embedding.shape[0]
        loop = jnp.arange(N, dtype=edge_index.dtype)
        src = jnp.concatenate([edge_index[0], loop])
        dst = jnp.concatenate([edge_index[1], loop])
        deg = jax.ops.segment_sum(jnp.ones_like(dst, dtype=embedding.dtype), dst, num_segments=N)
        dinv = jnp.where(deg > 0, jax.lax.rsqrt(deg), 0.0)
        norm = dinv[src] * dinv[dst]
        h = embedding @ W_gcn
        msg = h[src] * norm[:, None]
        agg = jax.ops.segment_sum(msg, dst, num_segments=N) + b_gcn
        return agg @ W_dense + b_dense

    def _L1_mix_ref(x, w_qkv, w_proj, b_proj, w_q, w_k):
        import jax, jax.numpy as jnp
        import numpy as np
        B, N, C = (8, 512, 512)
        H = 8
        HD = C // H
        SCALE = HD ** (-0.5)
        b, n, c = x.shape
        qkv = jnp.einsum('bnc,dc->bnd', x, w_qkv)
        qkv = qkv.reshape(b, n, 3, H, HD).transpose(2, 0, 3, 1, 4)
        q, k, v = (qkv[0], qkv[1], qkv[2])
        alpha = jax.nn.softmax(jnp.einsum('bhnc,hc->bhn', q, w_q) * SCALE, axis=-1)
        global_q = jnp.einsum('bhn,bhnc->bhc', alpha, q)
        p = global_q[:, :, None, :] * k
        beta = jax.nn.softmax(jnp.einsum('bhnc,hc->bhn', p, w_k) * SCALE, axis=-1)
        global_k = jnp.einsum('bhn,bhnc->bhc', beta, k)
        u = global_k[:, :, None, :] * v
        u_flat = u.transpose(0, 2, 1, 3).reshape(b, n, c)
        q_flat = q.transpose(0, 2, 1, 3).reshape(b, n, c)
        out = jnp.einsum('bnc,dc->bnd', u_flat, w_proj) + b_proj + q_flat
        return out

    def _L1_ffn_ref(x, w_q, keys, weight_down_embed, weight_up_embed):
        import jax, jax.numpy as jnp
        import numpy as np
        DIM = 512
        HEADS = 8
        DIM_KEY = 32
        NUM_EXPERTS = 8192
        NUM_KEYS = 256
        TOPK = 16
        BN_EPS = 1e-05

        def peer_forward(x, w_q, keys, weight_down_embed, weight_up_embed):
            b, n, _ = x.shape
            q = x @ w_q * (1.0 / np.sqrt(1.0 + BN_EPS))
            queries = q.reshape(b, n, 2, HEADS, DIM_KEY).transpose(2, 0, 1, 3, 4)
            sim = jnp.einsum('pbnhd,hkpd->pbnhk', queries, keys)
            v0, i0 = jax.lax.top_k(sim[0], TOPK)
            v1, i1 = jax.lax.top_k(sim[1], TOPK)
            all_scores = v0[..., :, None] + i0[..., None, :].astype(v0.dtype)
            all_scores = all_scores.reshape(*all_scores.shape[:-2], -1)
            scores, pk_indices = jax.lax.top_k(all_scores, TOPK)
            weights_down = jnp.take(weight_down_embed, pk_indices, axis=0)
            weights_up = jnp.take(weight_up_embed, pk_indices, axis=0)
            h = jnp.einsum('bnd,bnhkd->bnhk', q, weights_down)
            h = jax.nn.gelu(h)
            h = h * jax.nn.softmax(scores, axis=-1)
            out = jnp.einsum('bnhk,bnhkd->bnd', h, weights_up)
            return out
        return peer_forward(x, w_q, keys, weight_down_embed, weight_up_embed)
    edge_index = jnp.stack([src, dst])
    xn = _layernorm(x, axis=-1)
    x = x + _L0_gnn_ref(xn, edge_index, edge_attr_8, L0_gnn_Wq, L0_gnn_bq, L0_gnn_Wk, L0_gnn_bk, L0_gnn_Wv, L0_gnn_bv, L0_gnn_Wo, L0_gnn_bo, L0_gnn_ln_att_g, L0_gnn_ln_att_b, L0_gnn_ln_ff_g, L0_gnn_ln_ff_b, L0_gnn_W1, L0_gnn_b1, L0_gnn_W2, L0_gnn_b2) + _L0_mix_ref(xn[None], L0_mix_Wq, L0_mix_bq, L0_mix_Wk, L0_mix_bk, L0_mix_Wv, L0_mix_bv, L0_mix_Wo, L0_mix_bo, L0_mix_ln1_scale, L0_mix_ln1_bias, L0_mix_W1, L0_mix_b1, L0_mix_W2, L0_mix_b2, L0_mix_ln2_scale, L0_mix_ln2_bias)[0]
    x = x + _L0_ffn_ref(_layernorm(x, axis=-1)[None], L0_ffn_ln_g, L0_ffn_ln_b, L0_ffn_Wq, L0_ffn_Wk, L0_ffn_Wv, L0_ffn_Wo, L0_ffn_qn_g, L0_ffn_kn_g, L0_ffn_gate_W, L0_ffn_gate_b, L0_ffn_W1, L0_ffn_b1, L0_ffn_W2, L0_ffn_b2)[0]
    xn = _layernorm(x, axis=-1)
    x = x + _L1_gnn_ref(xn, edge_index, L1_gnn_W_gcn, L1_gnn_b_gcn, L1_gnn_W_dense, L1_gnn_b_dense) + _L1_mix_ref(xn[None], L1_mix_w_qkv, L1_mix_w_proj, L1_mix_b_proj, L1_mix_w_q, L1_mix_w_k)[0]
    x = x + _L1_ffn_ref(_layernorm(x, axis=-1)[None], L1_ffn_w_q, L1_ffn_keys, L1_ffn_weight_down_embed, L1_ffn_weight_up_embed)[0]
    return x

_drawn_inputs = setup_inputs


def setup_inputs(seed=0):
    import zlib

    import numpy as np

    out = dict(_drawn_inputs(seed))
    spreads = {'L0_gnn_bq': (0.0, 0.567),
     'L0_gnn_bk': (0.0, 2.0),
     'L0_gnn_bv': (0.0, 0.1),
     'L0_gnn_bo': (0.0, 0.1),
     'L0_gnn_ln_att_g': (1.0, 0.2),
     'L0_gnn_ln_att_b': (0.0, 0.1),
     'L0_gnn_ln_ff_g': (1.0, 0.2),
     'L0_gnn_ln_ff_b': (0.0, 0.34),
     'L0_gnn_b1': (0.0, 0.338),
     'L0_gnn_b2': (0.0, 0.1),
     'L0_mix_bq': (0.0, 2.0),
     'L0_mix_bk': (0.0, 2.0),
     'L0_mix_bv': (0.0, 0.1),
     'L0_mix_bo': (0.0, 0.1),
     'L0_mix_ln1_scale': (1.0, 0.2),
     'L0_mix_ln1_bias': (0.0, 0.1),
     'L0_mix_b1': (0.0, 0.373),
     'L0_mix_b2': (0.0, 0.1),
     'L0_mix_ln2_scale': (1.0, 0.2),
     'L0_mix_ln2_bias': (0.0, 0.1),
     'L0_ffn_ln_g': (1.0, 0.6),
     'L0_ffn_ln_b': (0.0, 0.8),
     'L0_ffn_qn_g': (1.0, 0.6),
     'L0_ffn_kn_g': (1.0, 0.6),
     'L0_ffn_gate_b': (0.0, 0.8),
     'L0_ffn_b1': (0.0, 2.0),
     'L0_ffn_b2': (0.0, 2.0),
     'L1_gnn_b_gcn': (0.0, 0.8),
     'L1_gnn_b_dense': (0.0, 2.0),
     'L1_mix_b_proj': (0.0, 2.0)}
    factors = {'L0_mix_Wq': 8.0,
     'L0_mix_Wk': 8.0,
     'L0_mix_Wv': 4.817,
     'L0_ffn_Wq': 8.0,
     'L0_ffn_Wk': 8.0,
     'L0_ffn_Wv': 8.0,
     'L0_ffn_Wo': 8.0,
     'L0_ffn_gate_W': 8.0,
     'L0_ffn_W1': 8.0,
     'L0_ffn_W2': 8.0,
     'L1_ffn_w_q': 24.485,
     'L1_ffn_keys': 31.218,
     'L1_ffn_weight_down_embed': 31.111,
     'L1_ffn_weight_up_embed': 27.072,
     'L1_gnn_W_gcn': 5.766,
     'L1_gnn_W_dense': 6.017,
     'L1_mix_w_qkv': 3.603,
     'L1_mix_w_proj': 6.199,
     'L1_mix_w_q': 8.0,
     'L1_mix_w_k': 8.0}
    for name, (base, spread) in spreads.items():
        noise = np.random.default_rng([zlib.crc32(name.encode()), seed]).standard_normal(out[name].shape)
        drawn = base * np.exp(spread * noise) if base else spread * noise
        out[name] = jnp.asarray(drawn.astype(out[name].dtype))
    for name, factor in factors.items():
        out[name] = (out[name] * factor).astype(out[name].dtype)
    return out
```

```python
from contextlib import ExitStack

import concourse.bass as bass
from concourse import mybir

ALU = mybir.AluOpType
ACT = mybir.ActivationFunctionType
AX_X = mybir.AxisListType.X
F32 = mybir.dt.float32
I32 = mybir.dt.int32
U32 = mybir.dt.uint32

NODES = 1250
TP = 125
TILES = NODES // TP
C = 512
KC = C // 128
HEADS = 8
DH = C // HEADS
PAIRS = HEADS // 2
EDGES = 40000
EC = EDGES // TP
GE = 4
GROUPS = EC // GE
ROW = HEADS + 1
CELLS = NODES * NODES
TABLE_ROWS = CELLS + GE * TP
HID = 1024
FF = 256
EXPERTS = 8
KEYS = 256
TOPK = 16
NEG = -1.0e30
LOWEST = -3.0e38
BANK = 512
SLOT = 5120


def gps_two_layers(nc, d):
    ctx = ExitStack()
    with ctx:
        def sem(name):
            return ctx.enter_context(nc.semaphore(name))

        TOP = 53200
        arena = ctx.enter_context(nc.sbuf_tensor("arena", [128, TOP], F32))
        banks = ctx.enter_context(nc.psum_tensor("banks", [128, 8 * BANK], F32))

        class Space:

            def __init__(self, at, end):
                self.at, self.end = at, end

            def take(self, n):
                self.at += n
                assert self.at <= self.end, (self.at, self.end)
                return arena[:, self.at - n:self.at]

        def bank(b, n=1):
            return banks[:, b * BANK:(b + n) * BANK]

        def rows(flat):
            return flat.rearrange("p (t c) -> p t c", c=C)

        def cols(flat, k=KC):
            return flat[:, 0:k * NODES].rearrange("p (k n) -> p k n", k=k)

        def chunks(flat, n=TP, k=KC):
            return flat[:, 0:k * n].rearrange("p (k n) -> p k n", k=k)

        def tok(t, n=1):
            return slice(t * TP, (t + n) * TP)

        X = rows(arena[:, 0:SLOT])
        XN = rows(arena[:, SLOT:2 * SLOT])
        slot = [arena[:, (2 + i) * SLOT:(3 + i) * SLOT] for i in range(4)]
        BIG = 6 * SLOT
        SMALL = 42480
        const = Space(SMALL, TOP)
        ident = const.take(128)
        ones = const.take(128)
        lnv = const.take(160)
        bn6 = lnv[:, 0:60].rearrange("p (t s) -> p t s", s=6)
        mv = lnv[:, 60:80].rearrange("p (t s) -> p t s", s=2)
        var_eps, sd, r0, ra, rstd = (lnv[:, 80 + 16 * i:80 + 16 * i + TILES] for i in range(5))
        BUF = const.at

        s_dve = sem("dve_step")
        s_act = sem("act_step")
        s_var = sem("ln_variances_ready")
        s_sd = sem("ln_deviations_ready")
        s_stage = sem("stage_left")
        s_const = sem("constants_ready")
        s_x = sem("x_loaded")
        s_zeroed = sem("buffer_zeroed")
        s_xn = sem("xn_ready")
        steps = {"dve": 0, "act": 0, "var": 0, "sd": 0, "PE": 0, "ACT": 0, "DVE": 0}

        def link(dve, ins):
            steps["dve"] += 1
            ins.then_inc(s_dve, 1)
            dve.wait_ge(s_dve, steps["dve"])

        def act_link(act, ins):
            steps["act"] += 1
            ins.then_inc(s_act, 1)
            act.wait_ge(s_act, steps["act"])

        def leave_stage(eng, name):
            steps[name] += 1
            eng.drain().then_inc(s_stage, 1)
            eng.wait_ge(s_stage, 3 * steps[name])

        def inverse_root_dve(dve, src, eps):
            steps["var"] += 1
            nc.vector.tensor_scalar(var_eps[0:TP, :], src, eps, None, ALU.add).then_inc(s_var, 1)
            dve.wait_ge(s_var, steps["var"])
            dve.wait_ge(s_sd, steps["var"])
            link(dve, nc.vector.reciprocal(r0[0:TP, :], sd[0:TP, :]))
            link(dve, nc.vector.tensor_tensor(ra[0:TP, :], var_eps[0:TP, :], r0[0:TP, :], ALU.mult))
            link(dve, nc.vector.tensor_tensor(ra[0:TP, :], ra[0:TP, :], r0[0:TP, :], ALU.mult))
            link(dve, nc.vector.tensor_scalar(ra[0:TP, :], ra[0:TP, :], -0.5, 1.5, ALU.mult, ALU.add))
            link(dve, nc.vector.tensor_tensor(rstd[0:TP, :], r0[0:TP, :], ra[0:TP, :], ALU.mult))

        def ln_stats_dve(dve, src, eps):
            for t in range(TILES):
                last = nc.vector.bn_stats(bn6[0:TP, t, :], src[0:TP, t, :])
            link(dve, last)
            for t in range(TILES):
                last = nc.vector.bn_aggr(mv[0:TP, t, :], bn6[0:TP, t, :])
            link(dve, last)
            inverse_root_dve(dve, mv[0:TP, :, 1], eps)

        def ln_stats_act(act):
            steps["sd"] += 1
            act.wait_ge(s_var, steps["sd"])
            nc.scalar.activation(sd[0:TP, :], var_eps[0:TP, :], ACT.Sqrt).then_inc(s_sd, 1)

        def normalize(dst, src, t):
            return nc.vector.tensor_scalar(dst, src, mv[0:TP, t, 0:1], rstd[0:TP, t:t + 1],
                                           ALU.subtract, ALU.mult)

        def transpose_tile(dst, src):
            for k in range(KC):
                last = nc.tensor.transpose(dst[:, k, :], src[:, k * 128:(k + 1) * 128], ident[0:TP, 0:TP])
            return last

        def project(dst, xT, w, n=C, k=KC):
            for i in range(k):
                last = nc.tensor.matmul(dst, xT[:, i, :], w[:, i, 0:n], start=(i == 0), stop=(i == k - 1))
            return last

        def load(eng, dst, name, s):
            src = d[name]
            if src.shape[0] == 1:
                src = src[0].partition_broadcast(128)
            eng.dma_start(dst, src).then_inc(s, 16)

        programs = {"SP": [], "PE": [], "ACT": [], "DVE": [], "POOL": []}

        space = Space(BUF, TOP)
        zeros = space.take(2250)

        UG = 4
        s_zero = sem("zeros_ready")
        s_table0 = sem("table_zeroed")
        edge = Space(36864, SMALL)
        vals = edge.take(EC * ROW)
        key = edge.take(EC)
        cell = edge.take(EC)
        later = edge.take(GE * TP)
        spill = edge.take(2 * GE)
        bias = slot[0]
        src_i, dst_i, dst_f = (slot[1][:, i * EC:(i + 1) * EC] for i in range(3))
        hmax = space.take(48)
        vg = [space.take(GE * ROW) for _ in range(UG)]
        first = [space.take(2 * GE) for _ in range(UG)]
        diag = [space.take(GE * TP) for _ in range(UG)]
        same = [space.take(TP * (1 + 2 + 3 + 4)) for _ in range(UG)]
        s_sd_in = sem("edge_ends_loaded")
        s_bias = sem("edge_bias_loaded")
        s_key = sem("keys_ready")
        s_pmax = sem("partition_maxima_ready")
        s_tmax = sem("maxima_transposed")
        s_hmax = sem("head_maxima_ready")
        s_bmax = sem("head_maxima_spread")
        s_shift = sem("bias_shifted")
        s_grp = sem("group_copied")
        s_diag = sem("group_keys_on_diagonals")
        s_keyrow = sem("group_keys_spread")
        s_same = sem("equal_keys_marked")
        s_first = sem("repeats_counted")
        s_sum = sem("repeats_summed")
        s_group = sem("group_done")
        s_scat = sem("group_scattered")

        def const_pool(pool):
            nc.gpsimd.memset(zeros, 0.0).then_inc(s_zero, 1)
            nc.gpsimd.memset(ident, 0.0)
            nc.gpsimd.memset(ones, 1.0)
            nc.gpsimd.iota(spill[0:TP, 0:GE].bitcast(I32), pattern=[[TP, GE]], base=CELLS,
                           channel_multiplier=1)
            nc.gpsimd.memset(later, 1.0).then_inc(s_zero, 1)
            pool.wait_ge(s_zero, 2)
            nc.gpsimd.affine_select(out=ident, in_=ident, compare_op=ALU.not_equal, fill=1.0, base=0,
                                    pattern=[[-1, 128]], channel_multiplier=1)
            own = later[0:TP, (GE - 1) * TP:GE * TP]
            nc.gpsimd.affine_select(out=own, in_=own, compare_op=ALU.is_gt, fill=0.0, base=0,
                                    pattern=[[-1, TP]], channel_multiplier=1).then_inc(s_const, 1)

        def const_sp(sp):
            sp.dma_start(src_i[0:TP, :].bitcast(I32), d["src"]).then_inc(s_sd_in, 16)
            sp.dma_start(dst_i[0:TP, :].bitcast(I32), d["dst"]).then_inc(s_sd_in, 16)
            sp.dma_start(bias[0:TP, 0:EC * HEADS], d["edge_attr_8"]).then_inc(s_bias, 16)
            sp.dma_start(X[0:TP, :, :], d["x"].rearrange("(t p) c -> p t c", p=TP)).then_inc(s_x, 16)

        def zero_table(sp):
            sp.wait_ge(s_zero, 1)
            flat = d["table"].rearrange("r w -> (r w)")
            n = TP * zeros.shape[1]
            sp.dma_start(flat[CELLS * ROW:TABLE_ROWS * ROW].rearrange("(p a) -> p a", p=TP),
                         zeros[0:TP, 0:GE * ROW]).then_inc(s_table0, 16)
            with sp.Fori(0, CELLS * ROW // n) as i:
                sp.dma_start(flat[bass.ds(i * n, n)].rearrange("(p a) -> p a", p=TP),
                             zeros[0:TP, :]).then_inc(s_table0, 16)
            return 16 * (CELLS * ROW // n + 1)

        TABLE_ZEROED = 16 * (CELLS * ROW // (TP * 2250) + 1)

        def edges_dve(dve):
            dve.wait_ge(s_sd_in, 32)
            dve.wait_ge(s_const, 1)
            nc.vector.tensor_copy(key[0:TP, :], src_i[0:TP, :].bitcast(I32))
            nc.vector.tensor_copy(spill[0:TP, GE:2 * GE], spill[0:TP, 0:GE].bitcast(I32))
            link(dve, nc.vector.tensor_copy(dst_f[0:TP, :], dst_i[0:TP, :].bitcast(I32)))
            nc.vector.scalar_tensor_tensor(out=key[0:TP, :], in0=key[0:TP, :], scalar=float(NODES),
                                           in1=dst_f[0:TP, :], op0=ALU.mult, op1=ALU.add).then_inc(s_key, 1)
            dve.wait_ge(s_key, 1)
            by_edge = vals[0:TP, :].rearrange("p (c w) -> p c w", w=ROW)
            nc.vector.memset(by_edge[:, :, HEADS:ROW], 1.0)
            dve.wait_ge(s_bias, 16)
            by_head = bias[0:TP, 0:EC * HEADS].rearrange("p (c h) -> p h c", h=HEADS)
            nc.vector.tensor_reduce(hmax[0:TP, 0:8], by_head, AX_X, ALU.max).then_inc(s_pmax, 1)
            dve.wait_ge(s_tmax, 1)
            link(dve, nc.vector.tensor_reduce(hmax[0:8, 8:9], bank(0)[0:8, 0:TP], AX_X, ALU.max))
            nc.vector.tensor_scalar(hmax[0:8, 16:24], ident[0:8, 0:8], hmax[0:8, 8:9], None,
                                    ALU.mult).then_inc(s_hmax, 1)
            dve.wait_ge(s_bmax, 1)
            link(dve, nc.vector.tensor_copy(hmax[0:TP, 24:32], bank(1)[0:TP, 0:8]))
            flat = bias[0:TP, 0:EC * HEADS].rearrange("p (c h) -> p c h", h=HEADS)
            nc.vector.tensor_tensor(flat, flat, hmax[0:TP, 24:32].unsqueeze(1).to_broadcast([TP, EC, HEADS]),
                                    ALU.subtract).then_inc(s_shift, 1)

            with dve.Fori(0, GROUPS // UG) as i:
                keys = [key[0:TP, bass.ds(i * (UG * GE) + u * GE, GE)] for u in range(UG)]
                for u in range(UG):
                    nc.vector.tensor_tensor(
                        diag[u][0:TP, :].rearrange("p (c f) -> p c f", c=GE),
                        ident[0:TP, 0:TP].unsqueeze(1).to_broadcast([TP, GE, TP]),
                        keys[u].unsqueeze(2).to_broadcast([TP, GE, TP]), ALU.mult).then_inc(s_diag, 1)
                for u in range(UG):
                    dve.wait_ge(s_keyrow, i * UG + (u + 1))
                    at = 0
                    for c in range(GE):
                        n = (c + 1) * TP
                        last = nc.vector.scalar_tensor_tensor(
                            out=same[u][0:TP, at:at + n], in0=bank(u)[0:TP, 0:n],
                            scalar=key[0:TP, bass.ds(i * (UG * GE) + (u * GE + c), 1)], in1=later[0:TP, GE * TP - n:GE * TP],
                            op0=ALU.is_equal, op1=ALU.mult, accum_out=first[u][0:TP, c:c + 1])
                        at += n
                    last.then_inc(s_same, 1)
                    dve.wait_ge(s_same, i * UG + (u + 1))
                    nc.vector.tensor_tensor(first[u][0:TP, GE:2 * GE], spill[0:TP, GE:2 * GE],
                                            keys[u], ALU.subtract)
                    nc.vector.tensor_scalar(first[u][0:TP, 0:GE], first[u][0:TP, 0:GE], 0.0, None,
                                            ALU.is_gt).then_inc(s_first, 1)
                    dve.wait_ge(s_first, i * (2 * UG) + (2 * u + 1))
                    nc.vector.tensor_tensor(first[u][0:TP, 0:GE], first[u][0:TP, 0:GE],
                                            first[u][0:TP, GE:2 * GE], ALU.mult).then_inc(s_first, 1)
                    dve.wait_ge(s_first, i * (2 * UG) + (2 * u + 2))
                    nc.vector.tensor_tensor(cell[0:TP, bass.ds(i * (UG * GE) + u * GE, GE)].bitcast(U32),
                                            first[u][0:TP, 0:GE], keys[u], ALU.add)
                for u in range(UG):
                    dve.wait_ge(s_grp, i * UG + (u + 1))
                    dve.wait_ge(s_sum, i * UG + (u + 1))
                    nc.vector.tensor_tensor(vals[0:TP, bass.ds(i * (UG * GE * ROW) + u * GE * ROW, GE * ROW)],
                                            vg[u][0:TP, :], bank(4 + u)[0:TP, 0:GE * ROW],
                                            ALU.add).then_inc(s_group, 1)
            leave_stage(dve, "DVE")

        def edges_act(act):
            act.wait_ge(s_shift, 1)
            by_edge = vals[0:TP, :].rearrange("p (c w) -> p c w", w=ROW)
            nc.scalar.activation(by_edge[:, :, 0:HEADS],
                                 bias[0:TP, 0:EC * HEADS].rearrange("p (c h) -> p c h", h=HEADS),
                                 ACT.Exp).then_inc(s_group, 1)
            with act.Fori(0, GROUPS // UG) as i:
                act.wait_ge(s_group, i * UG + 1)
                for u in range(UG):
                    nc.scalar.activation(vg[u][0:TP, :],
                                         vals[0:TP, bass.ds(i * (UG * GE * ROW) + u * GE * ROW, GE * ROW)],
                                         ACT.Copy).then_inc(s_grp, 1)
            leave_stage(act, "ACT")

        def edges_pe(pe):
            pe.wait_ge(s_const, 1)
            pe.wait_ge(s_pmax, 1)
            nc.tensor.transpose(bank(0)[0:8, 0:TP], hmax[0:TP, 0:8], ident[0:TP, 0:TP]).then_inc(s_tmax, 1)
            pe.wait_ge(s_hmax, 1)
            nc.tensor.matmul(bank(1)[0:TP, 0:8], ones[0:8, 0:TP], hmax[0:8, 16:24],
                             start=True, stop=True).then_inc(s_bmax, 1)
            with pe.Fori(0, GROUPS // UG) as i:
                for u in range(UG):
                    pe.wait_ge(s_diag, i * UG + (u + 1))
                    nc.tensor.matmul(bank(u)[0:TP, 0:GE * TP], ones[0:TP, 0:TP], diag[u][0:TP, :],
                                     start=True, stop=True).then_inc(s_keyrow, 1)
                for u in range(UG):
                    pe.wait_ge(s_grp, i * UG + (u + 1))
                    pe.wait_ge(s_same, i * UG + (u + 1))
                    for c0 in range(GE):
                        for c in range(c0, GE):
                            at = TP * (c * (c + 1) // 2 + c0)
                            last = nc.tensor.matmul(bank(4 + u)[0:TP, c0 * ROW:(c0 + 1) * ROW],
                                                    same[u][0:TP, at:at + TP],
                                                    vg[u][0:TP, c * ROW:(c + 1) * ROW],
                                                    start=(c == c0), stop=(c == GE - 1))
                    last.then_inc(s_sum, 1)
            leave_stage(pe, "PE")

        def edges_pool(pool):
            pool.wait_ge(s_table0, TABLE_ZEROED)
            for g in range(GROUPS):
                pool.wait_ge(s_group, g + 2)
                if g > 0:
                    pool.wait_ge(s_scat, 16 * GE * g)
                for c in range(GE * g, GE * (g + 1)):
                    pool.indirect_dma_start(
                        d["table"], bass.IndirectOffsetOnAxis(ap=cell[0:TP, c:c + 1].bitcast(U32), axis=0),
                        vals[0:TP, c * ROW:(c + 1) * ROW], None, compute_op=ALU.add).then_inc(s_scat, 16)

        TABLE_DONE = 16 * EC

        wm = Space(4 * SLOT, 6 * SLOT)
        wq_m, wk_m, wv_m = (chunks(wm.take(KC * C), C) for _ in range(3))
        wo_m = chunks(wm.take(KC * C), C)
        w1_m = chunks(wm.take(KC * FF), FF)
        w2_m = chunks(wm.take(2 * C), C, 2)
        qT_m = cols(slot[0])
        Hm = rows(slot[1])
        space = Space(BUF, TOP)
        bq_m, bk_m, bv_m, bo_m, b2_m = (space.take(C) for _ in range(5))
        ln1_s, ln1_b, ln2_s, ln2_b = (space.take(C) for _ in range(4))
        b1_m = space.take(2)
        xT_m = [chunks(space.take(C)) for _ in range(2)]
        q_m, k_m, v_m = space.take(C), space.take(C), space.take(C)
        kv_m = chunks(space.take(C), 128, PAIRS)
        ks_m = space.take(32)
        rd_m = space.take(8)
        f1_m = [chunks(space.take(2 * TP), TP, 2) for _ in range(2)]
        row_m = q_m
        s_wm = sem("mix_qkv_weights_loaded")
        s_wm2 = sem("mix_rest_weights_loaded")
        m_tx = sem("mix_x_transposed")
        m_xT = sem("mix_xT_copied")
        m_proj = sem("mix_projected")
        m_ev = sem("mix_projection_read")
        m_rows = sem("mix_rows_ready")
        m_kv = sem("mix_kv_added")
        m_tq = sem("mix_q_transposed")
        m_qT = sem("mix_qT_copied")
        m_kvb = sem("mix_kv_blocks_ready")
        m_nd = sem("mix_num_den_ready")
        m_att = sem("mix_attention_row_ready")
        m_ta = sem("mix_attention_transposed")
        m_aT = sem("mix_attention_T_copied")
        m_wo = sem("mix_out_projected")
        m_h = sem("mix_h_ready")
        m_h1 = sem("mix_h_normalized")
        m_th = sem("mix_h_transposed")
        m_hT = sem("mix_hT_copied")
        m_f1 = sem("mix_ff1_ready")
        m_r1 = sem("mix_relu_ready")
        m_f2 = sem("mix_ff2_ready")
        m_g = sem("mix_ff_added")

        def mix_sp(sp):
            for w, n in ((wq_m, "Wq"), (wk_m, "Wk"), (wv_m, "Wv")):
                sp.dma_start(w.rearrange("p k n -> p (k n)"), d["L0_mix_" + n]).then_inc(s_wm, 16)
            for w, n in ((wo_m, "Wo"), (w1_m, "W1"), (w2_m, "W2")):
                sp.dma_start(w.rearrange("p k n -> p (k n)"), d["L0_mix_" + n]).then_inc(s_wm2, 16)

        def mix_bias_sp(sp):
            sp.wait_ge(s_stage, 3)
            sp.wait_ge(s_table0, TABLE_ZEROED)
            for b, n in ((bq_m, "bq"), (bk_m, "bk"), (bv_m, "bv")):
                load(sp, b, "L0_mix_" + n, s_wm)
            for b, n in ((bo_m, "bo"), (ln1_s, "ln1_scale"), (ln1_b, "ln1_bias"), (b2_m, "b2"),
                         (ln2_s, "ln2_scale"), (ln2_b, "ln2_bias"), (b1_m, "b1")):
                load(sp, b, "L0_mix_" + n, s_wm2)

        def mix_dve(dve):
            dve.wait_ge(s_x, 16)
            ln_stats_dve(dve, X, 1e-5)
            for t in range(TILES):
                last = normalize(XN[0:TP, t, :], X[0:TP, t, :], t)
            last.then_inc(s_xn, 1)
            nc.vector.memset(kv_m, 0.0)
            link(dve, nc.vector.memset(ks_m, 0.0))
            dve.wait_ge(s_wm, 16 * 6)
            for t in range(TILES):
                for j, (row, b) in enumerate(((q_m, bq_m), (k_m, bk_m), (v_m, bv_m))):
                    n = 3 * t + j
                    dve.wait_ge(m_proj, n + 1)
                    if t >= 1:
                        dve.wait_ge(m_kv, t)
                    nc.vector.tensor_tensor(row[0:TP, :], bank(2 + n % 3)[0:TP, :], b[0:TP, :],
                                            ALU.add).then_inc(m_ev, 1)
                dve.wait_ge(m_ev, 3 * t + 3)
                nc.vector.tensor_scalar(q_m[0:TP, :], q_m[0:TP, :], 0.0, 0.001, ALU.max, ALU.add)
                nc.vector.tensor_scalar(k_m[0:TP, :], k_m[0:TP, :], 0.0, 0.001, ALU.max, ALU.add).then_inc(m_rows, 1)
            dve.wait_ge(m_kv, TILES)
            kv = bank(6)[:, :].rearrange("p (j n) -> p j n", j=PAIRS)
            for s in (0, 64):
                nc.vector.tensor_copy(kv_m[s:s + 64, :, s:s + 64], kv[s:s + 64, :, s:s + 64])
                last = nc.vector.tensor_copy(
                    ks_m[s:s + 64, s // 64:s // 64 + 31:10],
                    bank(7)[s:s + 64, 0:8].rearrange("p (j n) -> p j n", n=2)[:, :, 0])
            last.then_inc(m_kvb, 1)
            dve.wait_ge(s_wm2, 16 * 10)
            for t in range(TILES):
                dve.wait_ge(m_nd, t + 1)
                link(dve, nc.vector.reciprocal(rd_m[0:TP, :], bank(2 + t % 2)[0:TP, 0:8]))
                if t >= 1:
                    dve.wait_ge(m_ta, t)
                nc.vector.tensor_tensor(row_m[0:TP, :].rearrange("p (h n) -> p h n", h=HEADS),
                                        bank(t % 2)[0:TP, :].rearrange("p (h n) -> p h n", h=HEADS),
                                        rd_m[0:TP, :].unsqueeze(2).to_broadcast([TP, HEADS, DH]),
                                        ALU.mult).then_inc(m_att, 1)
                dve.wait_ge(m_wo, t + 1)
                link(dve, nc.vector.tensor_tensor(Hm[0:TP, t, :], bank(5 + t % 2)[0:TP, :], bo_m[0:TP, :], ALU.add))
                nc.vector.tensor_tensor(Hm[0:TP, t, :], Hm[0:TP, t, :], XN[0:TP, t, :], ALU.add).then_inc(m_h, 1)
            dve.wait_ge(m_h, TILES)
            ln_stats_dve(dve, Hm, 1e-6)

            def normed(t):
                h = Hm[0:TP, t, :]
                link(dve, normalize(h, h, t))
                link(dve, nc.vector.tensor_tensor(h, h, ln1_s[0:TP, :], ALU.mult))
                nc.vector.tensor_tensor(h, h, ln1_b[0:TP, :], ALU.add).then_inc(m_h1, 1)

            normed(0)
            for t in range(TILES):
                if t + 1 < TILES:
                    normed(t + 1)
                dve.wait_ge(m_f2, t + 1)
                dve.wait_ge(m_h1, t + 1)
                h = Hm[0:TP, t, :]
                link(dve, nc.vector.tensor_tensor(h, bank(5 + t % 2)[0:TP, :], h, ALU.add))
                nc.vector.tensor_tensor(h, h, b2_m[0:TP, :], ALU.add).then_inc(m_g, 1)
            dve.wait_ge(m_g, TILES)
            ln_stats_dve(dve, Hm, 1e-6)
            for step in range(4):
                for t in range(TILES):
                    h = Hm[0:TP, t, :]
                    if step == 0:
                        last = normalize(h, h, t)
                    elif step == 1:
                        last = nc.vector.tensor_tensor(h, h, ln2_s[0:TP, :], ALU.mult)
                    elif step == 2:
                        last = nc.vector.tensor_tensor(h, h, ln2_b[0:TP, :], ALU.add)
                    else:
                        last = nc.vector.tensor_tensor(X[0:TP, t, :], X[0:TP, t, :], h, ALU.add)
                link(dve, last)
            leave_stage(dve, "DVE")

        def mix_act(act):
            ln_stats_act(act)
            for t in range(TILES + 1):
                if t < TILES:
                    act.wait_ge(m_tx, t + 1)
                    if t >= 2:
                        act.wait_ge(m_proj, 3 * t - 3)
                    nc.scalar.activation(xT_m[t % 2], chunks(bank(t % 2)[:, :], TP), ACT.Copy).then_inc(m_xT, 1)
                if t >= 1:
                    act.wait_ge(m_tq, t)
                    nc.scalar.activation(qT_m[:, :, tok(t - 1)], chunks(bank(5)[:, :], TP), ACT.Copy).then_inc(m_qT, 1)
            for t in range(TILES):
                act.wait_ge(m_ta, t + 1)
                if t >= 2:
                    act.wait_ge(m_wo, t - 1)
                nc.scalar.activation(xT_m[t % 2], chunks(bank(4)[:, :], TP), ACT.Copy).then_inc(m_aT, 1)
            ln_stats_act(act)
            for t in range(TILES):
                act.wait_ge(m_th, t + 1)
                if t >= 2:
                    act.wait_ge(m_f1, t - 1)
                nc.scalar.activation(xT_m[t % 2], chunks(bank(t % 2)[:, :], TP), ACT.Copy).then_inc(m_hT, 1)
                act.wait_ge(m_f1, t + 1)
                if t >= 2:
                    act.wait_ge(m_f2, t - 1)
                for m in range(2):
                    last = nc.scalar.activation(f1_m[t % 2][:, m, :], bank(2 + t % 2)[:, m * TP:(m + 1) * TP],
                                                ACT.Relu, bias=b1_m[:, m:m + 1])
                last.then_inc(m_r1, 1)
            ln_stats_act(act)
            leave_stage(act, "ACT")

        def mix_pe(pe):
            pe.wait_ge(s_xn, 1)
            pe.wait_ge(s_wm, 16 * 6)

            def after(t):
                pe.wait_ge(m_rows, t + 1)
                if t >= 1:
                    pe.wait_ge(m_qT, t)
                transpose_tile(chunks(bank(5)[:, :], TP), q_m[0:TP, :]).then_inc(m_tq, 1)
                for j in range(PAIRS):
                    kj = k_m[0:TP, j * 128:(j + 1) * 128]
                    first = t == 0 and j == 0
                    end = t == TILES - 1 and j == PAIRS - 1
                    nc.tensor.matmul(bank(6)[:, j * 128:(j + 1) * 128], kj, v_m[0:TP, j * 128:(j + 1) * 128],
                                     start=first, stop=end, skip_group_check=True)
                    last = nc.tensor.matmul(bank(7)[:, 2 * j:2 * j + 2], kj, ones[0:TP, 0:2],
                                            start=first, stop=end, skip_group_check=True)
                last.then_inc(m_kv, 1)

            for t in range(TILES):
                transpose_tile(chunks(bank(t % 2)[:, :], TP), XN[0:TP, t, :]).then_inc(m_tx, 1)
                if t >= 1:
                    after(t - 1)
                pe.wait_ge(m_xT, t + 1)
                for j, w in enumerate((wq_m, wk_m, wv_m)):
                    n = 3 * t + j
                    if n >= 3:
                        pe.wait_ge(m_ev, n - 2)
                    project(bank(2 + n % 3)[0:TP, :], xT_m[t % 2], w).then_inc(m_proj, 1)
            after(TILES - 1)
            pe.wait_ge(m_kvb, 1)
            pe.wait_ge(m_qT, TILES)
            pe.wait_ge(s_wm2, 16 * 10)

            def num_den(t):
                if t >= 2:
                    pe.wait_ge(m_att, t - 1)
                for j in range(PAIRS):
                    nc.tensor.matmul(bank(t % 2)[0:TP, j * 128:(j + 1) * 128], qT_m[:, j, tok(t)], kv_m[:, j, :],
                                     start=True, stop=True)
                for j in range(PAIRS):
                    last = nc.tensor.matmul(bank(2 + t % 2)[0:TP, 0:8], qT_m[:, j, tok(t)],
                                            ks_m[:, 8 * j:8 * j + 8], start=(j == 0), stop=(j == PAIRS - 1))
                last.then_inc(m_nd, 1)

            num_den(0)
            for t in range(TILES):
                if t + 1 < TILES:
                    num_den(t + 1)
                pe.wait_ge(m_att, t + 1)
                if t >= 1:
                    pe.wait_ge(m_aT, t)
                transpose_tile(chunks(bank(4)[:, :], TP), row_m[0:TP, :]).then_inc(m_ta, 1)
                pe.wait_ge(m_aT, t + 1)
                if t >= 2:
                    pe.wait_ge(m_h, t - 1)
                project(bank(5 + t % 2)[0:TP, :], xT_m[t % 2], wo_m).then_inc(m_wo, 1)

            def turn_h(t):
                pe.wait_ge(m_h1, t + 1)
                if t >= 2:
                    pe.wait_ge(m_hT, t - 1)
                transpose_tile(chunks(bank(t % 2)[:, :], TP), Hm[0:TP, t, :]).then_inc(m_th, 1)

            turn_h(0)
            for t in range(TILES):
                pe.wait_ge(m_hT, t + 1)
                if t >= 2:
                    pe.wait_ge(m_r1, t - 1)
                for m in range(2):
                    for k in range(KC):
                        last = nc.tensor.matmul(bank(2 + t % 2)[:, m * TP:(m + 1) * TP],
                                                w1_m[:, k, m * 128:(m + 1) * 128], xT_m[t % 2][:, k, :],
                                                start=(k == 0), stop=(k == KC - 1))
                last.then_inc(m_f1, 1)
                if t + 1 < TILES:
                    turn_h(t + 1)
                pe.wait_ge(m_r1, t + 1)
                if t >= 2:
                    pe.wait_ge(m_g, t - 1)
                project(bank(5 + t % 2)[0:TP, :], f1_m[t % 2], w2_m, k=2).then_inc(m_f2, 1)
            leave_stage(pe, "PE")

        wg = Space(BIG, 36864)
        wq_g, wk_g, wv_g = (chunks(wg.take(KC * C), C) for _ in range(3))
        qT_g, kT_g, V_g = cols(slot[0]), cols(slot[1]), rows(slot[2])
        space = Space(BUF, TOP)
        bq_g, bk_g, bv_g, bo_g = (space.take(C) for _ in range(4))
        lg_g = space.take(2 * KC)
        z_g = space.take(C)
        zT_g = [chunks(space.take(C)) for _ in range(2)]
        q_g, k_g = space.take(C), space.take(C)
        s_wg = sem("gnn_qkv_weights_loaded")
        s_bg = sem("gnn_qkv_biases_loaded")
        g_z = sem("gnn_z_ready")
        g_tz = sem("gnn_z_transposed")
        g_zT = sem("gnn_zT_ready")
        g_proj = sem("gnn_projected")
        g_ev = sem("gnn_projection_read")
        g_tqk = sem("gnn_qk_transposed")
        g_qkT = sem("gnn_qkT_copied")

        def gnn_w_sp(sp):
            for w, n in ((wq_g, "Wq"), (wk_g, "Wk"), (wv_g, "Wv")):
                sp.dma_start(w.rearrange("p k n -> p (k n)"), d["L0_gnn_" + n]).then_inc(s_wg, 16)

        def gnn_sp(sp):
            sp.wait_ge(s_stage, 6)
            for b, n in ((bq_g, "bq"), (bk_g, "bk"), (bv_g, "bv"), (bo_g, "bo"),
                         (lg_g[:, 0:KC], "ln_att_g"), (lg_g[:, KC:2 * KC], "ln_att_b")):
                load(sp, b, "L0_gnn_" + n, s_bg)

        def gnn_dve(dve):
            ln_stats_dve(dve, XN, 1e-5)
            dve.wait_ge(s_bg, 16 * 6)

            def z(t):
                if t >= 1:
                    dve.wait_ge(g_tz, t)
                normalize(z_g[0:TP, :], XN[0:TP, t, :], t).then_inc(g_z, 1)

            z(0)
            for t in range(TILES):
                if t + 1 < TILES:
                    z(t + 1)
                for j, (row, b) in enumerate(((q_g[0:TP, :], bq_g), (k_g[0:TP, :], bk_g), (V_g[0:TP, t, :], bv_g))):
                    dve.wait_ge(g_proj, 3 * t + j + 1)
                    if t >= 1 and j < 2:
                        dve.wait_ge(g_tqk, t)
                    nc.vector.tensor_tensor(row, bank(2 + j)[0:TP, :], b[0:TP, :], ALU.add).then_inc(g_ev, 1)
            for t in range(TILES):
                nc.vector.tensor_tensor(XN[0:TP, t, :], XN[0:TP, t, :], bo_g[0:TP, :], ALU.add)
            leave_stage(dve, "DVE")

        def gnn_act(act):
            ln_stats_act(act)
            act.wait_ge(s_bg, 16 * 6)
            for t in range(TILES + 1):
                if t < TILES:
                    act.wait_ge(g_tz, t + 1)
                    if t >= 2:
                        act.wait_ge(g_proj, 3 * t - 3)
                    for k in range(KC):
                        last = nc.scalar.activation(zT_g[t % 2][:, k, :], bank(t % 2)[:, k * TP:(k + 1) * TP],
                                                    ACT.Identity, scale=lg_g[:, k:k + 1],
                                                    bias=lg_g[:, KC + k:KC + k + 1])
                    last.then_inc(g_zT, 1)
                if t >= 1:
                    act.wait_ge(g_tqk, t)
                    nc.scalar.activation(qT_g[:, :, tok(t - 1)], chunks(bank(5)[:, :], TP), ACT.Copy,
                                         scale=DH ** -0.5)
                    nc.scalar.activation(kT_g[:, :, tok(t - 1)], chunks(bank(6)[:, :], TP),
                                         ACT.Copy).then_inc(g_qkT, 1)
            leave_stage(act, "ACT")

        def gnn_pe(pe):
            pe.wait_ge(s_wg, 16 * 3)

            def turn(t):
                pe.wait_ge(g_z, t + 1)
                if t >= 2:
                    pe.wait_ge(g_zT, t - 1)
                transpose_tile(chunks(bank(t % 2)[:, :], TP), z_g[0:TP, :]).then_inc(g_tz, 1)

            def after(t):
                pe.wait_ge(g_ev, 3 * t + 2)
                if t >= 1:
                    pe.wait_ge(g_qkT, t)
                transpose_tile(chunks(bank(5)[:, :], TP), q_g[0:TP, :])
                transpose_tile(chunks(bank(6)[:, :], TP), k_g[0:TP, :]).then_inc(g_tqk, 1)

            turn(0)
            for t in range(TILES):
                pe.wait_ge(g_zT, t + 1)
                for j, w in enumerate((wq_g, wk_g, wv_g)):
                    if t >= 1:
                        pe.wait_ge(g_ev, 3 * t - 2 + j)
                    project(bank(2 + j)[0:TP, :], zT_g[t % 2], w).then_inc(g_proj, 1)
                    if j == 0 and t + 1 < TILES:
                        turn(t + 1)
                after(t)
            leave_stage(pe, "PE")

        HALF = NODES // 2
        ring = [arena[:, 5 * SLOT + i * HALF * ROW:5 * SLOT + (i + 1) * HALF * ROW]
                .rearrange("p (n w) -> p n w", w=ROW) for i in range(3)]
        space = Space(BUF, TOP)
        S_g = [space.take(NODES) for _ in range(2)]
        absent = space.take(NODES)
        pT = space.take(NODES)
        pT_v = pT.rearrange("p (b n) -> p b n", b=TILES)
        qz = space.take(HEADS * TP).rearrange("p (h n) -> p h n", h=HEADS)
        wo_g = chunks(space.take(KC * C), C)
        row_g = space.take(C)
        aT_g = chunks(space.take(C))
        st_g = space.take(64)
        mx3, mx, nmx = st_g[:, 0:3], st_g[:, 4:5], [st_g[:, 6 + i:7 + i] for i in range(2)]
        den2 = st_g[:, 8:24].rearrange("p (h a) -> p h a", a=2)
        den, dz = st_g[:, 24:32], st_g[:, 32:40]
        CH = [(0, 512), (512, 1024), (1024, NODES)]
        s_tab = [sem(f"table_part_loaded_{i}") for i in range(3)]
        s_wo_g = sem("gnn_out_weights_loaded")
        s_adj = sem("adjacency_stored")
        a_qz = sem("att_q_padded")
        a_s = sem("att_scores_ready")
        a_m = sem("att_scores_masked")
        a_nm = sem("att_maximum_ready")
        a_e = sem("att_exponentials_ready")
        a_abs = sem("att_absent_ready")
        a_p = sem("att_weights_ready")
        a_tp = sem("att_weights_transposed")
        a_pt = sem("att_weightsT_copied")
        a_pv = sem("att_values_added")
        a_adj = sem("att_adjacency_copied")
        a_row = sem("att_row_ready")
        a_tr = sem("att_row_transposed")
        a_aT = sem("att_rowT_copied")
        a_wo = sem("att_out_projected")
        a_x1 = sem("att_added_to_x")
        STEPS = TILES * HEADS

        def att_sp(sp):
            sp.wait_ge(s_stage, 9)
            sp.dma_start(wo_g.rearrange("p k n -> p (k n)"), d["L0_gnn_Wo"]).then_inc(s_wo_g, 16)
            sp.wait_ge(s_scat, TABLE_DONE)
            table = d["table"][0:CELLS, :].rearrange("(s n) w -> s n w", n=NODES)
            for n in range(2 * TILES):
                t, half = divmod(n, 2)
                if n >= 3:
                    sp.wait_ge(a_p, HEADS * ((n - 3) // 2 + 1))
                    sp.wait_ge(a_adj, (n - 3) // 2 + 1)
                sp.dma_start(ring[n % 3][0:TP, :, :], table[tok(t), half * HALF:(half + 1) * HALF, :])\
                    .then_inc(s_tab[n % 3], 16)
                if half == 0 and t >= 1:
                    store_adj(sp, t - 1)
            store_adj(sp, TILES - 1)

        def store_adj(sp, t):
            sp.wait_ge(a_adj, t + 1)
            sp.dma_start(d["adj"][tok(t), :], pT[0:TP, :]).then_inc(s_adj, 16)

        def part_loaded(eng, t):
            for n in (2 * t, 2 * t + 1):
                eng.wait_ge(s_tab[n % 3], 16 * (n // 3 + 1))

        def halves(t):
            return [(h, ring[(2 * t + h) % 3], slice(h * HALF, (h + 1) * HALF)) for h in range(2)]

        def att_dve(dve):
            nc.vector.memset(qz, 0.0).then_inc(s_zeroed, 1)

            def mask(s):
                t, h = divmod(s, HEADS)
                if h == 0:
                    part_loaded(dve, t)
                    for _, part, c in halves(t):
                        last = nc.vector.tensor_scalar(absent[0:TP, c], part[0:TP, :, HEADS], 0.0, NEG,
                                                       ALU.is_equal, ALU.mult)
                    last.then_inc(a_abs, 1)
                    dve.wait_ge(a_abs, t + 1)
                if s >= 2:
                    dve.wait_ge(a_tp, s - 1)
                for j, (c0, c1) in enumerate(CH):
                    dve.wait_ge(a_s, 3 * s + j + 1)
                    nc.vector.tensor_tensor_reduce(
                        out=S_g[s % 2][0:TP, c0:c1], in0=bank(j)[0:TP, 0:c1 - c0], in1=absent[0:TP, c0:c1],
                        scale=1.0, scalar=LOWEST, op0=ALU.add, op1=ALU.max,
                        accum_out=mx3[0:TP, j:j + 1]).then_inc(a_m, 1)
                dve.wait_ge(a_m, 3 * s + 3)
                link(dve, nc.vector.tensor_reduce(mx[0:TP, :], mx3[0:TP, :], AX_X, ALU.max))
                nc.vector.tensor_scalar(nmx[s % 2][0:TP, :], mx[0:TP, :], -1.0, None, ALU.mult).then_inc(a_nm, 1)

            def weigh(s):
                t, h = divmod(s, HEADS)
                dve.wait_ge(a_e, s + 1)
                for a, part, c in halves(t):
                    last = nc.vector.tensor_tensor_reduce(
                        out=S_g[s % 2][0:TP, c], in0=S_g[s % 2][0:TP, c], in1=part[0:TP, :, h],
                        scale=1.0, scalar=0.0, op0=ALU.mult, op1=ALU.add, accum_out=den2[0:TP, h, a:a + 1])
                last.then_inc(a_p, 1)

            def finish(t):
                dve.wait_ge(a_p, HEADS * (t + 1))
                link(dve, nc.vector.tensor_tensor(den[0:TP, :], den2[0:TP, :, 0], den2[0:TP, :, 1], ALU.add))
                link(dve, nc.vector.tensor_scalar(dz[0:TP, :], den[0:TP, :], 0.0, None, ALU.is_equal))
                link(dve, nc.vector.tensor_tensor(den[0:TP, :], den[0:TP, :], dz[0:TP, :], ALU.add))
                link(dve, nc.vector.reciprocal(den[0:TP, :], den[0:TP, :]))
                dve.wait_ge(a_pv, HEADS * (t + 1))
                if t >= 1:
                    dve.wait_ge(a_tr, t)
                nc.vector.tensor_tensor(row_g[0:TP, :].rearrange("p (h n) -> p h n", h=HEADS),
                                        bank(6)[0:TP, :].rearrange("p (h n) -> p h n", h=HEADS),
                                        den[0:TP, :].unsqueeze(2).to_broadcast([TP, HEADS, DH]),
                                        ALU.mult).then_inc(a_row, 1)

            def add(t):
                dve.wait_ge(a_wo, t + 1)
                nc.vector.tensor_tensor(XN[0:TP, t, :], bank(7)[0:TP, :], XN[0:TP, t, :], ALU.add).then_inc(a_x1, 1)

            mask(0)
            for s in range(STEPS):
                t, h = divmod(s, HEADS)
                if h == 0 and t >= 1:
                    finish(t - 1)
                if h < HEADS - 1:
                    mask(s + 1)
                weigh(s)
                if h == HEADS - 1 and t + 1 < TILES:
                    mask(s + 1)
                if h == 2 and t >= 1:
                    add(t - 1)
            finish(TILES - 1)
            add(TILES - 1)
            dve.wait_ge(a_x1, TILES)
            leave_stage(dve, "DVE")

        def att_act(act):
            act.wait_ge(s_zeroed, 1)

            def pad_q(t):
                if t >= 1:
                    act.wait_ge(a_s, 3 * HEADS * t)
                by_pair = qz.rearrange("p (j e) n -> p j e n", e=2)
                for e in range(2):
                    last = nc.scalar.activation(by_pair[64 * e:64 * e + 64, :, e, :],
                                                qT_g[64 * e:64 * e + 64, :, tok(t)], ACT.Copy)
                last.then_inc(a_qz, 1)

            def exps(s):
                act.wait_ge(a_nm, s + 1)
                b = S_g[s % 2][0:TP, :]
                nc.scalar.activation(b, b, ACT.Exp, bias=nmx[s % 2][0:TP, :]).then_inc(a_e, 1)

            pad_q(0)
            exps(0)
            for s in range(STEPS):
                t, h = divmod(s, HEADS)
                if h < HEADS - 1:
                    exps(s + 1)
                if h == 0:
                    part_loaded(act, t)
                    act.wait_ge(a_pv, HEADS * t)
                    for _, part, c in halves(t):
                        last = nc.scalar.activation(pT[0:TP, c], part[0:TP, :, HEADS], ACT.Copy)
                    last.then_inc(a_adj, 1)
                    act.wait_ge(s_adj, 16 * (t + 1))
                act.wait_ge(a_tp, s + 1)
                nc.scalar.activation(pT_v[0:TP, 0:8, :], banks[0:TP, 3 * BANK:5 * BANK]
                                     .rearrange("p (b n) -> p b n", n=128)[:, :, 0:TP], ACT.Copy)
                nc.scalar.activation(pT_v[0:TP, 8:10, :], bank(5)[0:TP, 0:256]
                                     .rearrange("p (b n) -> p b n", n=128)[:, :, 0:TP], ACT.Copy).then_inc(a_pt, 1)
                if h == 6 and t + 1 < TILES:
                    pad_q(t + 1)
                if h == HEADS - 1 and t + 1 < TILES:
                    exps(s + 1)
                if h == 1 and t >= 1:
                    act.wait_ge(a_tr, t)
                    nc.scalar.activation(aT_g, chunks(bank(7)[:, :], TP), ACT.Copy).then_inc(a_aT, 1)
            act.wait_ge(a_tr, TILES)
            nc.scalar.activation(aT_g, chunks(bank(7)[:, :], TP), ACT.Copy).then_inc(a_aT, 1)
            leave_stage(act, "ACT")

        def att_pe(pe):
            pe.wait_ge(s_wo_g, 16)

            def scores(s):
                t, h = divmod(s, HEADS)
                if h == 0:
                    pe.wait_ge(a_qz, t + 1)
                for j, (c0, c1) in enumerate(CH):
                    if s >= 1:
                        pe.wait_ge(a_m, 3 * (s - 1) + j + 1)
                    nc.tensor.matmul(bank(j)[0:TP, 0:c1 - c0], qz[:, h, :], kT_g[:, h // 2, c0:c1],
                                     start=True, stop=True).then_inc(a_s, 1)

            def turn(s):
                pe.wait_ge(a_p, s + 1)
                if s >= 1:
                    pe.wait_ge(a_pt, s)
                for b in range(TILES):
                    last = nc.tensor.transpose(banks[0:TP, 3 * BANK + 128 * b:3 * BANK + 128 * b + TP],
                                               S_g[s % 2][0:TP, b * TP:(b + 1) * TP], ident[0:TP, 0:TP])
                last.then_inc(a_tp, 1)

            def values(s):
                t, h = divmod(s, HEADS)
                pe.wait_ge(a_pt, s + 1)
                if h == 0 and t >= 1:
                    pe.wait_ge(a_row, t)
                for b in range(TILES):
                    last = nc.tensor.matmul(bank(6)[0:TP, h * DH:(h + 1) * DH], pT_v[0:TP, b, :],
                                            V_g[0:TP, b, h * DH:(h + 1) * DH],
                                            start=(b == 0), stop=(b == TILES - 1))
                last.then_inc(a_pv, 1)

            def turn_row(t):
                pe.wait_ge(a_row, t + 1)
                if t >= 1:
                    pe.wait_ge(a_x1, t)
                transpose_tile(chunks(bank(7)[:, :], TP), row_g[0:TP, :]).then_inc(a_tr, 1)

            def out(t):
                pe.wait_ge(a_aT, t + 1)
                project(bank(7)[0:TP, :], aT_g, wo_g).then_inc(a_wo, 1)

            scores(0)
            scores(1)
            for s in range(STEPS):
                t, h = divmod(s, HEADS)
                turn(s)
                if h == 1 and t >= 1:
                    turn_row(t - 1)
                if s + 2 < STEPS:
                    scores(s + 2)
                values(s)
                if h == 1 and t >= 1:
                    out(t - 1)
            turn_row(TILES - 1)
            out(TILES - 1)
            leave_stage(pe, "PE")

        w1_g = chunks(arena[:, 2 * SLOT:2 * SLOT + KC * HID], HID)
        w2_g = arena[:, 3 * SLOT:3 * SLOT + 8 * C].rearrange("p (k n) -> p k n", k=8)
        space = Space(BUF, TOP)
        b2_g = space.take(C)
        lf_g = space.take(2 * KC)
        b1_g = space.take(8)
        z_f = space.take(C)
        zT_f = [chunks(space.take(C)) for _ in range(2)]
        hT_f = [chunks(space.take(8 * TP), TP, 8) for _ in range(2)]
        s_wf = sem("gnn_ff_weights_loaded")
        f_z = sem("ff_z_ready")
        f_tz = sem("ff_z_transposed")
        f_zT = sem("ff_zT_ready")
        f_h = sem("ff_hidden_ready")
        f_s = sem("ff_silu_ready")
        f_o = sem("ff_out_ready")
        f_x = sem("ff_added")

        def ff_sp(sp):
            sp.wait_ge(s_stage, 12)
            sp.dma_start(w1_g.rearrange("p k n -> p (k n)"), d["L0_gnn_W1"]).then_inc(s_wf, 16)
            sp.dma_start(w2_g.rearrange("p k n -> p (k n)"), d["L0_gnn_W2"]).then_inc(s_wf, 16)
            for b, n in ((b2_g, "b2"), (b1_g, "b1"), (lf_g[:, 0:KC], "ln_ff_g"), (lf_g[:, KC:2 * KC], "ln_ff_b")):
                load(sp, b, "L0_gnn_" + n, s_wf)

        def ff_dve(dve):
            ln_stats_dve(dve, XN, 1e-5)
            dve.wait_ge(s_wf, 16 * 6)

            def z(t):
                if t >= 1:
                    dve.wait_ge(f_tz, t)
                normalize(z_f[0:TP, :], XN[0:TP, t, :], t).then_inc(f_z, 1)

            z(0)
            for t in range(TILES):
                if t + 1 < TILES:
                    z(t + 1)
                link(dve, nc.vector.tensor_tensor(X[0:TP, t, :], X[0:TP, t, :], XN[0:TP, t, :], ALU.add))
                link(dve, nc.vector.tensor_tensor(X[0:TP, t, :], X[0:TP, t, :], b2_g[0:TP, :], ALU.add))
                dve.wait_ge(f_o, t + 1)
                nc.vector.tensor_tensor(X[0:TP, t, :], bank(6 + t % 2)[0:TP, :], X[0:TP, t, :],
                                        ALU.add).then_inc(f_x, 1)
            leave_stage(dve, "DVE")

        def ff_act(act):
            ln_stats_act(act)
            act.wait_ge(s_wf, 16 * 6)

            def zT(t):
                act.wait_ge(f_tz, t + 1)
                if t >= 2:
                    act.wait_ge(f_h, 2 * (t - 1))
                for k in range(KC):
                    last = nc.scalar.activation(zT_f[t % 2][:, k, :], bank(t % 2)[:, k * TP:(k + 1) * TP],
                                                ACT.Identity, scale=lf_g[:, k:k + 1],
                                                bias=lf_g[:, KC + k:KC + k + 1])
                last.then_inc(f_zT, 1)

            zT(0)
            for t in range(TILES):
                if t + 1 < TILES:
                    zT(t + 1)
                if t >= 2:
                    act.wait_ge(f_o, t - 1)
                for a in range(2):
                    n = 2 * t + a
                    act.wait_ge(f_h, n + 1)
                    for m in range(4):
                        last = nc.scalar.activation(hT_f[t % 2][:, 4 * a + m, :],
                                                    bank(2 + n % 4)[:, m * TP:(m + 1) * TP], ACT.Silu,
                                                    bias=b1_g[:, 4 * a + m:4 * a + m + 1])
                    last.then_inc(f_s, 1)
            leave_stage(act, "ACT")

        def ff_pe(pe):
            pe.wait_ge(s_wf, 16 * 6)

            def turn(t):
                pe.wait_ge(f_z, t + 1)
                if t >= 2:
                    pe.wait_ge(f_zT, t - 1)
                transpose_tile(chunks(bank(t % 2)[:, :], TP), z_f[0:TP, :]).then_inc(f_tz, 1)

            def hidden(t):
                pe.wait_ge(f_zT, t + 1)
                for a in range(2):
                    n = 2 * t + a
                    if n >= 4:
                        pe.wait_ge(f_s, n - 3)
                    for m in range(4):
                        for k in range(KC):
                            last = nc.tensor.matmul(bank(2 + n % 4)[:, m * TP:(m + 1) * TP],
                                                    w1_g[:, k, (4 * a + m) * 128:(4 * a + m + 1) * 128],
                                                    zT_f[t % 2][:, k, :], start=(k == 0), stop=(k == KC - 1))
                    last.then_inc(f_h, 1)

            turn(0)
            hidden(0)
            for t in range(TILES):
                if t + 1 < TILES:
                    turn(t + 1)
                    hidden(t + 1)
                pe.wait_ge(f_s, 2 * t + 2)
                if t >= 2:
                    pe.wait_ge(f_x, t - 1)
                project(bank(6 + t % 2)[0:TP, :], hT_f[t % 2], w2_g, k=8).then_inc(f_o, 1)
            leave_stage(pe, "PE")

        wf = Space(BIG, SMALL)
        wq_f, wk_f, wv_f, wo_f = (chunks(wf.take(KC * C), C) for _ in range(4))
        qT_f, kT_f, V_f = cols(slot[0]), cols(slot[1]), rows(slot[2])
        Q_f, K_f = XN, rows(slot[3])
        space = Space(BUF, TOP)
        lg_f = space.take(2 * KC)
        gain = space.take(4)
        z_c = space.take(C)
        zT_c = [chunks(space.take(C)) for _ in range(2)]
        sq_c = [space.take(C) for _ in range(2)]
        ss, sr, sa, sv = (space.take(2 * TILES * HEADS) for _ in range(4))
        s_wc = sem("ffn_qkv_weights_loaded")
        c_z = sem("ffn_z_ready")
        c_tz = sem("ffn_z_transposed")
        c_zT = sem("ffn_zT_ready")
        c_proj = sem("ffn_projected")
        c_ev = sem("ffn_projection_read")
        c_sq = sem("ffn_squares_ready")
        c_ss = sem("ffn_squares_summed")
        c_sr = sem("ffn_norms_ready")
        c_n = sem("ffn_rows_normalized")
        c_tqk = sem("ffn_qk_transposed")
        c_qkT = sem("ffn_qkT_copied")

        def ffn_sp(sp):
            sp.wait_ge(s_stage, 15)
            for w, n in ((wq_f, "Wq"), (wk_f, "Wk"), (wv_f, "Wv"), (wo_f, "Wo")):
                sp.dma_start(w.rearrange("p k n -> p (k n)"), d["L0_ffn_" + n]).then_inc(s_wc, 16)
            for b, n in ((lg_f[:, 0:KC], "ln_g"), (lg_f[:, KC:2 * KC], "ln_b"), (gain[:, 0:1], "qn_g"),
                         (gain[:, 1:2], "kn_g")):
                load(sp, b, "L0_ffn_" + n, s_wc)

        def ffn_dve(dve):
            ln_stats_dve(dve, X, 1e-5)
            for t in range(TILES):
                last = normalize(XN[0:TP, t, :], X[0:TP, t, :], t)
            link(dve, last)
            ln_stats_dve(dve, XN, 1e-5)
            dve.wait_ge(s_wc, 16 * 8)
            nc.vector.tensor_scalar(gain[:, 2:3], gain[:, 1:2], float(DH) ** 0.5, None, ALU.mult)

            def z(t):
                if t >= 1:
                    dve.wait_ge(c_tz, t)
                normalize(z_c[0:TP, :], XN[0:TP, t, :], t).then_inc(c_z, 1)

            z(0)
            for t in range(TILES):
                if t + 1 < TILES:
                    z(t + 1)
                for j, row in enumerate((Q_f[0:TP, t, :], K_f[0:TP, t, :], V_f[0:TP, t, :])):
                    dve.wait_ge(c_proj, 3 * t + j + 1)
                    nc.vector.tensor_copy(row, bank(2 + j)[0:TP, :]).then_inc(c_ev, 1)
            for n in range(2 * TILES):
                dve.wait_ge(c_sq, n + 1)
                nc.vector.tensor_reduce(ss[0:TP, n * HEADS:(n + 1) * HEADS],
                                        sq_c[n % 2][0:TP, :].rearrange("p (h n) -> p h n", h=HEADS),
                                        AX_X, ALU.add).then_inc(c_ss, 1)
            dve.wait_ge(c_ss, 2 * TILES)
            nc.vector.tensor_scalar(sv[0:TP, :], ss[0:TP, :], 1e-12, None, ALU.add).then_inc(c_ss, 1)
            dve.wait_ge(c_ss, 2 * TILES + 1)
            dve.wait_ge(c_sr, 1)
            link(dve, nc.vector.reciprocal(sr[0:TP, :], sa[0:TP, :]))
            link(dve, nc.vector.tensor_tensor(ss[0:TP, :], sv[0:TP, :], sr[0:TP, :], ALU.mult))
            link(dve, nc.vector.tensor_tensor(ss[0:TP, :], ss[0:TP, :], sr[0:TP, :], ALU.mult))
            link(dve, nc.vector.tensor_scalar(ss[0:TP, :], ss[0:TP, :], -0.5, 1.5, ALU.mult, ALU.add))
            link(dve, nc.vector.tensor_tensor(sr[0:TP, :], sr[0:TP, :], ss[0:TP, :], ALU.mult))
            for n in range(2 * TILES):
                t, which = divmod(n, 2)
                row = (Q_f, K_f)[which][0:TP, t, :].rearrange("p (h n) -> p h n", h=HEADS)
                nc.vector.tensor_tensor(row, row, sr[0:TP, n * HEADS:(n + 1) * HEADS].unsqueeze(2)
                                        .to_broadcast([TP, HEADS, DH]), ALU.mult).then_inc(c_n, 1)
            leave_stage(dve, "DVE")

        def ffn_act(act):
            ln_stats_act(act)
            ln_stats_act(act)
            act.wait_ge(s_wc, 16 * 8)
            for t in range(TILES):
                act.wait_ge(c_tz, t + 1)
                if t >= 2:
                    act.wait_ge(c_proj, 3 * t - 3)
                for k in range(KC):
                    last = nc.scalar.activation(zT_c[t % 2][:, k, :], bank(t % 2)[:, k * TP:(k + 1) * TP],
                                                ACT.Identity, scale=lg_f[:, k:k + 1],
                                                bias=lg_f[:, KC + k:KC + k + 1])
                last.then_inc(c_zT, 1)
            for n in range(2 * TILES):
                t, which = divmod(n, 2)
                act.wait_ge(c_ev, 3 * t + 1 + which)
                if n >= 2:
                    act.wait_ge(c_ss, n - 1)
                nc.scalar.activation(sq_c[n % 2][0:TP, :], (Q_f, K_f)[which][0:TP, t, :],
                                     ACT.Square).then_inc(c_sq, 1)
            act.wait_ge(c_ss, 2 * TILES + 1)
            nc.scalar.activation(sa[0:TP, :], sv[0:TP, :], ACT.Sqrt).then_inc(c_sr, 1)
            for n in range(2 * TILES):
                t, which = divmod(n, 2)
                act.wait_ge(c_tqk, n + 1)
                nc.scalar.activation((qT_f, kT_f)[which][:, :, tok(t)], chunks(bank(n % 4)[:, :], TP), ACT.Copy,
                                     scale=gain[:, 2 * which:2 * which + 1]).then_inc(c_qkT, 1)
            leave_stage(act, "ACT")

        def ffn_pe(pe):
            pe.wait_ge(s_wc, 16 * 8)

            def turn(t):
                pe.wait_ge(c_z, t + 1)
                if t >= 2:
                    pe.wait_ge(c_zT, t - 1)
                transpose_tile(chunks(bank(t % 2)[:, :], TP), z_c[0:TP, :]).then_inc(c_tz, 1)

            turn(0)
            for t in range(TILES):
                pe.wait_ge(c_zT, t + 1)
                for j, w in enumerate((wq_f, wk_f, wv_f)):
                    if t >= 1:
                        pe.wait_ge(c_ev, 3 * t - 2 + j)
                    project(bank(2 + j)[0:TP, :], zT_c[t % 2], w).then_inc(c_proj, 1)
                    if j == 0 and t + 1 < TILES:
                        turn(t + 1)
            pe.wait_ge(c_ev, 3 * TILES)
            for n in range(2 * TILES):
                t, which = divmod(n, 2)
                pe.wait_ge(c_n, n + 1)
                if n >= 4:
                    pe.wait_ge(c_qkT, n - 3)
                transpose_tile(chunks(bank(n % 4)[:, :], TP), (Q_f, K_f)[which][0:TP, t, :]).then_inc(c_tqk, 1)
            leave_stage(pe, "PE")

        yT = cols(arena[:, BIG:BIG + KC * NODES])
        space = Space(BUF, TOP)
        S_c = [space.take(NODES) for _ in range(2)]
        future = space.take(NODES)
        pT_c = space.take(NODES)
        pTc_v = pT_c.rearrange("p (b n) -> p b n", b=TILES)
        qz_c = space.take(HEADS * TP).rearrange("p (h n) -> p h n", h=HEADS)
        row_c = space.take(C)
        aT_c = chunks(space.take(C))
        st_c = space.take(64)
        mx3_c, mx_c, nmx_c = st_c[:, 0:3], st_c[:, 4:5], [st_c[:, 6 + i:7 + i] for i in range(2)]
        den_c = [st_c[:, 8 + 8 * i:16 + 8 * i] for i in range(2)]
        rden_c = st_c[:, 24:32]
        b_qz = sem("causal_q_padded")
        b_s = sem("causal_scores_ready")
        b_m = sem("causal_scores_masked")
        b_nm = sem("causal_maximum_ready")
        b_e = sem("causal_exponentials_ready")
        b_tp = sem("causal_weights_transposed")
        b_pt = sem("causal_weightsT_copied")
        b_pv = sem("causal_values_added")
        b_row = sem("causal_row_ready")
        b_tr = sem("causal_row_transposed")
        b_aT = sem("causal_rowT_copied")
        b_y = sem("causal_out_projected")
        b_yT = sem("causal_yT_copied")
        parts = [[(c, min(c + BANK, (s // HEADS + 1) * TP)) for c in range(0, (s // HEADS + 1) * TP, BANK)]
                 for s in range(STEPS)]
        before = [sum(len(p) for p in parts[:s]) for s in range(STEPS + 1)]

        def score_bank(s, j):
            return (before[s] + j) % 3

        def causal_pool(pool):
            pool.wait_ge(s_stage, 18)
            nc.gpsimd.memset(future, 0.0).then_inc(s_const, 1)
            pool.wait_ge(s_const, 2)
            own = future[0:TP, NODES - TP:NODES]
            nc.gpsimd.affine_select(out=own, in_=own, compare_op=ALU.is_ge, fill=NEG, base=0,
                                    pattern=[[-1, TP]], channel_multiplier=1).then_inc(s_const, 1)

        def causal_dve(dve):
            nc.vector.memset(qz_c, 0.0).then_inc(s_zeroed, 1)
            dve.wait_ge(s_const, 3)

            def mask(s):
                t, h = divmod(s, HEADS)
                width = (t + 1) * TP
                if s >= 2:
                    dve.wait_ge(b_tp, s - 1)
                for j, (c0, c1) in enumerate(parts[s]):
                    dve.wait_ge(b_s, before[s] + j + 1)
                    nc.vector.tensor_tensor_reduce(
                        out=S_c[s % 2][0:TP, c0:c1], in0=bank(score_bank(s, j))[0:TP, 0:c1 - c0],
                        in1=future[0:TP, NODES - width + c0:NODES - width + c1], scale=1.0, scalar=LOWEST,
                        op0=ALU.add, op1=ALU.max, accum_out=mx3_c[0:TP, j:j + 1]).then_inc(b_m, 1)
                dve.wait_ge(b_m, before[s + 1])
                link(dve, nc.vector.tensor_reduce(mx_c[0:TP, :], mx3_c[0:TP, 0:len(parts[s])], AX_X, ALU.max))
                nc.vector.tensor_scalar(nmx_c[s % 2][0:TP, :], mx_c[0:TP, :], -1.0, None, ALU.mult).then_inc(b_nm, 1)

            def finish(t):
                dve.wait_ge(b_e, HEADS * (t + 1))
                link(dve, nc.vector.reciprocal(rden_c[0:TP, :], den_c[t % 2][0:TP, :]))
                dve.wait_ge(b_pv, HEADS * (t + 1))
                if t >= 1:
                    dve.wait_ge(b_tr, t)
                nc.vector.tensor_tensor(row_c[0:TP, :].rearrange("p (h n) -> p h n", h=HEADS),
                                        bank(6)[0:TP, :].rearrange("p (h n) -> p h n", h=HEADS),
                                        rden_c[0:TP, :].unsqueeze(2).to_broadcast([TP, HEADS, DH]),
                                        ALU.mult).then_inc(b_row, 1)

            mask(0)
            for s in range(STEPS):
                t, h = divmod(s, HEADS)
                if s + 1 < STEPS:
                    mask(s + 1)
                if h == 0 and t >= 1:
                    finish(t - 1)
            finish(TILES - 1)
            leave_stage(dve, "DVE")

        def causal_act(act):
            act.wait_ge(s_zeroed, 2)

            def pad_q(t):
                if t >= 1:
                    act.wait_ge(b_s, before[HEADS * t])
                by_pair = qz_c.rearrange("p (j e) n -> p j e n", e=2)
                for e in range(2):
                    last = nc.scalar.activation(by_pair[64 * e:64 * e + 64, :, e, :],
                                                qT_f[64 * e:64 * e + 64, :, tok(t)], ACT.Copy)
                last.then_inc(b_qz, 1)

            def exps(s):
                t, h = divmod(s, HEADS)
                act.wait_ge(b_nm, s + 1)
                if h == 0 and t >= 2:
                    act.wait_ge(b_row, t - 1)
                b = S_c[s % 2][0:TP, 0:(t + 1) * TP]
                nc.scalar.activation(b, b, ACT.Exp, bias=nmx_c[s % 2][0:TP, :],
                                     accum_out=den_c[t % 2][0:TP, h:h + 1]).then_inc(b_e, 1)

            def row_T(t):
                act.wait_ge(b_tr, t + 1)
                nc.scalar.activation(aT_c, chunks(bank(7)[:, :], TP), ACT.Copy).then_inc(b_aT, 1)
                act.wait_ge(b_y, t + 1)
                nc.scalar.activation(yT[:, :, tok(t)], chunks(bank(7)[:, :], TP), ACT.Copy).then_inc(b_yT, 1)

            pad_q(0)
            exps(0)
            for s in range(STEPS):
                t, h = divmod(s, HEADS)
                if s + 1 < STEPS:
                    exps(s + 1)
                act.wait_ge(b_tp, s + 1)
                for b0 in range(0, t + 1, 4):
                    n = min(4, t + 1 - b0)
                    last = nc.scalar.activation(
                        pTc_v[0:TP, b0:b0 + n, :], bank(3 + b0 // 4)[0:TP, 0:128 * n]
                        .rearrange("p (b n) -> p b n", n=128)[:, :, 0:TP], ACT.Copy)
                last.then_inc(b_pt, 1)
                if h == 6 and t + 1 < TILES:
                    pad_q(t + 1)
                if h == 2 and t >= 1:
                    row_T(t - 1)
            row_T(TILES - 1)
            leave_stage(act, "ACT")

        def causal_pe(pe):
            def scores(s):
                t, h = divmod(s, HEADS)
                if h == 0:
                    pe.wait_ge(b_qz, t + 1)
                for j, (c0, c1) in enumerate(parts[s]):
                    if before[s] + j >= 3:
                        pe.wait_ge(b_m, before[s] + j - 2)
                    nc.tensor.matmul(bank(score_bank(s, j))[0:TP, 0:c1 - c0], qz_c[:, h, :],
                                     kT_f[:, h // 2, c0:c1], start=True, stop=True).then_inc(b_s, 1)

            def turn(s):
                t = s // HEADS
                pe.wait_ge(b_e, s + 1)
                if s >= 1:
                    pe.wait_ge(b_pt, s)
                for b in range(t + 1):
                    last = nc.tensor.transpose(banks[0:TP, 3 * BANK + 128 * b:3 * BANK + 128 * b + TP],
                                               S_c[s % 2][0:TP, b * TP:(b + 1) * TP], ident[0:TP, 0:TP])
                last.then_inc(b_tp, 1)

            def values(s):
                t, h = divmod(s, HEADS)
                pe.wait_ge(b_pt, s + 1)
                if h == 0 and t >= 1:
                    pe.wait_ge(b_row, t)
                for b in range(t + 1):
                    last = nc.tensor.matmul(bank(6)[0:TP, h * DH:(h + 1) * DH], pTc_v[0:TP, b, :],
                                            V_f[0:TP, b, h * DH:(h + 1) * DH], start=(b == 0), stop=(b == t))
                last.then_inc(b_pv, 1)

            def turn_row(t):
                pe.wait_ge(b_row, t + 1)
                if t >= 1:
                    pe.wait_ge(b_yT, t)
                transpose_tile(chunks(bank(7)[:, :], TP), row_c[0:TP, :]).then_inc(b_tr, 1)

            def out(t):
                pe.wait_ge(b_aT, t + 1)
                for m in range(KC):
                    for k in range(KC):
                        last = nc.tensor.matmul(bank(7)[:, m * TP:(m + 1) * TP], wo_f[:, k, m * 128:(m + 1) * 128],
                                                aT_c[:, k, :], start=(k == 0), stop=(k == KC - 1))
                last.then_inc(b_y, 1)

            scores(0)
            scores(1)
            for s in range(STEPS):
                t, h = divmod(s, HEADS)
                turn(s)
                if h == 1 and t >= 1:
                    turn_row(t - 1)
                if s + 2 < STEPS:
                    scores(s + 2)
                values(s)
                if h == 2 and t >= 1:
                    out(t - 1)
            turn_row(TILES - 1)
            out(TILES - 1)
            leave_stage(pe, "PE")

        NH = EXPERTS * FF // 128
        w1_e = arena[:, 2 * SLOT:2 * SLOT + KC * EXPERTS * FF].rearrange("p (k n) -> p k n", k=KC)
        w2_e = arena[:, 4 * SLOT:4 * SLOT + NH * C].rearrange("p (k n) -> p k n", k=NH)
        space = Space(BUF, TOP)
        gw_e = chunks(space.take(KC * EXPERTS), EXPERTS)
        gb_e = space.take(EXPERTS)
        b1_e = space.take(NH)
        b2_e = space.take(C)
        gate = space.take(TILES * EXPERTS)
        gsum = space.take(2 * TILES)
        gateT = space.take(TILES * 128)
        hT_e = [chunks(space.take(NH * TP), TP, NH) for _ in range(2)]
        s_we = sem("expert_weights_loaded")
        e_gl = sem("gate_logits_ready")
        e_gs = sem("gate_logits_shifted")
        e_ge = sem("gate_exponentials_ready")
        e_g = sem("gates_ready")
        e_gt = sem("gates_transposed")
        e_gT = sem("gatesT_copied")
        e_h = sem("expert_hidden_ready")
        e_a = sem("expert_gelu_ready")
        e_b = sem("expert_biases_ready")
        e_o = sem("expert_out_ready")
        e_x = sem("expert_added")

        def expert_sp(sp):
            sp.wait_ge(s_stage, 21)
            load(sp, gw_e.rearrange("p k n -> p (k n)"), "L0_ffn_gate_W", s_we)
            for b, n in ((gb_e, "gate_b"), (b1_e, "b1")):
                load(sp, b, "L0_ffn_" + n, s_we)
            sp.dma_start(b2_e[0:EXPERTS, :], d["L0_ffn_b2"]).then_inc(s_we, 16)
            sp.dma_start(w1_e.rearrange("p k n -> p (k n)"), d["L0_ffn_W1"]).then_inc(s_we, 16)
            sp.dma_start(w2_e.rearrange("p k n -> p (k n)"), d["L0_ffn_W2"]).then_inc(s_we, 16)

        def expert_dve(dve):
            g = gate[0:TP, :].rearrange("p (t e) -> p t e", e=EXPERTS)
            dve.wait_ge(s_we, 16 * 6)
            dve.wait_ge(e_gl, 1)
            link(dve, nc.vector.tensor_tensor(
                g, bank(0)[0:TP, 0:TILES * EXPERTS].rearrange("p (t e) -> p t e", e=EXPERTS),
                gb_e[0:TP, :].unsqueeze(1).to_broadcast([TP, TILES, EXPERTS]), ALU.add))
            link(dve, nc.vector.tensor_reduce(gsum[0:TP, 0:TILES], g, AX_X, ALU.max))
            nc.vector.tensor_tensor(g, g, gsum[0:TP, 0:TILES].unsqueeze(2).to_broadcast([TP, TILES, EXPERTS]),
                                    ALU.subtract).then_inc(e_gs, 1)
            dve.wait_ge(e_ge, 1)
            link(dve, nc.vector.tensor_reduce(gsum[0:TP, TILES:2 * TILES], g, AX_X, ALU.add))
            link(dve, nc.vector.reciprocal(gsum[0:TP, 0:TILES], gsum[0:TP, TILES:2 * TILES]))
            nc.vector.tensor_tensor(g, g, gsum[0:TP, 0:TILES].unsqueeze(2).to_broadcast([TP, TILES, EXPERTS]),
                                    ALU.mult).then_inc(e_g, 1)
            dve.wait_ge(e_g, 1)
            for t in range(TILES):
                x = X[0:TP, t, :]
                dve.wait_ge(e_b, t + 1)
                nc.vector.tensor_tensor(x, bank(1)[0:TP, :], x, ALU.add).then_inc(e_x, 1)
                for e in range(EXPERTS):
                    n = (EXPERTS + 1) * t + e + 1
                    dve.wait_ge(e_x, n)
                    dve.wait_ge(e_o, EXPERTS * t + e + 1)
                    nc.vector.scalar_tensor_tensor(
                        out=x, in0=bank(5 + (EXPERTS * t + e) % 3)[0:TP, :],
                        scalar=gate[0:TP, EXPERTS * t + e:EXPERTS * t + e + 1], in1=x,
                        op0=ALU.mult, op1=ALU.add).then_inc(e_x, 1)
            leave_stage(dve, "DVE")

        def expert_act(act):
            act.wait_ge(s_we, 16 * 6)
            act.wait_ge(e_gs, 1)
            nc.scalar.activation(gate[0:TP, :], gate[0:TP, :], ACT.Exp).then_inc(e_ge, 1)
            act.wait_ge(e_gt, 1)
            for b in range(3):
                n = min(4, TILES - 4 * b) * 128
                last = nc.scalar.activation(
                    gateT[0:EXPERTS, 512 * b:512 * b + n].rearrange("p (b n) -> p b n", n=128)[:, :, 0:TP],
                    bank(5 + b)[0:EXPERTS, 0:n].rearrange("p (b n) -> p b n", n=128)[:, :, 0:TP], ACT.Copy)
            last.then_inc(e_gT, 1)
            for t in range(TILES):
                if t >= 2:
                    act.wait_ge(e_o, EXPERTS * (t - 1))
                for a in range(NH // 4):
                    n = NH // 4 * t + a
                    act.wait_ge(e_h, n + 1)
                    for m in range(4):
                        c = 4 * a + m
                        last = nc.scalar.activation(hT_e[t % 2][:, c, :], bank(2 + n % 3)[:, m * TP:(m + 1) * TP],
                                                    ACT.Gelu_apprx_tanh, bias=b1_e[:, c:c + 1])
                    last.then_inc(e_a, 1)
            leave_stage(act, "ACT")

        def expert_pe(pe):
            pe.wait_ge(s_we, 16 * 6)
            for t in range(TILES):
                for k in range(KC):
                    last = nc.tensor.matmul(bank(0)[0:TP, EXPERTS * t:EXPERTS * (t + 1)], yT[:, k, tok(t)],
                                            gw_e[:, k, :], start=(k == 0), stop=(k == KC - 1))
            last.then_inc(e_gl, 1)

            def hidden(t):
                for a in range(NH // 4):
                    n = NH // 4 * t + a
                    if n >= 3:
                        pe.wait_ge(e_a, n - 2)
                    for m in range(4):
                        c = 4 * a + m
                        for k in range(KC):
                            last = nc.tensor.matmul(bank(2 + n % 3)[:, m * TP:(m + 1) * TP],
                                                    w1_e[:, k, c * 128:(c + 1) * 128], yT[:, k, tok(t)],
                                                    start=(k == 0), stop=(k == KC - 1))
                    last.then_inc(e_h, 1)

            pe.wait_ge(e_g, 1)
            for t in range(TILES):
                last = nc.tensor.transpose(banks[0:EXPERTS, 5 * BANK + 128 * t:5 * BANK + 128 * t + TP],
                                           gate[0:TP, EXPERTS * t:EXPERTS * (t + 1)], ident[0:TP, 0:TP])
            last.then_inc(e_gt, 1)
            hidden(0)
            pe.wait_ge(e_gT, 1)
            for t in range(TILES):
                if t >= 1:
                    pe.wait_ge(e_x, (EXPERTS + 1) * (t - 1) + 1)
                nc.tensor.matmul(bank(1)[0:TP, :], gateT[0:EXPERTS, 128 * t:128 * t + TP], b2_e[0:EXPERTS, :],
                                 start=True, stop=True).then_inc(e_b, 1)
                if t + 1 < TILES:
                    hidden(t + 1)
                for e in range(EXPERTS):
                    n = EXPERTS * t + e
                    pe.wait_ge(e_a, NH // 4 * t + e // 2 + 1)
                    if n >= 3:
                        u, f = divmod(n - 3, EXPERTS)
                        pe.wait_ge(e_x, (EXPERTS + 1) * u + f + 2)
                    for c in range(2):
                        last = nc.tensor.matmul(bank(5 + n % 3)[0:TP, :], hT_e[t % 2][:, 2 * e + c, :],
                                                w2_e[:, 2 * e + c, :], start=(c == 0), stop=(c == 1))
                    last.then_inc(e_o, 1)
            leave_stage(pe, "PE")

        L1_STAGE = 24
        wgcn = chunks(arena[:, BIG:BIG + KC * C], C)
        wqkv = arena[:, BIG + KC * C:BIG + 4 * KC * C].rearrange("p (k n) -> p k n", k=KC)
        H_n, Q_n, K_n, V_n = (rows(slot[i]) for i in range(4))
        adj = [arena[0:TP, SLOT + b * NODES:SLOT + (b + 1) * NODES] for b in range(4)] \
            + [arena[0:TP, BIG + b * NODES:BIG + (b + 1) * NODES] for b in range(TILES - 4)]
        after_w = Space(BIG + 4 * KC * C, SMALL)
        wdense = chunks(after_w.take(KC * C), C)
        wT_n = after_w.take(NODES)
        wT_v = wT_n.rearrange("p (b n) -> p b n", b=TILES)
        space = Space(BUF, TOP)
        wproj = chunks(space.take(KC * C), C)
        bgcn, bdense, bproj, wq_bc, wk_bc = (space.take(C) for _ in range(5))
        zT_n = [chunks(space.take(C)) for _ in range(2)]
        prod = [space.take(C) for _ in range(2)]
        gspread = space.take(C)
        logit = space.take(TILES * HEADS)
        wtok = space.take(TILES * HEADS)
        st_n = space.take(8)
        gmask = space.take(C)
        s_wn = sem("l1_qkv_weights_loaded")
        s_wn2 = sem("l1_out_weights_loaded")
        s_an = sem("adjacency_loaded")
        n_tz = sem("l1_z_transposed")
        n_zT = sem("l1_zT_copied")
        n_proj = sem("l1_projected")
        n_ev = sem("l1_projection_read")
        o_pe = sem("global_step_of_pe")
        o_act = sem("global_step_of_act")
        o_dve = sem("global_step_of_dve")
        n_deg = sem("degrees_ready")
        n_hs = sem("h_scaled")
        n_agg = sem("neighbours_added")
        n_row = sem("l1_row_ready")
        n_tr = sem("l1_row_transposed")
        n_rT = sem("l1_rowT_copied")
        n_out = sem("l1_out_projected")
        n_x = sem("l1_out_added")

        def l1_sp(sp):
            sp.wait_ge(s_stage, L1_STAGE)
            sp.dma_start(wgcn.rearrange("p k n -> p (k n)"), d["L1_gnn_W_gcn"]).then_inc(s_wn, 16)
            sp.dma_start(wqkv.rearrange("p k n -> p (k n)"), d["L1_mix_w_qkv"]).then_inc(s_wn, 16)
            for b, n in ((bdense, "gnn_b_dense"), (bproj, "mix_b_proj"), (wq_bc, "mix_w_q"), (bgcn, "gnn_b_gcn"),
                         (wk_bc, "mix_w_k")):
                load(sp, b, "L1_" + n, s_wn)
            sp.dma_start(wdense.rearrange("p k n -> p (k n)"), d["L1_gnn_W_dense"]).then_inc(s_wn2, 16)
            sp.dma_start(wproj.rearrange("p k n -> p (k n)"), d["L1_mix_w_proj"]).then_inc(s_wn2, 16)
            sp.wait_ge(n_proj, 4 * TILES)
            for b in range(TILES):
                sp.dma_start(adj[b], d["adj"][tok(b), :]).then_inc(s_an, 16)

        def l1_dve(dve):
            ln_stats_dve(dve, X, 1e-5)
            for t in range(TILES):
                last = normalize(XN[0:TP, t, :], X[0:TP, t, :], t)
            last.then_inc(s_xn, 1)
            dve.wait_ge(s_wn, 16 * 7)
            link(dve, nc.vector.tensor_tensor(bproj[0:TP, :], bproj[0:TP, :], bdense[0:TP, :], ALU.add))

            def head_sums(t, row, by, dst):
                link(dve, nc.vector.tensor_tensor(prod[t % 2][0:TP, :], row, by[0:TP, :], ALU.mult))
                return nc.vector.tensor_reduce(dst[0:TP, t * HEADS:(t + 1) * HEADS],
                                               prod[t % 2][0:TP, :].rearrange("p (h n) -> p h n", h=HEADS),
                                               AX_X, ALU.add)

            for t in range(TILES):
                for j, m in enumerate((H_n, Q_n, K_n, V_n)):
                    dve.wait_ge(n_proj, 4 * t + j + 1)
                    nc.vector.tensor_copy(m[0:TP, t, :], bank(2 + j)[0:TP, :]).then_inc(n_ev, 1)
                dve.wait_ge(n_ev, 4 * t + 2)
                link(dve, head_sums(t, Q_n[0:TP, t, :], wq_bc, logit))
                link(dve, nc.vector.tensor_tensor(X[0:TP, t, :], X[0:TP, t, :], Q_n[0:TP, t, :], ALU.add))
                link(dve, nc.vector.tensor_tensor(X[0:TP, t, :], X[0:TP, t, :], bproj[0:TP, :], ALU.add))
            dve.wait_ge(n_ev, 4 * TILES)
            for r in range(2):
                if r == 1:
                    dve.wait_ge(o_pe, 4)
                    link(dve, nc.vector.tensor_tensor(gspread[0:TP, :], bank(5)[0:TP, :], wk_bc[0:TP, :], ALU.mult))
                    for t in range(TILES):
                        link(dve, head_sums(t, K_n[0:TP, t, :], gspread, logit))
                nc.vector.memset(st_n[0:8, 2:3], 0.0).then_inc(o_dve, 1)
                dve.wait_ge(o_act, 3 * r + 1)
                link(dve, nc.vector.tensor_reduce(st_n[0:8, 0:1], wT_n[0:8, :], AX_X, ALU.max))
                nc.vector.tensor_scalar(st_n[0:8, 1:2], st_n[0:8, 0:1], -(DH ** -0.5), None,
                                        ALU.mult).then_inc(o_dve, 1)
                dve.wait_ge(o_act, 3 * r + 2)
                link(dve, nc.vector.reciprocal(st_n[0:8, 3:4], st_n[0:8, 2:3]))
                nc.vector.tensor_scalar(wT_n[0:8, :], wT_n[0:8, :], st_n[0:8, 3:4], None,
                                        ALU.mult).then_inc(o_dve, 1)
                dve.wait_ge(o_pe, 4 * r + 3)
                nc.vector.tensor_tensor(gmask[0:8, :].rearrange("p (h n) -> p h n", h=HEADS),
                                        bank(4)[0:8, :].rearrange("p (h n) -> p h n", h=HEADS),
                                        ident[0:8, 0:8].unsqueeze(2).to_broadcast([8, HEADS, DH]),
                                        ALU.mult).then_inc(o_dve, 1)
            dve.wait_ge(o_pe, 8)
            link(dve, nc.vector.tensor_copy(gspread[0:TP, :], bank(5)[0:TP, :]))
            nc.vector.tensor_tensor(V_n[0:TP, :, :], V_n[0:TP, :, :],
                                    gspread[0:TP, :].unsqueeze(1).to_broadcast([TP, TILES, C]),
                                    ALU.mult).then_inc(o_dve, 1)
            dve.wait_ge(n_deg, 1)
            inverse_root_dve(dve, bank(6)[0:TP, 0:2 * TILES].rearrange("p (t n) -> p t n", n=2)[:, :, 0], 1.0)
            for t in range(TILES):
                nc.vector.tensor_scalar(H_n[0:TP, t, :], H_n[0:TP, t, :], rstd[0:TP, t:t + 1], None,
                                        ALU.mult).then_inc(n_hs, 1)
            dve.wait_ge(n_hs, TILES)

            def gcn_row(n):
                dve.wait_ge(n_agg, n + 1)
                if n >= 2:
                    dve.wait_ge(n_tr, n - 1)
                row = prod[n % 2][0:TP, :]
                link(dve, nc.vector.tensor_tensor(row, bank(n % 2)[0:TP, :], H_n[0:TP, n, :], ALU.add))
                nc.vector.scalar_tensor_tensor(out=row, in0=row, scalar=rstd[0:TP, n:n + 1], in1=bgcn[0:TP, :],
                                               op0=ALU.mult, op1=ALU.add).then_inc(n_row, 1)

            def add(n):
                t = n % TILES
                dve.wait_ge(n_out, n + 1)
                if n >= TILES:
                    dve.wait_ge(n_x, t + 1)
                nc.vector.tensor_tensor(X[0:TP, t, :], bank(4 + n % 2)[0:TP, :], X[0:TP, t, :],
                                        ALU.add).then_inc(n_x, 1)

            gcn_row(0)
            gcn_row(1)
            for n in range(2 * TILES):
                if n + 2 < TILES:
                    gcn_row(n + 2)
                add(n)
            dve.wait_ge(n_x, 2 * TILES)
            leave_stage(dve, "DVE")

        def l1_act(act):
            ln_stats_act(act)
            for t in range(TILES):
                act.wait_ge(n_tz, t + 1)
                if t >= 2:
                    act.wait_ge(n_proj, 4 * t - 4)
                nc.scalar.activation(zT_n[t % 2], chunks(bank(t % 2)[:, :], TP), ACT.Copy).then_inc(n_zT, 1)
            for r in range(2):
                act.wait_ge(o_pe, 4 * r + 1)
                for b in range(3):
                    n = min(4, TILES - 4 * b)
                    last = nc.scalar.activation(
                        wT_v[0:8, 4 * b:4 * b + n, :],
                        bank(b)[0:8, 0:128 * n].rearrange("p (b n) -> p b n", n=128)[:, :, 0:TP], ACT.Copy)
                last.then_inc(o_act, 1)
                act.wait_ge(o_dve, 4 * r + 2)
                nc.scalar.activation(wT_n[0:8, :], wT_n[0:8, :], ACT.Exp, bias=st_n[0:8, 1:2], scale=DH ** -0.5,
                                     accum_out=st_n[0:8, 2:3]).then_inc(o_act, 1)
                act.wait_ge(o_pe, 4 * r + 2)
                nc.scalar.activation(wtok[0:TP, :], bank(3)[0:TP, 0:TILES * HEADS], ACT.Copy).then_inc(o_act, 1)
            ln_stats_act(act)
            for n in range(2 * TILES):
                act.wait_ge(n_tr, n + 1)
                if n >= 2:
                    act.wait_ge(n_out, n - 1)
                nc.scalar.activation(zT_n[n % 2], chunks(bank(2 + n % 2)[:, :], TP), ACT.Copy).then_inc(n_rT, 1)
            leave_stage(act, "ACT")

        def l1_pe(pe):
            pe.wait_ge(s_xn, 2)
            pe.wait_ge(s_wn, 16 * 7)

            def turn_z(t):
                if t >= 2:
                    pe.wait_ge(n_zT, t - 1)
                transpose_tile(chunks(bank(t % 2)[:, :], TP), XN[0:TP, t, :]).then_inc(n_tz, 1)

            turn_z(0)
            for t in range(TILES):
                if t + 1 < TILES:
                    turn_z(t + 1)
                pe.wait_ge(n_zT, t + 1)
                for j in range(4):
                    if t >= 1:
                        pe.wait_ge(n_ev, 4 * t - 3 + j)
                    w = wgcn if j == 0 else wqkv[:, :, (j - 1) * C:j * C]
                    project(bank(2 + j)[0:TP, :], zT_n[t % 2], w).then_inc(n_proj, 1)
            for r in range(2):
                pe.wait_ge(o_dve, 4 * r + 1)
                for t in range(TILES):
                    last = nc.tensor.transpose(banks[0:HEADS, 128 * t:128 * t + TP],
                                               logit[0:TP, HEADS * t:HEADS * (t + 1)], ident[0:TP, 0:TP])
                last.then_inc(o_pe, 1)
                pe.wait_ge(o_dve, 4 * r + 3)
                for t in range(TILES):
                    last = nc.tensor.transpose(bank(3)[0:TP, HEADS * t:HEADS * (t + 1)],
                                               wT_v[0:HEADS, t, :], ident[0:HEADS, 0:HEADS])
                last.then_inc(o_pe, 1)
                pe.wait_ge(o_act, 3 * r + 3)
                for t in range(TILES):
                    last = nc.tensor.matmul(bank(4)[0:HEADS, :], wtok[0:TP, HEADS * t:HEADS * (t + 1)],
                                            (Q_n, K_n)[r][0:TP, t, :], start=(t == 0), stop=(t == TILES - 1))
                last.then_inc(o_pe, 1)
                pe.wait_ge(o_dve, 4 * r + 4)
                nc.tensor.matmul(bank(5)[0:TP, :], ones[0:HEADS, 0:TP], gmask[0:HEADS, :],
                                 start=True, stop=True).then_inc(o_pe, 1)
            pe.wait_ge(s_an, 16 * TILES)
            pe.wait_ge(s_wn2, 16 * 2)
            for b in range(TILES):
                for t in range(TILES):
                    last = nc.tensor.matmul(bank(6)[0:TP, 2 * b:2 * b + 2], adj[t][:, tok(b)], ones[0:TP, 0:2],
                                            start=(t == 0), stop=(t == TILES - 1))
            last.then_inc(n_deg, 1)

            def aggregate(n):
                if n >= 2:
                    pe.wait_ge(n_row, n - 1)
                for t in range(TILES):
                    pe.wait_ge(n_hs, t + 1)
                    last = nc.tensor.matmul(bank(n % 2)[0:TP, :], adj[t][:, tok(n)], H_n[0:TP, t, :],
                                            start=(t == 0), stop=(t == TILES - 1))
                last.then_inc(n_agg, 1)

            def turn(n):
                if n < TILES:
                    pe.wait_ge(n_row, n + 1)
                else:
                    pe.wait_ge(o_dve, 9)
                if n >= 2:
                    pe.wait_ge(n_rT, n - 1)
                row = prod[n % 2][0:TP, :] if n < TILES else V_n[0:TP, n - TILES, :]
                transpose_tile(chunks(bank(2 + n % 2)[:, :], TP), row).then_inc(n_tr, 1)

            def out(n):
                pe.wait_ge(n_rT, n + 1)
                if n >= 2:
                    pe.wait_ge(n_x, n - 1)
                project(bank(4 + n % 2)[0:TP, :], zT_n[n % 2], wdense if n < TILES else wproj).then_inc(n_out, 1)

            aggregate(0)
            for n in range(2 * TILES):
                if n + 1 < TILES:
                    aggregate(n + 1)
                turn(n)
                if n >= 1:
                    out(n - 1)
            out(2 * TILES - 1)
            leave_stage(pe, "PE")

        PEER_STAGE = 27
        PAIR_CELLS = TOPK * TOPK
        mem = Space(SLOT * 2, SMALL)
        wq_p, down_p = chunks(mem.take(KC * C), C), chunks(mem.take(KC * PAIR_CELLS), PAIR_CELLS)
        keys_p = [mem.take(4 * KEYS) for _ in range(2)]
        up_p = chunks(mem.take(2 * C), C, 2)
        zT_p, qT_p = ([chunks(mem.take(KC * TP)) for _ in range(2)] for _ in range(2))
        R_p = mem.take(HEADS * KEYS)
        S_p = [mem.take(HEADS * PAIR_CELLS) for _ in range(2)]
        M_p = [mem.take(HEADS * PAIR_CELLS) for _ in range(2)]
        G_p = [mem.take(PAIR_CELLS) for _ in range(2)]
        gw_p = mem.take(PAIR_CELLS)
        gwT_p = chunks(mem.take(2 * TP), TP, 2)
        v0_p, i0_p, f0_p = (mem.take(HEADS * TOPK) for _ in range(3))
        top_p, shift_p = ([mem.take(HEADS * TOPK) for _ in range(2)] for _ in range(2))
        nmax_p, rsum_p = ([mem.take(HEADS) for _ in range(2)] for _ in range(2))
        wsum_p = mem.take(PAIR_CELLS)
        s_wp = sem("peer_weights_loaded")
        p_q = sem("peer_q_ready")
        p_qT = sem("peer_qT_copied")
        p_h = sem("peer_hidden_ready")
        p_g = sem("peer_gelu_ready")
        p_s = sem("peer_similarities_ready")
        p_sr = sem("peer_similarities_read")
        p_top = sem("peer_tops_ready")
        p_e = sem("peer_exponentials_ready")
        p_gw = sem("peer_weighted_gelu_ready")
        s_out = sem("out_stored")
        Z0, R0 = TILES, 2 * TILES

        def peer_sp(sp):
            sp.wait_ge(s_stage, PEER_STAGE)
            for w, n in ((wq_p, "w_q"), (down_p, "down"), (up_p, "up")):
                sp.dma_start(w.rearrange("p k n -> p (k n)"), d["L1_ffn_" + n]).then_inc(s_wp, 16)
            sp.wait_ge(s_zeroed, 3)
            for h in range(HEADS):
                p = h % 4
                sp.dma_start(keys_p[h // 4][32 * p:32 * p + 32, KEYS * p:KEYS * (p + 1)],
                             d["L1_ffn_keys"][32 * h:32 * h + 32, :]).then_inc(s_wp, 16)
            for t in range(TILES):
                sp.wait_ge(n_x, R0 + t + 1)
                sp.dma_start(d["out"][tok(t), :], X[0:TP, t, :]).then_inc(s_out, 16)
            sp.wait_ge(s_out, 16 * TILES)

        def peer_dve(dve):
            for w in keys_p:
                last = nc.vector.memset(w, 0.0)
            last.then_inc(s_zeroed, 1)
            ln_stats_dve(dve, X, 1e-5)
            for t in range(TILES):
                last = normalize(XN[0:TP, t, :], X[0:TP, t, :], t)
            last.then_inc(s_xn, 1)
            hs = range(HEADS)

            def sims(h):
                return bank(4 + h // 2)[0:TP, KEYS * (h % 2):KEYS * (h % 2 + 1)]

            def cells(m, h):
                return m[0:TP, PAIR_CELLS * h:PAIR_CELLS * (h + 1)]

            def eight(m, h, a):
                return m[0:TP, TOPK * h + 8 * a:TOPK * h + 8 * a + 8]

            def by_head(m, n):
                return m[0:TP, :].rearrange("p (h n) -> p h n", n=n)

            def largest_keys(t):
                dve.wait_ge(p_s, t + 1)
                for h in hs:
                    last = nc.vector.max(eight(v0_p, h, 0), sims(h))
                link(dve, last)

            def next_keys(t):
                for h in hs:
                    nc.vector.match_replace(cells(R_p, h), eight(v0_p, h, 0), sims(h), LOWEST)
                    last = nc.vector.max_index(eight(i0_p, h, 0).bitcast(U32), eight(v0_p, h, 0), sims(h))
                last.then_inc(p_sr, 1)
                dve.wait_ge(p_sr, t + 1)
                for h in hs:
                    last = nc.vector.max(eight(v0_p, h, 1), cells(R_p, h))
                link(dve, last)
                for h in hs:
                    last = nc.vector.max_index(eight(i0_p, h, 1).bitcast(U32), eight(v0_p, h, 1), cells(R_p, h))
                link(dve, last)
                link(dve, nc.vector.tensor_copy(f0_p[0:TP, :], i0_p[0:TP, :].bitcast(U32)))

            def pairs(t):
                S, M, top = S_p[t % 2], M_p[t % 2], top_p[t % 2]
                link(dve, nc.vector.tensor_tensor(
                    S[0:TP, :].rearrange("p (h a b) -> p h a b", h=HEADS, a=TOPK),
                    by_head(v0_p, TOPK).unsqueeze(3).to_broadcast([TP, HEADS, TOPK, TOPK]),
                    by_head(f0_p, TOPK).unsqueeze(2).to_broadcast([TP, HEADS, TOPK, TOPK]), ALU.add))
                for h in hs:
                    last = nc.vector.max(eight(top, h, 0), cells(S, h))
                link(dve, last)
                for h in hs:
                    last = nc.vector.match_replace(cells(M, h), eight(top, h, 0), cells(S, h), LOWEST)
                link(dve, last)
                for h in hs:
                    last = nc.vector.max(eight(top, h, 1), cells(M, h))
                link(dve, last)
                for h in hs:
                    nc.vector.match_replace(cells(M, h), eight(top, h, 1), cells(M, h), LOWEST)
                largest = by_head(top, TOPK)[:, :, 0:1]
                nc.vector.tensor_scalar(nmax_p[t % 2][0:TP, :], largest[:, :, 0], -1.0, None, ALU.mult)
                nc.vector.tensor_tensor(by_head(shift_p[t % 2], TOPK), by_head(top, TOPK),
                                        largest.to_broadcast([TP, HEADS, TOPK]), ALU.subtract).then_inc(p_top, 1)

            def sums(t):
                dve.wait_ge(p_e, 2 * t + 1)
                link(dve, nc.vector.tensor_reduce(rsum_p[t % 2][0:TP, :], by_head(shift_p[t % 2], TOPK),
                                                  AX_X, ALU.add))
                nc.vector.reciprocal(rsum_p[t % 2][0:TP, :], rsum_p[t % 2][0:TP, :]).then_inc(p_top, 1)

            def weigh(t):
                S, M = S_p[t % 2], M_p[t % 2]
                dve.wait_ge(p_e, 2 * t + 2)
                link(dve, nc.vector.scalar_tensor_tensor(out=S[0:TP, :], in0=M[0:TP, :], scalar=LOWEST,
                                                         in1=S[0:TP, :], op0=ALU.is_equal, op1=ALU.mult))
                link(dve, nc.vector.tensor_reduce(wsum_p[0:TP, :], S[0:TP, :].rearrange("p (h n) -> p n h", h=HEADS),
                                                  AX_X, ALU.add))
                dve.wait_ge(p_g, t + 1)
                if t >= 1:
                    dve.wait_ge(n_tr, R0 + t)
                nc.vector.tensor_tensor(gw_p[0:TP, :], G_p[t % 2][0:TP, :], wsum_p[0:TP, :],
                                        ALU.mult).then_inc(p_gw, 1)

            def add(t):
                dve.wait_ge(n_out, R0 + t + 1)
                nc.vector.tensor_tensor(X[0:TP, t, :], bank(3)[0:TP, :], X[0:TP, t, :], ALU.add).then_inc(n_x, 1)

            for t in range(TILES):
                largest_keys(t)
                if t >= 1:
                    sums(t - 1)
                next_keys(t)
                if t >= 1:
                    weigh(t - 1)
                pairs(t)
                if t >= 1:
                    add(t - 1)
            sums(TILES - 1)
            weigh(TILES - 1)
            add(TILES - 1)

        def peer_act(act):
            ln_stats_act(act)
            bn_scale = 1.0 / (1.0 + 1e-5) ** 0.5

            def prepare(t):
                act.wait_ge(n_tz, Z0 + t + 1)
                if t >= 2:
                    act.wait_ge(p_q, t - 1)
                nc.scalar.activation(zT_p[t % 2], chunks(bank(0)[:, :], TP), ACT.Copy).then_inc(n_zT, 1)
                act.wait_ge(p_q, t + 1)
                if t >= 2:
                    act.wait_ge(p_s, t - 1)
                nc.scalar.activation(qT_p[t % 2], chunks(bank(1)[:, :], TP), ACT.Copy,
                                     scale=bn_scale).then_inc(p_qT, 1)
                act.wait_ge(p_h, t + 1)
                if t >= 2:
                    act.wait_ge(p_gw, t - 1)
                nc.scalar.activation(G_p[t % 2][0:TP, :], bank(2)[0:TP, 0:PAIR_CELLS],
                                     ACT.Gelu_apprx_tanh).then_inc(p_g, 1)

            prepare(0)
            for t in range(TILES):
                if t + 1 < TILES:
                    prepare(t + 1)
                S = S_p[t % 2]
                act.wait_ge(p_top, 2 * t + 1)
                nc.scalar.activation(shift_p[t % 2][0:TP, :], shift_p[t % 2][0:TP, :], ACT.Exp).then_inc(p_e, 1)
                for h in range(HEADS):
                    c = slice(PAIR_CELLS * h, PAIR_CELLS * (h + 1))
                    last = nc.scalar.activation(S[0:TP, c], S[0:TP, c], ACT.Exp, bias=nmax_p[t % 2][0:TP, h:h + 1])
                act_link(act, last)
                act.wait_ge(p_top, 2 * t + 2)
                for h in range(HEADS):
                    c = slice(PAIR_CELLS * h, PAIR_CELLS * (h + 1))
                    last = nc.scalar.activation(S[0:TP, c], S[0:TP, c], ACT.Copy, scale=rsum_p[t % 2][0:TP, h:h + 1])
                last.then_inc(p_e, 1)
                act.wait_ge(n_tr, R0 + t + 1)
                nc.scalar.activation(gwT_p, chunks(bank(3)[:, :], TP, 2), ACT.Copy).then_inc(n_rT, 1)

        def peer_pe(pe):
            pe.wait_ge(s_xn, 3)
            pe.wait_ge(s_wp, 16 * (3 + HEADS))

            def prepare(t):
                if t >= 1:
                    pe.wait_ge(n_zT, Z0 + t)
                transpose_tile(chunks(bank(0)[:, :], TP), XN[0:TP, t, :]).then_inc(n_tz, 1)
                pe.wait_ge(n_zT, Z0 + t + 1)
                if t >= 1:
                    pe.wait_ge(p_qT, t)
                for m in range(KC):
                    for k in range(KC):
                        last = nc.tensor.matmul(bank(1)[:, m * TP:(m + 1) * TP], wq_p[:, k, m * 128:(m + 1) * 128],
                                                zT_p[t % 2][:, k, :], start=(k == 0), stop=(k == KC - 1))
                last.then_inc(p_q, 1)
                pe.wait_ge(p_qT, t + 1)
                if t >= 1:
                    pe.wait_ge(p_g, t)
                project(bank(2)[0:TP, 0:PAIR_CELLS], qT_p[t % 2], down_p, n=PAIR_CELLS).then_inc(p_h, 1)
                if t >= 1:
                    pe.wait_ge(p_sr, t)
                for b in range(HEADS // 2):
                    last = nc.tensor.matmul(bank(4 + b)[0:TP, :], qT_p[t % 2][:, b // 2, :],
                                            keys_p[b // 2][:, 2 * KEYS * (b % 2):2 * KEYS * (b % 2 + 1)],
                                            start=True, stop=True)
                last.then_inc(p_s, 1)

            prepare(0)
            for t in range(TILES):
                if t + 1 < TILES:
                    prepare(t + 1)
                pe.wait_ge(p_gw, t + 1)
                if t >= 1:
                    pe.wait_ge(n_x, R0 + t)
                for k in range(2):
                    last = nc.tensor.transpose(bank(3)[:, k * TP:(k + 1) * TP], gw_p[0:TP, k * 128:(k + 1) * 128],
                                               ident[0:TP, 0:TP])
                last.then_inc(n_tr, 1)
                pe.wait_ge(n_rT, R0 + t + 1)
                project(bank(3)[0:TP, :], gwT_p, up_p, k=2).then_inc(n_out, 1)

        block = ctx.enter_context(nc.Block())

        @block.sync
        def _(sp):
            const_sp(sp)
            gnn_w_sp(sp)
            zero_table(sp)
            mix_sp(sp)
            mix_bias_sp(sp)
            gnn_sp(sp)
            att_sp(sp)
            ff_sp(sp)
            ffn_sp(sp)
            expert_sp(sp)
            l1_sp(sp)
            peer_sp(sp)

        @block.gpsimd
        def _(pool):
            const_pool(pool)
            edges_pool(pool)
            causal_pool(pool)

        @block.scalar
        def _(act):
            edges_act(act)
            mix_act(act)
            gnn_act(act)
            att_act(act)
            ff_act(act)
            ffn_act(act)
            causal_act(act)
            expert_act(act)
            l1_act(act)
            peer_act(act)

        @block.vector
        def _(dve):
            edges_dve(dve)
            mix_dve(dve)
            gnn_dve(dve)
            att_dve(dve)
            ff_dve(dve)
            ffn_dve(dve)
            causal_dve(dve)
            expert_dve(dve)
            l1_dve(dve)
            peer_dve(dve)

        @block.tensor
        def _(pe):
            edges_pe(pe)
            mix_pe(pe)
            gnn_pe(pe)
            att_pe(pe)
            ff_pe(pe)
            ffn_pe(pe)
            causal_pe(pe)
            expert_pe(pe)
            l1_pe(pe)
            peer_pe(pe)




def scratch(nc, d):
    d["table"] = nc.dram_tensor("edge_table", (TABLE_ROWS, ROW), F32).ap()
    d["adj"] = nc.dram_tensor("adjacency", (NODES, NODES), F32).ap()


def lay_out(a):
    import numpy as np

    def w4(w):
        k = w.shape[0] // 128
        return np.ascontiguousarray(w.reshape(k, 128, -1).transpose(1, 0, 2).reshape(128, -1))

    def row(v):
        return np.ascontiguousarray(v.reshape(1, -1))

    def col(v):
        return np.ascontiguousarray(v.reshape(-1, 128).T)

    a = {k: np.asarray(v) for k, v in a.items()}
    o = {"x": np.ascontiguousarray(a["x"]),
         "src": np.ascontiguousarray(a["src"].reshape(TP, EC)),
         "dst": np.ascontiguousarray(a["dst"].reshape(TP, EC)),
         "edge_attr_8": np.ascontiguousarray(a["edge_attr_8"].reshape(TP, EC * HEADS))}
    for n in ("Wq", "Wk", "Wv", "Wo", "W1", "W2"):
        o["L0_gnn_" + n] = w4(a["L0_gnn_" + n].T)
    for n in ("bq", "bk", "bv", "bo", "b2"):
        o["L0_gnn_" + n] = row(a["L0_gnn_" + n])
    for n in ("ln_att_g", "ln_att_b", "ln_ff_g", "ln_ff_b", "b1"):
        o["L0_gnn_" + n] = col(a["L0_gnn_" + n])
    for n in ("Wq", "Wk", "Wv", "Wo", "W1", "W2"):
        w = a["L0_mix_" + n]
        if n == "Wo":
            w = w.reshape(C, C)
        o["L0_mix_" + n] = w4(w.reshape(w.shape[0], -1))
    for n in ("bq", "bk", "bv", "bo", "ln1_scale", "ln1_bias", "b2", "ln2_scale", "ln2_bias"):
        o["L0_mix_" + n] = row(a["L0_mix_" + n])
    o["L0_mix_b1"] = col(a["L0_mix_b1"])
    for n in ("Wq", "Wk", "Wv", "Wo", "gate_W"):
        o["L0_ffn_" + n] = w4(a["L0_ffn_" + n])
    for n in ("ln_g", "ln_b"):
        o["L0_ffn_" + n] = col(a["L0_ffn_" + n])
    for n in ("qn_g", "kn_g"):
        o["L0_ffn_" + n] = np.ascontiguousarray(np.tile(a["L0_ffn_" + n], 2).reshape(128, 1))
    o["L0_ffn_gate_b"] = row(a["L0_ffn_gate_b"])
    o["L0_ffn_W1"] = w4(a["L0_ffn_W1"].transpose(1, 0, 2).reshape(C, EXPERTS * FF))
    o["L0_ffn_b1"] = col(a["L0_ffn_b1"])
    o["L0_ffn_W2"] = w4(a["L0_ffn_W2"].reshape(EXPERTS * FF, C))
    o["L0_ffn_b2"] = np.ascontiguousarray(a["L0_ffn_b2"])
    o["L1_gnn_W_gcn"], o["L1_gnn_W_dense"] = w4(a["L1_gnn_W_gcn"]), w4(a["L1_gnn_W_dense"])
    o["L1_gnn_b_gcn"], o["L1_gnn_b_dense"] = row(a["L1_gnn_b_gcn"]), row(a["L1_gnn_b_dense"])
    o["L1_mix_w_qkv"] = w4(a["L1_mix_w_qkv"].T)
    o["L1_mix_w_proj"] = w4(a["L1_mix_w_proj"].T)
    for n in ("b_proj", "w_q", "w_k"):
        o["L1_mix_" + n] = row(a["L1_mix_" + n])
    o["L1_ffn_w_q"] = w4(a["L1_ffn_w_q"])
    o["L1_ffn_keys"] = np.ascontiguousarray(a["L1_ffn_keys"][:, :, 0, :].transpose(0, 2, 1).reshape(HEADS * 32, KEYS))
    o["L1_ffn_down"] = w4(a["L1_ffn_weight_down_embed"][:TOPK * TOPK].T)
    o["L1_ffn_up"] = w4(a["L1_ffn_weight_up_embed"][:TOPK * TOPK])
    return o


def kernel(**inputs):
    import concourse.bacc as bacc
    from concourse import mybir as mb
    from concourse.bass_utils import run_bass_kernel_spmd

    arrays = lay_out(inputs)
    nc = bacc.Bacc("TRN2", target_bir_lowering=False, num_devices=1)
    d = {k: nc.dram_tensor(k, v.shape, mb.dt.from_np(v.dtype), kind="ExternalInput").ap()
         for k, v in arrays.items()}
    scratch(nc, d)
    d["out"] = nc.dram_tensor("out", (NODES, C), F32, kind="ExternalOutput").ap()
    gps_two_layers(nc, d)
    r = run_bass_kernel_spmd(nc, [arrays], core_ids=[0])
    return r.results[0]["out"]
```

```python
from contextlib import ExitStack

import concourse.bass as bass
from concourse import mybir

ALU = mybir.AluOpType
ACT = mybir.ActivationFunctionType
AX_X = mybir.AxisListType.X
F32 = mybir.dt.float32
I32 = mybir.dt.int32
U32 = mybir.dt.uint32
BF16 = mybir.dt.bfloat16

NODES = 1250
TP = 125
TILES = NODES // TP
C = 512
KC = C // 128
HEADS = 8
DH = C // HEADS
PAIRS = HEADS // 2
EDGES = 40000
EC = EDGES // TP
GE = 4
GROUPS = EC // GE
ROW = HEADS + 1
CELLS = NODES * NODES
TABLE_ROWS = CELLS + GE * TP
HID = 1024
FF = 256
EXPERTS = 8
KEYS = 256
TOPK = 16
NEG = -1.0e30
LOWEST = -3.0e38
BANK = 512
SLOT = 5120


def gps_two_layers(nc, d):
    ctx = ExitStack()
    with ctx:
        def sem(name):
            return ctx.enter_context(nc.semaphore(name))

        TOP = 53200
        arena = ctx.enter_context(nc.sbuf_tensor("arena", [128, TOP], F32))
        banks = ctx.enter_context(nc.psum_tensor("banks", [128, 8 * BANK], F32))

        class Space:

            def __init__(self, at, end):
                self.at, self.end = at, end

            def take(self, n):
                self.at += n
                assert self.at <= self.end, (self.at, self.end)
                return arena[:, self.at - n:self.at]

        def bank(b, n=1):
            return banks[:, b * BANK:(b + n) * BANK]

        def rows(flat):
            return flat.rearrange("p (t c) -> p t c", c=C)

        def cols(flat, k=KC):
            return flat[:, 0:k * NODES].rearrange("p (k n) -> p k n", k=k)

        def chunks(flat, n=TP, k=KC):
            return flat[:, 0:k * n].rearrange("p (k n) -> p k n", k=k)

        def tok(t, n=1):
            return slice(t * TP, (t + n) * TP)

        X = rows(arena[:, 0:SLOT])
        XN = rows(arena[:, SLOT:2 * SLOT])
        slot = [arena[:, (2 + i) * SLOT:(3 + i) * SLOT] for i in range(4)]
        BIG = 6 * SLOT
        SMALL = 42480
        const = Space(SMALL, TOP)
        ident = const.take(128)
        ones = const.take(128)
        lnv = const.take(160)
        bn6 = lnv[:, 0:60].rearrange("p (t s) -> p t s", s=6)
        mv = lnv[:, 60:80].rearrange("p (t s) -> p t s", s=2)
        var_eps, sd, r0, ra, rstd = (lnv[:, 80 + 16 * i:80 + 16 * i + TILES] for i in range(5))
        kept = const.take(32)
        kept_mean, kept_rstd = kept[:, 0:TILES], kept[:, 16:16 + TILES]
        BUF = const.at

        s_dve = sem("dve_step")
        s_act = sem("act_step")
        s_var = sem("ln_variances_ready")
        s_sd = sem("ln_deviations_ready")
        s_stage = sem("stage_left")
        s_const = sem("constants_ready")
        s_x = sem("x_loaded")
        z_rows, z_turned, z_cols = sem("z_ready"), sem("z_transposed"), sem("zT_ready")
        Z_FF, Z_FFN = TILES, 2 * TILES
        s_zeroed = sem("buffer_zeroed")
        s_xn = sem("xn_ready")
        steps = {"dve": 0, "act": 0, "var": 0, "sd": 0, "PE": 0, "ACT": 0, "DVE": 0}

        def link(dve, ins):
            steps["dve"] += 1
            ins.then_inc(s_dve, 1)
            dve.wait_ge(s_dve, steps["dve"])

        def act_link(act, ins):
            steps["act"] += 1
            ins.then_inc(s_act, 1)
            act.wait_ge(s_act, steps["act"])

        def leave_stage(eng, name):
            steps[name] += 1
            eng.drain().then_inc(s_stage, 1)
            eng.wait_ge(s_stage, 3 * steps[name])

        def inverse_root_dve(dve, src, eps):
            steps["var"] += 1
            nc.vector.tensor_scalar(var_eps[0:TP, :], src, eps, None, ALU.add).then_inc(s_var, 1)
            dve.wait_ge(s_var, steps["var"])
            dve.wait_ge(s_sd, steps["var"])
            link(dve, nc.vector.reciprocal(r0[0:TP, :], sd[0:TP, :]))
            link(dve, nc.vector.tensor_tensor(ra[0:TP, :], var_eps[0:TP, :], r0[0:TP, :], ALU.mult))
            link(dve, nc.vector.tensor_tensor(ra[0:TP, :], ra[0:TP, :], r0[0:TP, :], ALU.mult))
            link(dve, nc.vector.tensor_scalar(ra[0:TP, :], ra[0:TP, :], -0.5, 1.5, ALU.mult, ALU.add))
            link(dve, nc.vector.tensor_tensor(rstd[0:TP, :], r0[0:TP, :], ra[0:TP, :], ALU.mult))

        def gather_stats(src, t):
            return nc.vector.bn_stats(bn6[0:TP, t, :], src[0:TP, t, :])

        def ln_stats_dve(dve, src, eps, gathered=False):
            for t in range(TILES - 1 if gathered else 0, TILES):
                last = gather_stats(src, t)
            link(dve, last)
            for t in range(TILES):
                last = nc.vector.bn_aggr(mv[0:TP, t, :], bn6[0:TP, t, :])
            link(dve, last)
            inverse_root_dve(dve, mv[0:TP, :, 1], eps)

        def ln_stats_act(act):
            steps["sd"] += 1
            act.wait_ge(s_var, steps["sd"])
            nc.scalar.activation(sd[0:TP, :], var_eps[0:TP, :], ACT.Sqrt).then_inc(s_sd, 1)

        def normalize(dst, src, t, mean=None, root=None):
            mean, root = mv[:, :, 0] if mean is None else mean, rstd if root is None else root
            return nc.vector.tensor_scalar(dst, src, mean[0:TP, t:t + 1], root[0:TP, t:t + 1],
                                           ALU.subtract, ALU.mult)

        def transpose_tile(dst, src):
            for k in range(KC):
                last = nc.tensor.transpose(dst[:, k, :], src[:, k * 128:(k + 1) * 128], ident[0:TP, 0:TP])
            return last

        def project(dst, xT, w, n=C, k=KC):
            for i in range(k):
                last = nc.tensor.matmul(dst, xT[:, i, :], w[:, i, 0:n], start=(i == 0), stop=(i == k - 1))
            return last

        def load(eng, dst, name, s):
            src = d[name]
            if src.shape[0] == 1:
                src = src[0].partition_broadcast(128)
            eng.dma_start(dst, src).then_inc(s, 16)


        space = Space(BUF, TOP)
        zeros = space.take(2250)

        UG = 4
        s_zero = sem("zeros_ready")
        s_table0 = [sem(f"table_zeroed_{v}") for v in range(2)]
        TURNS = GROUPS // UG
        edge = Space(36864, SMALL)
        vals = edge.take(EC * ROW)
        key = edge.take(EC)
        cell = edge.take(EC)
        away = edge.take(EC)
        later = edge.take(GE * TP)
        spill = edge.take(2 * GE)
        repeats = edge.take(UG * GE)
        keyT = edge.take(3 * 128)
        early = Space(2 * SLOT, 4 * SLOT)
        bias = early.take(EC * HEADS)
        src_i, dst_i, dst_f = (early.take(EC) for _ in range(3))
        rest = arena[:, 2 * SLOT:2 * SLOT + EC * ROW]
        parts3 = early.take(EC * ROW * 3 // 2).bitcast(BF16)
        by_part = parts3.rearrange("p (n w) -> p n w", w=3)
        hmax = space.take(48)
        keyrow = [space.take(UG * GE * TP) for _ in range(2)]
        same = [space.take(TP * (1 + 2 + 3 + 4) // 2).bitcast(BF16) for _ in range(UG)]
        total = space.take(UG * GE * ROW)
        s_sd_in = sem("edge_ends_loaded")
        s_bias = sem("edge_bias_loaded")
        s_key = sem("keys_ready")
        s_keyT = sem("keys_transposed")
        s_keyst = sem("key_rows_stored")
        s_pmax = sem("partition_maxima_ready")
        s_tmax = sem("maxima_transposed")
        s_hmax = sem("head_maxima_ready")
        s_bmax = sem("head_maxima_spread")
        s_shift = sem("bias_shifted")
        s_part = sem("weight_parts_ready")
        s_keyrow = [sem(f"key_row_loaded_{v}") for v in range(2)]
        s_same = sem("equal_keys_marked")
        s_first = sem("rows_of_repeats_ready")
        s_sum = sem("repeats_summed")
        s_group = sem("turn_done")
        s_scat = sem("group_scattered")

        def const_pool(pool):
            nc.gpsimd.memset(zeros, 0.0).then_inc(s_zero, 1)
            nc.gpsimd.memset(ident, 0.0)
            nc.gpsimd.memset(ones, 1.0)
            nc.gpsimd.iota(spill[0:TP, 0:GE].bitcast(I32), pattern=[[TP, GE]], base=CELLS,
                           channel_multiplier=1)
            nc.gpsimd.memset(later, 1.0).then_inc(s_zero, 1)
            pool.wait_ge(s_zero, 2)
            nc.gpsimd.affine_select(out=ident, in_=ident, compare_op=ALU.not_equal, fill=1.0, base=0,
                                    pattern=[[-1, 128]], channel_multiplier=1)
            own = later[0:TP, (GE - 1) * TP:GE * TP]
            nc.gpsimd.affine_select(out=own, in_=own, compare_op=ALU.is_gt, fill=0.0, base=0,
                                    pattern=[[-1, TP]], channel_multiplier=1).then_inc(s_const, 1)

        def const_sp(sp):
            sp.dma_start(src_i[0:TP, :].bitcast(I32), d["src"]).then_inc(s_sd_in, 16)
            sp.dma_start(dst_i[0:TP, :].bitcast(I32), d["dst"]).then_inc(s_sd_in, 16)
            sp.dma_start(bias[0:TP, 0:EC * HEADS], d["edge_attr_8"]).then_inc(s_bias, 16)
            sp.dma_start(X[0:TP, :, :], d["x"].rearrange("(t p) c -> p t c", p=TP)).then_inc(s_x, 16)

        ZERO = 2 * TP * zeros.shape[1]
        ZERO_PARTS = CELLS * ROW // ZERO
        ZERO_PAIRS = ZERO_PARTS // 2

        def zero_table(sp):
            sp.wait_ge(s_zero, 1)
            flat = d["table"].rearrange("r w -> (r w)")

            def part(n, v):
                sp.dma_start(flat[bass.ds(n * ZERO, ZERO)].rearrange("(p r a) -> p r a", p=TP, r=2),
                             zeros[0:TP, :].unsqueeze(1).to_broadcast([TP, 2, zeros.shape[1]])).then_inc(s_table0[v], 16)

            part(0, 0)
            part(1, 1)
            with sp.Fori(0, ZERO_PAIRS - 1) as i:
                for v in range(2):
                    sp.wait_ge(s_table0[v], i * 16 + 16)
                    part(i * 2 + (v + 2), v)
            sp.wait_ge(s_table0[0], 16 * ZERO_PAIRS)
            part(ZERO_PARTS - 1, 0)
            sp.dma_start(flat[CELLS * ROW:TABLE_ROWS * ROW].rearrange("(p a) -> p a", p=TP),
                         zeros[0:TP, 0:GE * ROW]).then_inc(s_table0[0], 16)

        def table_zeroed(eng):
            eng.wait_ge(s_table0[0], 16 * ZERO_PAIRS + 32)
            eng.wait_ge(s_table0[1], 16 * ZERO_PAIRS)

        KEY_BLOCKS = [(b, min(128, EC - 128 * b)) for b in range(-(-EC // 128))]

        def key_rows_sp(sp):
            sp.wait_ge(s_keyT, 2)
            for b, n in KEY_BLOCKS:
                sp.dma_start(d["key_rows"][b * 128:b * 128 + n, :], keyT[0:n, b * 128:b * 128 + TP]).then_inc(s_keyst, 16)

        def load_key_row(eng, turn, buf):
            n = UG * GE * TP
            flat = d["key_rows"].rearrange("c p -> (c p)")
            eng.dma_start(keyrow[buf][0:TP, :], flat[bass.ds(turn * n, n)].partition_broadcast(TP))\
                .then_inc(s_keyrow[buf], 16)

        def edges_dve(dve):
            dve.wait_ge(s_sd_in, 32)
            dve.wait_ge(s_const, 1)
            nc.vector.tensor_copy(key[0:TP, :], src_i[0:TP, :].bitcast(I32))
            nc.vector.tensor_copy(spill[0:TP, GE:2 * GE], spill[0:TP, 0:GE].bitcast(I32))
            link(dve, nc.vector.tensor_copy(dst_f[0:TP, :], dst_i[0:TP, :].bitcast(I32)))
            nc.vector.scalar_tensor_tensor(out=key[0:TP, :], in0=key[0:TP, :], scalar=float(NODES),
                                           in1=dst_f[0:TP, :], op0=ALU.mult, op1=ALU.add).then_inc(s_key, 1)
            dve.wait_ge(s_key, 1)
            nc.vector.tensor_tensor(away[0:TP, :].rearrange("p (g c) -> p g c", c=GE),
                                    spill[0:TP, GE:2 * GE].unsqueeze(1).to_broadcast([TP, GROUPS, GE]),
                                    key[0:TP, :].rearrange("p (g c) -> p g c", c=GE), ALU.subtract)
            dve.wait_ge(s_keyT, 1)
            for b, n in KEY_BLOCKS:
                last = nc.vector.tensor_copy(keyT[0:n, b * 128:b * 128 + TP], bank(2)[0:n, b * 128:b * 128 + TP])
            last.then_inc(s_keyT, 1)
            by_edge = vals[0:TP, :].rearrange("p (c w) -> p c w", w=ROW)
            nc.vector.memset(by_edge[:, :, HEADS:ROW], 1.0)
            dve.wait_ge(s_bias, 16)
            by_head = bias[0:TP, 0:EC * HEADS].rearrange("p (c h) -> p h c", h=HEADS)
            nc.vector.tensor_reduce(hmax[0:TP, 0:8], by_head, AX_X, ALU.max).then_inc(s_pmax, 1)
            dve.wait_ge(s_tmax, 1)
            link(dve, nc.vector.tensor_reduce(hmax[0:8, 8:9], bank(0)[0:8, 0:TP], AX_X, ALU.max))
            nc.vector.tensor_scalar(hmax[0:8, 16:24], ident[0:8, 0:8], hmax[0:8, 8:9], None,
                                    ALU.mult).then_inc(s_hmax, 1)
            dve.wait_ge(s_bmax, 1)
            link(dve, nc.vector.tensor_copy(hmax[0:TP, 24:32], bank(1)[0:TP, 0:8]))
            flat = bias[0:TP, 0:EC * HEADS].rearrange("p (c h) -> p c h", h=HEADS)
            nc.vector.tensor_tensor(flat, flat, hmax[0:TP, 24:32].unsqueeze(1).to_broadcast([TP, EC, HEADS]),
                                    ALU.subtract).then_inc(s_shift, 1)

            def turn(i, v):
                n = i * 2 + v
                dve.wait_ge(s_keyrow[v], i * 16 + 16)
                for u in range(UG):
                    at = 0
                    for c in range(GE):
                        w = (c + 1) * TP
                        last = nc.vector.scalar_tensor_tensor(
                            out=same[u][0:TP, at:at + w], in0=keyrow[v][0:TP, u * GE * TP:u * GE * TP + w],
                            scalar=key[0:TP, bass.ds(n * (UG * GE) + (u * GE + c), 1)],
                            in1=later[0:TP, GE * TP - w:GE * TP],
                            op0=ALU.is_equal, op1=ALU.mult, accum_out=repeats[0:TP, u * GE + c:u * GE + c + 1])
                        at += w
                    last.then_inc(s_same, 1)
                cols_n = bass.ds(n * (UG * GE), UG * GE)
                dve.wait_ge(s_same, n * UG + UG)
                nc.vector.scalar_tensor_tensor(out=repeats[0:TP, :], in0=repeats[0:TP, :], scalar=0.0,
                                               in1=away[0:TP, cols_n], op0=ALU.is_gt, op1=ALU.mult).then_inc(s_first, 1)
                dve.wait_ge(s_first, n * 3 + 1)
                nc.vector.tensor_tensor(cell[0:TP, cols_n].bitcast(U32), repeats[0:TP, :], key[0:TP, cols_n],
                                        ALU.add).then_inc(s_first, 1)
                dve.wait_ge(s_sum, n + 1)
                nc.vector.tensor_reduce(total[0:TP, :], bank(4 + v)[0:TP, 0:UG * GE * ROW * 3]
                                        .rearrange("p (n w) -> p n w", w=3), AX_X, ALU.add).then_inc(s_first, 1)
                dve.wait_ge(s_first, n * 3 + 3)
                span = bass.ds(n * (UG * GE * ROW), UG * GE * ROW)
                nc.vector.tensor_tensor(vals[0:TP, span], vals[0:TP, span], total[0:TP, :], ALU.add).then_inc(s_group, 1)
                dve.wait_ge(s_group, n + 1)

            with dve.Fori(0, TURNS // 2) as i:
                for v in range(2):
                    turn(i, v)
            leave_stage(dve, "DVE")

        def edges_act(act):
            act.wait_ge(s_shift, 1)
            by_edge = vals[0:TP, :].rearrange("p (c w) -> p c w", w=ROW)
            act_link(act, nc.scalar.activation(by_edge[:, :, 0:HEADS],
                                               bias[0:TP, :].rearrange("p (c h) -> p c h", h=HEADS), ACT.Exp))
            nc.scalar.activation(by_part[0:TP, :, 0], vals[0:TP, :], ACT.Copy).then_inc(s_part, 1)
            act.wait_ge(s_keyst, 16 * len(KEY_BLOCKS))
            for v in range(2):
                load_key_row(act, v, v)
            for w in (1, 2):
                act.wait_ge(s_part, 2 * w)
                nc.scalar.activation(by_part[0:TP, :, w], rest[0:TP, :], ACT.Copy).then_inc(s_part, 1)
            with act.Fori(0, TURNS // 2 - 1) as i:
                for v in range(2):
                    act.wait_ge(s_same, i * (2 * UG) + (v + 1) * UG)
                    load_key_row(act, i * 2 + (v + 2), v)
            leave_stage(act, "ACT")

        def parts_pool(pool):
            pool.wait_ge(s_part, 1)
            nc.gpsimd.tensor_tensor(rest[0:TP, :], vals[0:TP, :], by_part[0:TP, :, 0], ALU.subtract).then_inc(s_part, 1)
            pool.wait_ge(s_part, 3)
            nc.gpsimd.tensor_tensor(rest[0:TP, :], rest[0:TP, :], by_part[0:TP, :, 1], ALU.subtract).then_inc(s_part, 1)

        def edges_pe(pe):
            pe.wait_ge(s_const, 1)
            pe.wait_ge(s_key, 1)
            for b, n in KEY_BLOCKS:
                last = nc.tensor.transpose(bank(2)[0:n, b * 128:b * 128 + TP], key[0:TP, b * 128:b * 128 + n],
                                           ident[0:TP, 0:TP])
            last.then_inc(s_keyT, 1)
            pe.wait_ge(s_pmax, 1)
            nc.tensor.transpose(bank(0)[0:8, 0:TP], hmax[0:TP, 0:8], ident[0:TP, 0:TP]).then_inc(s_tmax, 1)
            pe.wait_ge(s_hmax, 1)
            nc.tensor.matmul(bank(1)[0:TP, 0:8], ones[0:8, 0:TP], hmax[0:8, 16:24],
                             start=True, stop=True).then_inc(s_bmax, 1)
            pe.wait_ge(s_part, 5)
            with pe.Fori(0, TURNS // 2) as i:
                for v in range(2):
                    for u in range(UG):
                        pe.wait_ge(s_same, i * (2 * UG) + (v * UG + u + 1))
                        for c0 in range(GE):
                            to = ROW * 3 * (u * GE + c0)
                            for c in range(c0, GE):
                                at = TP * (c * (c + 1) // 2 + c0)
                                last = nc.tensor.matmul(
                                    bank(4 + v)[0:TP, to:to + ROW * 3], same[u][0:TP, at:at + TP],
                                    parts3[0:TP, bass.ds(i * (2 * UG * GE * ROW * 3)
                                                         + ((v * UG + u) * GE + c) * ROW * 3, ROW * 3)],
                                    start=(c == c0), stop=(c == GE - 1))
                    last.then_inc(s_sum, 1)
            leave_stage(pe, "PE")

        def edges_pool(pool):
            parts_pool(pool)
            table_zeroed(pool)
            for g in range(GROUPS):
                if g % UG == 0:
                    pool.wait_ge(s_group, g // UG + 1)
                if g > 0:
                    pool.wait_ge(s_scat, 16 * GE * g)
                for c in range(GE * g, GE * (g + 1)):
                    pool.indirect_dma_start(
                        d["table"], bass.IndirectOffsetOnAxis(ap=cell[0:TP, c:c + 1].bitcast(U32), axis=0),
                        vals[0:TP, c * ROW:(c + 1) * ROW], None, compute_op=ALU.add).then_inc(s_scat, 16)

        TABLE_DONE = 16 * EC

        wm = Space(4 * SLOT, 6 * SLOT)
        wq_m, wk_m, wv_m = (chunks(wm.take(KC * C), C) for _ in range(3))
        wo_m = chunks(wm.take(KC * C), C)
        w1_m = chunks(wm.take(KC * FF), FF)
        w2_m = chunks(wm.take(2 * C), C, 2)
        qT_m = cols(slot[0])
        Hm = rows(slot[1])
        space = Space(BUF, TOP)
        bq_m, bk_m, bv_m, bo_m, b2_m = (space.take(C) for _ in range(5))
        ln1_s, ln1_b, ln2_s, ln2_b = (space.take(C) for _ in range(4))
        b1_m = space.take(2)
        xT_m = [chunks(space.take(C)) for _ in range(2)]
        q_m, k_m, v_m = space.take(C), space.take(C), space.take(C)
        kv_m = chunks(space.take(C), 128, PAIRS)
        ks_m = space.take(32)
        rd_m = space.take(8)
        f1_m = [chunks(space.take(2 * TP), TP, 2) for _ in range(2)]
        row_m = q_m
        s_wm = sem("mix_qkv_weights_loaded")
        s_wm2 = sem("mix_rest_weights_loaded")
        m_tx = sem("mix_x_transposed")
        m_xT = sem("mix_xT_copied")
        m_proj = sem("mix_projected")
        m_ev = sem("mix_projection_read")
        m_rows = sem("mix_rows_ready")
        m_kv = sem("mix_kv_added")
        m_tq = sem("mix_q_transposed")
        m_qT = sem("mix_qT_copied")
        m_kvb = sem("mix_kv_blocks_ready")
        m_nd = sem("mix_num_den_ready")
        m_att = sem("mix_attention_row_ready")
        m_ta = sem("mix_attention_transposed")
        m_aT = sem("mix_attention_T_copied")
        m_wo = sem("mix_out_projected")
        m_h = sem("mix_h_ready")
        m_h1 = sem("mix_h_normalized")
        m_th = sem("mix_h_transposed")
        m_hT = sem("mix_hT_copied")
        m_f1 = sem("mix_ff1_ready")
        m_r1 = sem("mix_relu_ready")
        m_f2 = sem("mix_ff2_ready")
        m_g = sem("mix_ff_added")
        m_xb = sem("mix_bias_added_to_x")

        def mix_sp(sp):
            for w, n in ((wq_m, "Wq"), (wk_m, "Wk"), (wv_m, "Wv")):
                sp.dma_start(w.rearrange("p k n -> p (k n)"), d["L0_mix_" + n]).then_inc(s_wm, 16)
            for w, n in ((wo_m, "Wo"), (w1_m, "W1"), (w2_m, "W2")):
                sp.dma_start(w.rearrange("p k n -> p (k n)"), d["L0_mix_" + n]).then_inc(s_wm2, 16)

        def mix_bias_sp(sp):
            sp.wait_ge(s_stage, 3)
            table_zeroed(sp)
            for b, n in ((bq_m, "bq"), (bk_m, "bk"), (bv_m, "bv")):
                load(sp, b, "L0_mix_" + n, s_wm)
            for b, n in ((bo_m, "bo"), (ln1_s, "ln1_scale"), (ln1_b, "ln1_bias"), (b2_m, "b2"),
                         (ln2_s, "ln2_scale"), (ln2_b, "ln2_bias"), (b1_m, "b1")):
                load(sp, b, "L0_mix_" + n, s_wm2)

        def mix_dve(dve):
            dve.wait_ge(s_x, 16)
            ln_stats_dve(dve, X, 1e-5)
            for t in range(TILES):
                normalize(XN[0:TP, t, :], X[0:TP, t, :], t).then_inc(s_xn, 1)
            nc.vector.memset(kv_m, 0.0)
            link(dve, nc.vector.memset(ks_m, 0.0))
            dve.wait_ge(s_wm, 16 * 6)
            for t in range(TILES):
                for j, (row, b) in enumerate(((q_m, bq_m), (k_m, bk_m), (v_m, bv_m))):
                    n = 3 * t + j
                    dve.wait_ge(m_proj, n + 1)
                    if t >= 1:
                        dve.wait_ge(m_kv, t)
                    nc.vector.tensor_tensor(row[0:TP, :], bank(2 + n % 3)[0:TP, :], b[0:TP, :],
                                            ALU.add).then_inc(m_ev, 1)
                dve.wait_ge(m_ev, 3 * t + 3)
                nc.vector.tensor_scalar(q_m[0:TP, :], q_m[0:TP, :], 0.0, 0.001, ALU.max, ALU.add)
                nc.vector.tensor_scalar(k_m[0:TP, :], k_m[0:TP, :], 0.0, 0.001, ALU.max, ALU.add).then_inc(m_rows, 1)
                if t == 0:
                    dve.wait_ge(s_xn, TILES)
                if t < TILES - 1:
                    gather_stats(XN, t)
                if t == TILES // 2:
                    dve.wait_ge(s_wm2, 16 * 10)
                if t >= TILES // 2:
                    for n in (2 * t - TILES, 2 * t - TILES + 1):
                        nc.vector.tensor_tensor(X[0:TP, n, :], X[0:TP, n, :], ln2_b[0:TP, :], ALU.add).then_inc(m_xb, 1)
            dve.wait_ge(m_kv, TILES)
            kv = bank(6)[:, :].rearrange("p (j n) -> p j n", j=PAIRS)
            for s in (0, 64):
                nc.vector.tensor_copy(kv_m[s:s + 64, :, s:s + 64], kv[s:s + 64, :, s:s + 64])
                last = nc.vector.tensor_copy(
                    ks_m[s:s + 64, s // 64:s // 64 + 31:10],
                    bank(7)[s:s + 64, 0:8].rearrange("p (j n) -> p j n", n=2)[:, :, 0])
            last.then_inc(m_kvb, 1)
            ln_stats_dve(dve, XN, 1e-5, gathered=True)
            nc.vector.tensor_copy(kept_mean[0:TP, :], mv[0:TP, :, 0])
            link(dve, nc.vector.tensor_copy(kept_rstd[0:TP, :], rstd[0:TP, :]))
            dve.wait_ge(s_wm2, 16 * 10)

            def attention_row(t):
                dve.wait_ge(m_nd, t + 1)
                link(dve, nc.vector.reciprocal(rd_m[0:TP, :], bank(2 + t % 2)[0:TP, 0:8]))
                if t >= 1:
                    dve.wait_ge(m_ta, t)
                nc.vector.tensor_tensor(row_m[0:TP, :].rearrange("p (h n) -> p h n", h=HEADS),
                                        bank(t % 2)[0:TP, :].rearrange("p (h n) -> p h n", h=HEADS),
                                        rd_m[0:TP, :].unsqueeze(2).to_broadcast([TP, HEADS, DH]),
                                        ALU.mult).then_inc(m_att, 1)
                dve.wait_ge(m_att, t + 1)

            attention_row(0)
            attention_row(1)
            for t in range(TILES):
                if t + 2 < TILES:
                    attention_row(t + 2)
                dve.wait_ge(m_wo, t + 1)
                link(dve, nc.vector.tensor_tensor(Hm[0:TP, t, :], bank(5 + t % 2)[0:TP, :], bo_m[0:TP, :], ALU.add))
                nc.vector.tensor_tensor(Hm[0:TP, t, :], Hm[0:TP, t, :], XN[0:TP, t, :], ALU.add).then_inc(m_h, 1)
                if t >= 1:
                    dve.wait_ge(m_h, t)
                    gather_stats(Hm, t - 1)
            dve.wait_ge(m_h, TILES)
            ln_stats_dve(dve, Hm, 1e-6, gathered=True)

            def normed(t):
                h = Hm[0:TP, t, :]
                link(dve, normalize(h, h, t))
                link(dve, nc.vector.tensor_tensor(h, h, ln1_s[0:TP, :], ALU.mult))
                nc.vector.tensor_tensor(h, h, ln1_b[0:TP, :], ALU.add).then_inc(m_h1, 1)

            for t in range(4):
                normed(t)
            for t in range(TILES):
                if t + 4 < TILES:
                    normed(t + 4)
                dve.wait_ge(m_f2, t + 1)
                dve.wait_ge(m_h1, t + 1)
                h = Hm[0:TP, t, :]
                link(dve, nc.vector.tensor_tensor(h, bank(5 + t % 2)[0:TP, :], h, ALU.add))
                nc.vector.tensor_tensor(h, h, b2_m[0:TP, :], ALU.add).then_inc(m_g, 1)
                if t >= 1:
                    dve.wait_ge(m_g, t)
                    gather_stats(Hm, t - 1)
            dve.wait_ge(m_g, TILES)
            ln_stats_dve(dve, Hm, 1e-6, gathered=True)
            dve.wait_ge(m_xb, TILES)
            for step in range(3):
                for t in range(TILES):
                    h = Hm[0:TP, t, :]
                    if step == 0:
                        last = normalize(h, h, t)
                    elif step == 1:
                        last = nc.vector.tensor_tensor(h, h, ln2_s[0:TP, :], ALU.mult)
                    else:
                        last = nc.vector.tensor_tensor(X[0:TP, t, :], X[0:TP, t, :], h, ALU.add)
                link(dve, last)
            leave_stage(dve, "DVE")

        def mix_act(act):
            ln_stats_act(act)
            for t in range(TILES + 1):
                if t < TILES:
                    act.wait_ge(m_tx, t + 1)
                    if t >= 2:
                        act.wait_ge(m_proj, 3 * t - 3)
                    nc.scalar.activation(xT_m[t % 2], chunks(bank(t % 2)[:, :], TP), ACT.Copy).then_inc(m_xT, 1)
                if t >= 1:
                    act.wait_ge(m_tq, t)
                    nc.scalar.activation(qT_m[:, :, tok(t - 1)], chunks(bank(5)[:, :], TP), ACT.Copy).then_inc(m_qT, 1)
            ln_stats_act(act)
            for t in range(TILES):
                act.wait_ge(m_ta, t + 1)
                if t >= 2:
                    act.wait_ge(m_wo, t - 1)
                nc.scalar.activation(xT_m[t % 2], chunks(bank(4)[:, :], TP), ACT.Copy).then_inc(m_aT, 1)
            ln_stats_act(act)

            def hT(t):
                act.wait_ge(m_th, t + 1)
                if t >= 2:
                    act.wait_ge(m_f1, t - 1)
                nc.scalar.activation(xT_m[t % 2], chunks(bank(t % 2)[:, :], TP), ACT.Copy).then_inc(m_hT, 1)

            hT(0)
            hT(1)
            for t in range(TILES):
                act.wait_ge(m_f1, t + 1)
                if t >= 2:
                    act.wait_ge(m_f2, t - 1)
                for m in range(2):
                    last = nc.scalar.activation(f1_m[t % 2][:, m, :], bank(2 + t % 2)[:, m * TP:(m + 1) * TP],
                                                ACT.Relu, bias=b1_m[:, m:m + 1])
                last.then_inc(m_r1, 1)
                if t + 2 < TILES:
                    hT(t + 2)
            ln_stats_act(act)
            leave_stage(act, "ACT")

        def mix_pe(pe):
            pe.wait_ge(s_wm, 16 * 6)

            def after(t):
                pe.wait_ge(m_rows, t + 1)
                if t >= 1:
                    pe.wait_ge(m_qT, t)
                transpose_tile(chunks(bank(5)[:, :], TP), q_m[0:TP, :]).then_inc(m_tq, 1)
                for j in range(PAIRS):
                    kj = k_m[0:TP, j * 128:(j + 1) * 128]
                    first = t == 0 and j == 0
                    end = t == TILES - 1 and j == PAIRS - 1
                    nc.tensor.matmul(bank(6)[:, j * 128:(j + 1) * 128], kj, v_m[0:TP, j * 128:(j + 1) * 128],
                                     start=first, stop=end, skip_group_check=True)
                    last = nc.tensor.matmul(bank(7)[:, 2 * j:2 * j + 2], kj, ones[0:TP, 0:2],
                                            start=first, stop=end, skip_group_check=True)
                last.then_inc(m_kv, 1)

            for t in range(TILES):
                pe.wait_ge(s_xn, t + 1)
                transpose_tile(chunks(bank(t % 2)[:, :], TP), XN[0:TP, t, :]).then_inc(m_tx, 1)
                if t >= 1:
                    after(t - 1)
                pe.wait_ge(m_xT, t + 1)
                for j, w in enumerate((wq_m, wk_m, wv_m)):
                    n = 3 * t + j
                    if n >= 3:
                        pe.wait_ge(m_ev, n - 2)
                    project(bank(2 + n % 3)[0:TP, :], xT_m[t % 2], w).then_inc(m_proj, 1)
            after(TILES - 1)
            pe.wait_ge(m_kvb, 1)
            pe.wait_ge(m_qT, TILES)
            pe.wait_ge(s_wm2, 16 * 10)

            def num_den(t):
                if t >= 2:
                    pe.wait_ge(m_att, t - 1)
                for j in range(PAIRS):
                    nc.tensor.matmul(bank(t % 2)[0:TP, j * 128:(j + 1) * 128], qT_m[:, j, tok(t)], kv_m[:, j, :],
                                     start=True, stop=True)
                for j in range(PAIRS):
                    last = nc.tensor.matmul(bank(2 + t % 2)[0:TP, 0:8], qT_m[:, j, tok(t)],
                                            ks_m[:, 8 * j:8 * j + 8], start=(j == 0), stop=(j == PAIRS - 1))
                last.then_inc(m_nd, 1)

            def turn_row(t):
                pe.wait_ge(m_att, t + 1)
                if t >= 1:
                    pe.wait_ge(m_aT, t)
                transpose_tile(chunks(bank(4)[:, :], TP), row_m[0:TP, :]).then_inc(m_ta, 1)

            num_den(0)
            num_den(1)
            turn_row(0)
            for t in range(TILES):
                if t + 2 < TILES:
                    num_den(t + 2)
                if t + 1 < TILES:
                    turn_row(t + 1)
                pe.wait_ge(m_aT, t + 1)
                if t >= 2:
                    pe.wait_ge(m_h, t - 1)
                project(bank(5 + t % 2)[0:TP, :], xT_m[t % 2], wo_m).then_inc(m_wo, 1)

            def turn_h(t):
                pe.wait_ge(m_h1, t + 1)
                if t >= 2:
                    pe.wait_ge(m_hT, t - 1)
                transpose_tile(chunks(bank(t % 2)[:, :], TP), Hm[0:TP, t, :]).then_inc(m_th, 1)

            def hidden(t):
                pe.wait_ge(m_hT, t + 1)
                if t >= 2:
                    pe.wait_ge(m_r1, t - 1)
                for m in range(2):
                    for k in range(KC):
                        last = nc.tensor.matmul(bank(2 + t % 2)[:, m * TP:(m + 1) * TP],
                                                w1_m[:, k, m * 128:(m + 1) * 128], xT_m[t % 2][:, k, :],
                                                start=(k == 0), stop=(k == KC - 1))
                last.then_inc(m_f1, 1)

            turn_h(0)
            turn_h(1)
            hidden(0)
            for t in range(TILES):
                if t + 2 < TILES:
                    turn_h(t + 2)
                if t + 1 < TILES:
                    hidden(t + 1)
                pe.wait_ge(m_r1, t + 1)
                if t >= 2:
                    pe.wait_ge(m_g, t - 1)
                project(bank(5 + t % 2)[0:TP, :], f1_m[t % 2], w2_m, k=2).then_inc(m_f2, 1)
            leave_stage(pe, "PE")

        wg = Space(BIG, 36864)
        wq_g, wk_g, wv_g = (chunks(wg.take(KC * C), C) for _ in range(3))
        qT_g, kT_g, V_g = cols(slot[0]), cols(slot[1]), rows(slot[2])
        space = Space(BUF, TOP)
        bq_g, bk_g, bv_g, bo_g = (space.take(C) for _ in range(4))
        lg_g = space.take(2 * KC)
        z_g = space.take(C)
        zT_g = [chunks(space.take(C)) for _ in range(2)]
        q_g, k_g = space.take(C), space.take(C)
        s_wg = sem("gnn_qkv_weights_loaded")
        s_bg = sem("gnn_qkv_biases_loaded")
        g_proj = sem("gnn_projected")
        g_ev = sem("gnn_projection_read")
        g_tqk = sem("gnn_qk_transposed")
        g_qkT = sem("gnn_qkT_copied")

        def gnn_w_sp(sp):
            for w, n in ((wq_g, "Wq"), (wk_g, "Wk"), (wv_g, "Wv")):
                sp.dma_start(w.rearrange("p k n -> p (k n)"), d["L0_gnn_" + n]).then_inc(s_wg, 16)

        def gnn_sp(sp):
            sp.wait_ge(s_stage, 6)
            for b, n in ((bq_g, "bq"), (bk_g, "bk"), (bv_g, "bv"), (bo_g, "bo"),
                         (lg_g[:, 0:KC], "ln_att_g"), (lg_g[:, KC:2 * KC], "ln_att_b")):
                load(sp, b, "L0_gnn_" + n, s_bg)
            sp.dma_start(d["x_kept"].rearrange("(t p) c -> p t c", p=TP), X[0:TP, :, :]).then_inc(s_x, 16)

        def gnn_dve(dve):

            def z(t):
                if t >= 1:
                    dve.wait_ge(z_turned, t)
                normalize(z_g[0:TP, :], XN[0:TP, t, :], t, kept_mean, kept_rstd).then_inc(z_rows, 1)

            z(0)
            dve.wait_ge(s_bg, 16 * 6)
            for t in range(TILES):
                if t + 1 < TILES:
                    z(t + 1)
                for j, (row, b) in enumerate(((q_g[0:TP, :], bq_g), (k_g[0:TP, :], bk_g), (V_g[0:TP, t, :], bv_g))):
                    dve.wait_ge(g_proj, 3 * t + j + 1)
                    if t >= 1 and j < 2:
                        dve.wait_ge(g_tqk, t)
                    nc.vector.tensor_tensor(row, bank(2 + j)[0:TP, :], b[0:TP, :], ALU.add).then_inc(g_ev, 1)
            for t in range(TILES):
                nc.vector.tensor_tensor(XN[0:TP, t, :], XN[0:TP, t, :], bo_g[0:TP, :], ALU.add)
            leave_stage(dve, "DVE")

        def gnn_act(act):
            act.wait_ge(s_bg, 16 * 6)
            for t in range(TILES + 1):
                if t < TILES:
                    act.wait_ge(z_turned, t + 1)
                    if t >= 2:
                        act.wait_ge(g_proj, 3 * t - 3)
                    for k in range(KC):
                        last = nc.scalar.activation(zT_g[t % 2][:, k, :], bank(t % 2)[:, k * TP:(k + 1) * TP],
                                                    ACT.Identity, scale=lg_g[:, k:k + 1],
                                                    bias=lg_g[:, KC + k:KC + k + 1])
                    last.then_inc(z_cols, 1)
                if t >= 1:
                    act.wait_ge(g_tqk, t)
                    nc.scalar.activation(qT_g[:, :, tok(t - 1)], chunks(bank(5)[:, :], TP), ACT.Copy,
                                         scale=DH ** -0.5)
                    nc.scalar.activation(kT_g[:, :, tok(t - 1)], chunks(bank(6)[:, :], TP),
                                         ACT.Copy).then_inc(g_qkT, 1)
            leave_stage(act, "ACT")

        def gnn_pe(pe):
            pe.wait_ge(s_wg, 16 * 3)

            def turn(t):
                pe.wait_ge(z_rows, t + 1)
                if t >= 2:
                    pe.wait_ge(z_cols, t - 1)
                transpose_tile(chunks(bank(t % 2)[:, :], TP), z_g[0:TP, :]).then_inc(z_turned, 1)

            def after(t):
                pe.wait_ge(g_ev, 3 * t + 2)
                if t >= 1:
                    pe.wait_ge(g_qkT, t)
                transpose_tile(chunks(bank(5)[:, :], TP), q_g[0:TP, :])
                transpose_tile(chunks(bank(6)[:, :], TP), k_g[0:TP, :]).then_inc(g_tqk, 1)

            turn(0)
            for t in range(TILES):
                pe.wait_ge(z_cols, t + 1)
                for j, w in enumerate((wq_g, wk_g, wv_g)):
                    if t >= 1:
                        pe.wait_ge(g_ev, 3 * t - 2 + j)
                    project(bank(2 + j)[0:TP, :], zT_g[t % 2], w).then_inc(g_proj, 1)
                    if j == 0 and t + 1 < TILES:
                        turn(t + 1)
                after(t)
            leave_stage(pe, "PE")

        HALF = NODES // 2
        space = Space(BUF, TOP)
        ring = [flat.rearrange("p (n w) -> p n w", w=ROW) for flat in
                [arena[:, 5 * SLOT + i * HALF * ROW:5 * SLOT + (i + 1) * HALF * ROW] for i in range(3)]
                + [space.take(HALF * ROW)]]
        over_x = Space(0, SLOT)
        S_g = [over_x.take(NODES) for _ in range(2)]
        absent = over_x.take(NODES)
        pT = over_x.take(NODES)
        pT_v = pT.rearrange("p (b n) -> p b n", b=TILES)
        ADJ_PARTS = 5
        ADJ_N = NODES // ADJ_PARTS
        count_g = space.take(ADJ_N)
        qz = space.take(HEADS * TP).rearrange("p (h n) -> p h n", h=HEADS)
        wo_g = chunks(space.take(KC * C), C)
        row_g = space.take(C)
        aT_g = chunks(space.take(C))
        st_g = over_x.take(80)
        mx3, mx, nmx = st_g[:, 0:3], st_g[:, 4:5], [st_g[:, 6 + i:7 + i] for i in range(2)]
        den2 = [st_g[:, 8 + 16 * i:24 + 16 * i].rearrange("p (h a) -> p h a", a=2) for i in range(2)]
        den, dz = st_g[:, 40:48], st_g[:, 48:56]
        CH = [(0, 512), (512, 1024), (1024, NODES)]
        s_tab = [sem(f"table_block_loaded_{i}") for i in range(2)]
        s_wo_g = sem("gnn_out_weights_loaded")
        s_adj = sem("adjacency_stored")
        a_qz = sem("att_q_padded")
        a_s = sem("att_scores_ready")
        a_m = sem("att_scores_masked")
        a_nm = sem("att_maximum_ready")
        a_e = sem("att_exponentials_ready")
        a_abs = sem("att_absent_ready")
        a_p = sem("att_weights_ready")
        a_tp = sem("att_weights_transposed")
        a_pt = sem("att_weightsT_copied")
        a_pv = sem("att_values_added")
        a_adj = sem("att_adjacency_copied")
        a_row = sem("att_row_ready")
        a_tr = sem("att_row_transposed")
        a_aT = sem("att_rowT_copied")
        a_wo = sem("att_out_projected")
        a_x1 = sem("att_added_to_x")
        STEPS = TILES * HEADS

        def att_sp(sp):
            sp.wait_ge(s_stage, 9)
            sp.dma_start(wo_g.rearrange("p k n -> p (k n)"), d["L0_gnn_Wo"]).then_inc(s_wo_g, 16)
            sp.wait_ge(s_scat, TABLE_DONE)
            table = d["table"][0:CELLS, :].rearrange("(s n) w -> s n w", n=NODES)

            def load_block(t):
                for _, part, c in halves(t):
                    sp.dma_start(part[0:TP, :, :], table[tok(t), c, :]).then_inc(s_tab[t % 2], 16)

            load_block(0)
            load_block(1)
            for t in range(TILES):
                for k in range(ADJ_PARTS):
                    sp.wait_ge(a_adj, ADJ_PARTS * t + k + 1)
                    sp.dma_start(d["adj"][tok(t), k * ADJ_N:(k + 1) * ADJ_N], count_g[0:TP, :]).then_inc(s_adj, 16)
                if t + 2 <= TILES:
                    sp.wait_ge(a_p, HEADS * (t + 1))
                if t + 2 < TILES:
                    load_block(t + 2)
                elif t + 2 == TILES:
                    sp.dma_start(w1_g.rearrange("p k n -> p (k n)"), d["L0_gnn_W1"]).then_inc(s_wf, 16)
                    sp.dma_start(w2_g.rearrange("p k n -> p (k n)"), d["L0_gnn_W2"]).then_inc(s_wf, 16)
            sp.wait_ge(s_adj, 16 * ADJ_PARTS * TILES)

        def block_loaded(eng, t):
            eng.wait_ge(s_tab[t % 2], 32 * (t // 2 + 1))

        def halves(t):
            return [(h, ring[(2 * t + h) % 4], slice(h * HALF, (h + 1) * HALF)) for h in range(2)]

        def att_dve(dve):
            nc.vector.memset(qz, 0.0).then_inc(s_zeroed, 1)
            dve.wait_ge(s_x, 32)

            def mask(s):
                t, h = divmod(s, HEADS)
                if h == 0:
                    block_loaded(dve, t)
                    for _, part, c in halves(t):
                        last = nc.vector.tensor_scalar(absent[0:TP, c], part[0:TP, :, HEADS], 0.0, NEG,
                                                       ALU.is_equal, ALU.mult)
                    last.then_inc(a_abs, 1)
                    dve.wait_ge(a_abs, t + 1)
                if s >= 2:
                    dve.wait_ge(a_tp, s - 1)
                for j, (c0, c1) in enumerate(CH):
                    dve.wait_ge(a_s, 3 * s + j + 1)
                    nc.vector.tensor_tensor_reduce(
                        out=S_g[s % 2][0:TP, c0:c1], in0=bank(j)[0:TP, 0:c1 - c0], in1=absent[0:TP, c0:c1],
                        scale=1.0, scalar=LOWEST, op0=ALU.add, op1=ALU.max,
                        accum_out=mx3[0:TP, j:j + 1]).then_inc(a_m, 1)
                dve.wait_ge(a_m, 3 * s + 3)
                link(dve, nc.vector.tensor_reduce(mx[0:TP, :], mx3[0:TP, :], AX_X, ALU.max))
                nc.vector.tensor_scalar(nmx[s % 2][0:TP, :], mx[0:TP, :], -1.0, None, ALU.mult).then_inc(a_nm, 1)

            def weigh(s):
                t, h = divmod(s, HEADS)
                dve.wait_ge(a_e, s + 1)
                for a, part, c in halves(t):
                    last = nc.vector.tensor_tensor_reduce(
                        out=S_g[s % 2][0:TP, c], in0=S_g[s % 2][0:TP, c], in1=part[0:TP, :, h],
                        scale=1.0, scalar=0.0, op0=ALU.mult, op1=ALU.add, accum_out=den2[t % 2][0:TP, h, a:a + 1])
                last.then_inc(a_p, 1)

            def finish(t):
                dve.wait_ge(a_p, HEADS * (t + 1))
                link(dve, nc.vector.tensor_tensor(den[0:TP, :], den2[t % 2][0:TP, :, 0], den2[t % 2][0:TP, :, 1], ALU.add))
                link(dve, nc.vector.tensor_scalar(dz[0:TP, :], den[0:TP, :], 0.0, None, ALU.is_equal))
                link(dve, nc.vector.tensor_tensor(den[0:TP, :], den[0:TP, :], dz[0:TP, :], ALU.add))
                link(dve, nc.vector.reciprocal(den[0:TP, :], den[0:TP, :]))
                dve.wait_ge(a_pv, HEADS * (t + 1))
                if t >= 1:
                    dve.wait_ge(a_tr, t)
                nc.vector.tensor_tensor(row_g[0:TP, :].rearrange("p (h n) -> p h n", h=HEADS),
                                        bank(6)[0:TP, :].rearrange("p (h n) -> p h n", h=HEADS),
                                        den[0:TP, :].unsqueeze(2).to_broadcast([TP, HEADS, DH]),
                                        ALU.mult).then_inc(a_row, 1)

            def add(t):
                dve.wait_ge(a_wo, t + 1)
                nc.vector.tensor_tensor(XN[0:TP, t, :], bank(7)[0:TP, :], XN[0:TP, t, :], ALU.add).then_inc(a_x1, 1)
                if t >= 1:
                    dve.wait_ge(a_x1, t)
                    gather_stats(XN, t - 1)

            mask(0)
            for s in range(STEPS):
                t, h = divmod(s, HEADS)
                if s + 1 < STEPS:
                    mask(s + 1)
                if h == 1 and t >= 1:
                    finish(t - 1)
                weigh(s)
                if h == 3 and t >= 1:
                    add(t - 1)
            finish(TILES - 1)
            add(TILES - 1)
            dve.wait_ge(a_x1, TILES)
            leave_stage(dve, "DVE")

        def att_act(act):
            act.wait_ge(s_zeroed, 1)
            act.wait_ge(s_x, 32)

            def pad_q(t):
                if t >= 1:
                    act.wait_ge(a_s, 3 * HEADS * t)
                by_pair = qz.rearrange("p (j e) n -> p j e n", e=2)
                for e in range(2):
                    last = nc.scalar.activation(by_pair[64 * e:64 * e + 64, :, e, :],
                                                qT_g[64 * e:64 * e + 64, :, tok(t)], ACT.Copy)
                last.then_inc(a_qz, 1)

            def exps(s):
                act.wait_ge(a_nm, s + 1)
                b = S_g[s % 2][0:TP, :]
                nc.scalar.activation(b, b, ACT.Exp, bias=nmx[s % 2][0:TP, :]).then_inc(a_e, 1)

            pad_q(0)
            exps(0)
            for s in range(STEPS):
                t, h = divmod(s, HEADS)
                if s + 1 < STEPS:
                    exps(s + 1)
                act.wait_ge(a_tp, s + 1)
                if s >= 1:
                    act.wait_ge(a_pv, s)
                nc.scalar.activation(pT_v[0:TP, 0:8, :], banks[0:TP, 3 * BANK:5 * BANK]
                                     .rearrange("p (b n) -> p b n", n=128)[:, :, 0:TP], ACT.Copy)
                nc.scalar.activation(pT_v[0:TP, 8:10, :], bank(5)[0:TP, 0:256]
                                     .rearrange("p (b n) -> p b n", n=128)[:, :, 0:TP], ACT.Copy).then_inc(a_pt, 1)
                if h == 5 and t + 1 < TILES:
                    pad_q(t + 1)
                if h < ADJ_PARTS:
                    n = ADJ_PARTS * t + h
                    if n >= 1:
                        act.wait_ge(s_adj, 16 * n)
                    lo, hi = h * ADJ_N, (h + 1) * ADJ_N
                    for _, part, c in halves(t):
                        a, b = max(lo, c.start), min(hi, c.stop)
                        if a < b:
                            last = nc.scalar.activation(count_g[0:TP, a - lo:b - lo],
                                                        part[0:TP, a - c.start:b - c.start, HEADS], ACT.Copy)
                    last.then_inc(a_adj, 1)
                if h == 1 and t >= 1:
                    act.wait_ge(a_tr, t)
                    nc.scalar.activation(aT_g, chunks(bank(7)[:, :], TP), ACT.Copy).then_inc(a_aT, 1)
            act.wait_ge(a_tr, TILES)
            nc.scalar.activation(aT_g, chunks(bank(7)[:, :], TP), ACT.Copy).then_inc(a_aT, 1)
            leave_stage(act, "ACT")

        def att_pe(pe):
            pe.wait_ge(s_wo_g, 16)

            def scores(s):
                t, h = divmod(s, HEADS)
                if h == 0:
                    pe.wait_ge(a_qz, t + 1)
                for j, (c0, c1) in enumerate(CH):
                    if s >= 1:
                        pe.wait_ge(a_m, 3 * (s - 1) + j + 1)
                    nc.tensor.matmul(bank(j)[0:TP, 0:c1 - c0], qz[:, h, :], kT_g[:, h // 2, c0:c1],
                                     start=True, stop=True).then_inc(a_s, 1)

            def turn(s):
                pe.wait_ge(a_p, s + 1)
                if s >= 1:
                    pe.wait_ge(a_pt, s)
                for b in range(TILES):
                    last = nc.tensor.transpose(banks[0:TP, 3 * BANK + 128 * b:3 * BANK + 128 * b + TP],
                                               S_g[s % 2][0:TP, b * TP:(b + 1) * TP], ident[0:TP, 0:TP])
                last.then_inc(a_tp, 1)

            def values(s):
                t, h = divmod(s, HEADS)
                pe.wait_ge(a_pt, s + 1)
                if h == 0 and t >= 1:
                    pe.wait_ge(a_row, t)
                for b in range(TILES):
                    last = nc.tensor.matmul(bank(6)[0:TP, h * DH:(h + 1) * DH], pT_v[0:TP, b, :],
                                            V_g[0:TP, b, h * DH:(h + 1) * DH],
                                            start=(b == 0), stop=(b == TILES - 1))
                last.then_inc(a_pv, 1)

            def turn_row(t):
                pe.wait_ge(a_row, t + 1)
                if t >= 1:
                    pe.wait_ge(a_x1, t)
                transpose_tile(chunks(bank(7)[:, :], TP), row_g[0:TP, :]).then_inc(a_tr, 1)

            def out(t):
                pe.wait_ge(a_aT, t + 1)
                project(bank(7)[0:TP, :], aT_g, wo_g).then_inc(a_wo, 1)

            scores(0)
            scores(1)
            for s in range(STEPS):
                t, h = divmod(s, HEADS)
                if s + 2 < STEPS:
                    scores(s + 2)
                turn(s)
                if h == 1 and t >= 1:
                    turn_row(t - 1)
                if s >= 1:
                    values(s - 1)
                if h == 2 and t >= 1:
                    out(t - 1)
            values(STEPS - 1)
            turn_row(TILES - 1)
            out(TILES - 1)
            leave_stage(pe, "PE")

        wff = Space(5 * SLOT, 5 * SLOT + 2 * HALF * ROW)
        w1_g, w2_g = chunks(wff.take(KC * HID), HID), chunks(wff.take(HID // 128 * C), C, HID // 128)
        space = Space(BUF, TOP)
        b2_g = space.take(C)
        lf_g = space.take(2 * KC)
        b1_g = space.take(8)
        z_f = space.take(C)
        zT_f = [chunks(space.take(C)) for _ in range(2)]
        hT_f = [chunks(space.take(8 * TP), TP, 8) for _ in range(2)]
        s_wf = sem("gnn_ff_weights_loaded")
        f_h = sem("ff_hidden_ready")
        f_s = sem("ff_silu_ready")
        f_o = sem("ff_out_ready")
        f_x = sem("ff_added")

        def ff_sp(sp):
            sp.wait_ge(s_stage, 12)
            sp.wait_ge(s_x, 32)
            for b, n in ((b2_g, "b2"), (b1_g, "b1"), (lf_g[:, 0:KC], "ln_ff_g"), (lf_g[:, KC:2 * KC], "ln_ff_b")):
                load(sp, b, "L0_gnn_" + n, s_wf)
            sp.dma_start(X[0:TP, :, :], d["x_kept"].rearrange("(t p) c -> p t c", p=TP)).then_inc(s_x, 16)

        def ff_dve(dve):
            ln_stats_dve(dve, XN, 1e-5, gathered=True)
            dve.wait_ge(s_wf, 16 * 6)
            dve.wait_ge(s_x, 48)

            def z(t):
                if t >= 1:
                    dve.wait_ge(z_turned, Z_FF + t)
                normalize(z_f[0:TP, :], XN[0:TP, t, :], t).then_inc(z_rows, 1)

            z(0)
            z(1)
            for t in range(TILES):
                if t + 2 < TILES:
                    z(t + 2)
                link(dve, nc.vector.tensor_tensor(X[0:TP, t, :], X[0:TP, t, :], XN[0:TP, t, :], ALU.add))
                link(dve, nc.vector.tensor_tensor(X[0:TP, t, :], X[0:TP, t, :], b2_g[0:TP, :], ALU.add))
                dve.wait_ge(f_o, t + 1)
                nc.vector.tensor_tensor(X[0:TP, t, :], bank(6 + t % 2)[0:TP, :], X[0:TP, t, :],
                                        ALU.add).then_inc(f_x, 1)
                if t >= 1:
                    dve.wait_ge(f_x, t)
                    gather_stats(X, t - 1)
            dve.wait_ge(f_x, TILES)
            leave_stage(dve, "DVE")

        def ff_act(act):
            ln_stats_act(act)
            act.wait_ge(s_wf, 16 * 6)

            def zT(t):
                act.wait_ge(z_turned, Z_FF + t + 1)
                if t >= 2:
                    act.wait_ge(f_h, 2 * (t - 1))
                for k in range(KC):
                    last = nc.scalar.activation(zT_f[t % 2][:, k, :], bank(t % 2)[:, k * TP:(k + 1) * TP],
                                                ACT.Identity, scale=lf_g[:, k:k + 1],
                                                bias=lf_g[:, KC + k:KC + k + 1])
                last.then_inc(z_cols, 1)

            zT(0)
            zT(1)
            for t in range(TILES):
                if t + 2 < TILES:
                    zT(t + 2)
                if t >= 2:
                    act.wait_ge(f_o, t - 1)
                for a in range(2):
                    n = 2 * t + a
                    act.wait_ge(f_h, n + 1)
                    for m in range(4):
                        last = nc.scalar.activation(hT_f[t % 2][:, 4 * a + m, :],
                                                    bank(2 + n % 4)[:, m * TP:(m + 1) * TP], ACT.Silu,
                                                    bias=b1_g[:, 4 * a + m:4 * a + m + 1])
                    last.then_inc(f_s, 1)
            leave_stage(act, "ACT")

        def ff_pe(pe):
            pe.wait_ge(s_wf, 16 * 6)

            def turn(t):
                pe.wait_ge(z_rows, Z_FF + t + 1)
                if t >= 2:
                    pe.wait_ge(z_cols, Z_FF + t - 1)
                transpose_tile(chunks(bank(t % 2)[:, :], TP), z_f[0:TP, :]).then_inc(z_turned, 1)

            def hidden(t):
                pe.wait_ge(z_cols, Z_FF + t + 1)
                for a in range(2):
                    n = 2 * t + a
                    if n >= 4:
                        pe.wait_ge(f_s, n - 3)
                    for m in range(4):
                        for k in range(KC):
                            last = nc.tensor.matmul(bank(2 + n % 4)[:, m * TP:(m + 1) * TP],
                                                    w1_g[:, k, (4 * a + m) * 128:(4 * a + m + 1) * 128],
                                                    zT_f[t % 2][:, k, :], start=(k == 0), stop=(k == KC - 1))
                    last.then_inc(f_h, 1)

            turn(0)
            turn(1)
            hidden(0)
            for t in range(TILES):
                if t + 2 < TILES:
                    turn(t + 2)
                if t + 1 < TILES:
                    hidden(t + 1)
                pe.wait_ge(f_s, 2 * t + 2)
                if t >= 2:
                    pe.wait_ge(f_x, t - 1)
                project(bank(6 + t % 2)[0:TP, :], hT_f[t % 2], w2_g, k=8).then_inc(f_o, 1)
            leave_stage(pe, "PE")

        wf = Space(5 * SLOT + 2 * KC * HID, SMALL)
        wq_f, wk_f, wv_f, wo_f = (chunks(wf.take(KC * C), C) for _ in range(4))
        qT_f, kT_f, V_f = cols(slot[0]), cols(slot[1]), rows(slot[2])
        Q_f, K_f = XN, rows(slot[3])
        space = Space(BUF, TOP)
        lg_f = wf.take(2 * KC)
        gain = wf.take(4)
        z_c = space.take(C)
        zT_c = [chunks(space.take(C)) for _ in range(2)]
        sq_c = [space.take(C) for _ in range(2)]
        ss, sr, sa, sv = (space.take(2 * TILES * HEADS) for _ in range(4))
        s_wc = sem("ffn_qkv_weights_loaded")
        c_proj = sem("ffn_projected")
        c_ev = sem("ffn_projection_read")
        c_sq = sem("ffn_squares_ready")
        c_ss = sem("ffn_squares_summed")
        c_sr = sem("ffn_norms_ready")
        c_n = sem("ffn_rows_normalized")
        c_tqk = sem("ffn_qk_transposed")
        c_qkT = sem("ffn_qkT_copied")

        def ffn_sp(sp):
            for w, n in ((wq_f, "Wq"), (wk_f, "Wk"), (wv_f, "Wv"), (wo_f, "Wo")):
                sp.dma_start(w.rearrange("p k n -> p (k n)"), d["L0_ffn_" + n]).then_inc(s_wc, 16)
            for b, n in ((lg_f[:, 0:KC], "ln_g"), (lg_f[:, KC:2 * KC], "ln_b"), (gain[:, 0:1], "qn_g"),
                         (gain[:, 1:2], "kn_g")):
                load(sp, b, "L0_ffn_" + n, s_wc)

        def ffn_dve(dve):
            ln_stats_dve(dve, X, 1e-5, gathered=True)
            for t in range(TILES):
                last = normalize(XN[0:TP, t, :], X[0:TP, t, :], t)
            link(dve, last)
            ln_stats_dve(dve, XN, 1e-5)
            dve.wait_ge(s_wc, 16 * 8)
            nc.vector.tensor_scalar(gain[:, 2:3], gain[:, 1:2], float(DH) ** 0.5, None, ALU.mult)

            def z(t):
                if t >= 1:
                    dve.wait_ge(z_turned, Z_FFN + t)
                normalize(z_c[0:TP, :], XN[0:TP, t, :], t).then_inc(z_rows, 1)

            z(0)
            for t in range(TILES):
                if t + 1 < TILES:
                    z(t + 1)
                for j, row in enumerate((Q_f[0:TP, t, :], K_f[0:TP, t, :], V_f[0:TP, t, :])):
                    dve.wait_ge(c_proj, 3 * t + j + 1)
                    nc.vector.tensor_copy(row, bank(2 + j)[0:TP, :]).then_inc(c_ev, 1)
            for n in range(2 * TILES):
                dve.wait_ge(c_sq, n + 1)
                nc.vector.tensor_reduce(ss[0:TP, n * HEADS:(n + 1) * HEADS],
                                        sq_c[n % 2][0:TP, :].rearrange("p (h n) -> p h n", h=HEADS),
                                        AX_X, ALU.add).then_inc(c_ss, 1)
            dve.wait_ge(c_ss, 2 * TILES)
            nc.vector.tensor_scalar(sv[0:TP, :], ss[0:TP, :], 1e-12, None, ALU.add).then_inc(c_ss, 1)
            dve.wait_ge(c_ss, 2 * TILES + 1)
            dve.wait_ge(c_sr, 1)
            link(dve, nc.vector.reciprocal(sr[0:TP, :], sa[0:TP, :]))
            link(dve, nc.vector.tensor_tensor(ss[0:TP, :], sv[0:TP, :], sr[0:TP, :], ALU.mult))
            link(dve, nc.vector.tensor_tensor(ss[0:TP, :], ss[0:TP, :], sr[0:TP, :], ALU.mult))
            link(dve, nc.vector.tensor_scalar(ss[0:TP, :], ss[0:TP, :], -0.5, 1.5, ALU.mult, ALU.add))
            link(dve, nc.vector.tensor_tensor(sr[0:TP, :], sr[0:TP, :], ss[0:TP, :], ALU.mult))
            for n in range(2 * TILES):
                t, which = divmod(n, 2)
                row = (Q_f, K_f)[which][0:TP, t, :].rearrange("p (h n) -> p h n", h=HEADS)
                nc.vector.tensor_tensor(row, row, sr[0:TP, n * HEADS:(n + 1) * HEADS].unsqueeze(2)
                                        .to_broadcast([TP, HEADS, DH]), ALU.mult).then_inc(c_n, 1)
            leave_stage(dve, "DVE")

        def ffn_act(act):
            ln_stats_act(act)
            ln_stats_act(act)
            act.wait_ge(s_wc, 16 * 8)
            for t in range(TILES):
                act.wait_ge(z_turned, Z_FFN + t + 1)
                if t >= 2:
                    act.wait_ge(c_proj, 3 * t - 3)
                for k in range(KC):
                    last = nc.scalar.activation(zT_c[t % 2][:, k, :], bank(t % 2)[:, k * TP:(k + 1) * TP],
                                                ACT.Identity, scale=lg_f[:, k:k + 1],
                                                bias=lg_f[:, KC + k:KC + k + 1])
                last.then_inc(z_cols, 1)
            for n in range(2 * TILES):
                t, which = divmod(n, 2)
                act.wait_ge(c_ev, 3 * t + 1 + which)
                if n >= 2:
                    act.wait_ge(c_ss, n - 1)
                nc.scalar.activation(sq_c[n % 2][0:TP, :], (Q_f, K_f)[which][0:TP, t, :],
                                     ACT.Square).then_inc(c_sq, 1)
            act.wait_ge(c_ss, 2 * TILES + 1)
            nc.scalar.activation(sa[0:TP, :], sv[0:TP, :], ACT.Sqrt).then_inc(c_sr, 1)
            for n in range(2 * TILES):
                t, which = divmod(n, 2)
                act.wait_ge(c_tqk, n + 1)
                nc.scalar.activation((qT_f, kT_f)[which][:, :, tok(t)], chunks(bank(n % 4)[:, :], TP), ACT.Copy,
                                     scale=gain[:, 2 * which:2 * which + 1]).then_inc(c_qkT, 1)
            leave_stage(act, "ACT")

        def ffn_pe(pe):
            pe.wait_ge(s_wc, 16 * 8)

            def turn(t):
                pe.wait_ge(z_rows, Z_FFN + t + 1)
                if t >= 2:
                    pe.wait_ge(z_cols, Z_FFN + t - 1)
                transpose_tile(chunks(bank(t % 2)[:, :], TP), z_c[0:TP, :]).then_inc(z_turned, 1)

            turn(0)
            for t in range(TILES):
                pe.wait_ge(z_cols, Z_FFN + t + 1)
                for j, w in enumerate((wq_f, wk_f, wv_f)):
                    if t >= 1:
                        pe.wait_ge(c_ev, 3 * t - 2 + j)
                    project(bank(2 + j)[0:TP, :], zT_c[t % 2], w).then_inc(c_proj, 1)
                    if j == 0 and t + 1 < TILES:
                        turn(t + 1)
            pe.wait_ge(c_ev, 3 * TILES)
            for n in range(2 * TILES):
                t, which = divmod(n, 2)
                pe.wait_ge(c_n, n + 1)
                if n >= 4:
                    pe.wait_ge(c_qkT, n - 3)
                transpose_tile(chunks(bank(n % 4)[:, :], TP), (Q_f, K_f)[which][0:TP, t, :]).then_inc(c_tqk, 1)
            leave_stage(pe, "PE")

        yT = cols(arena[:, BIG:BIG + KC * NODES])
        space = Space(BUF, TOP)
        S_c = [space.take(NODES) for _ in range(2)]
        future = space.take(NODES)
        pT_c = space.take(NODES)
        pTc_v = pT_c.rearrange("p (b n) -> p b n", b=TILES)
        qz_c = space.take(HEADS * TP).rearrange("p (h n) -> p h n", h=HEADS)
        row_c = space.take(C)
        aT_c = chunks(space.take(C))
        st_c = space.take(64)
        mx3_c, mx_c, nmx_c = st_c[:, 0:3], st_c[:, 4:5], [st_c[:, 6 + i:7 + i] for i in range(2)]
        den_c = [st_c[:, 8 + 8 * i:16 + 8 * i] for i in range(2)]
        rden_c = st_c[:, 24:32]
        b_qz = sem("causal_q_padded")
        b_s = sem("causal_scores_ready")
        b_m = sem("causal_scores_masked")
        b_nm = sem("causal_maximum_ready")
        b_e = sem("causal_exponentials_ready")
        b_tp = sem("causal_weights_transposed")
        b_pt = sem("causal_weightsT_copied")
        b_pv = sem("causal_values_added")
        b_row = sem("causal_row_ready")
        b_tr = sem("causal_row_transposed")
        b_aT = sem("causal_rowT_copied")
        b_y = sem("causal_out_projected")
        b_yT = sem("causal_yT_copied")
        parts = [[(c, min(c + BANK, (s // HEADS + 1) * TP)) for c in range(0, (s // HEADS + 1) * TP, BANK)]
                 for s in range(STEPS)]
        before = [sum(len(p) for p in parts[:s]) for s in range(STEPS + 1)]

        def score_bank(s, j):
            return (before[s] + j) % 3

        def causal_pool(pool):
            pool.wait_ge(s_stage, 18)
            nc.gpsimd.memset(future, 0.0).then_inc(s_const, 1)
            pool.wait_ge(s_const, 2)
            own = future[0:TP, NODES - TP:NODES]
            nc.gpsimd.affine_select(out=own, in_=own, compare_op=ALU.is_ge, fill=NEG, base=0,
                                    pattern=[[-1, TP]], channel_multiplier=1).then_inc(s_const, 1)

        def causal_dve(dve):
            nc.vector.memset(qz_c, 0.0).then_inc(s_zeroed, 1)
            dve.wait_ge(s_const, 3)

            def mask(s):
                t, h = divmod(s, HEADS)
                width = (t + 1) * TP
                if s >= 2:
                    dve.wait_ge(b_tp, s - 1)
                for j, (c0, c1) in enumerate(parts[s]):
                    dve.wait_ge(b_s, before[s] + j + 1)
                    nc.vector.tensor_tensor_reduce(
                        out=S_c[s % 2][0:TP, c0:c1], in0=bank(score_bank(s, j))[0:TP, 0:c1 - c0],
                        in1=future[0:TP, NODES - width + c0:NODES - width + c1], scale=1.0, scalar=LOWEST,
                        op0=ALU.add, op1=ALU.max, accum_out=mx3_c[0:TP, j:j + 1]).then_inc(b_m, 1)
                dve.wait_ge(b_m, before[s + 1])
                link(dve, nc.vector.tensor_reduce(mx_c[0:TP, :], mx3_c[0:TP, 0:len(parts[s])], AX_X, ALU.max))
                nc.vector.tensor_scalar(nmx_c[s % 2][0:TP, :], mx_c[0:TP, :], -1.0, None, ALU.mult).then_inc(b_nm, 1)

            def finish(t):
                dve.wait_ge(b_e, HEADS * (t + 1))
                link(dve, nc.vector.reciprocal(rden_c[0:TP, :], den_c[t % 2][0:TP, :]))
                dve.wait_ge(b_pv, HEADS * (t + 1))
                if t >= 1:
                    dve.wait_ge(b_tr, t)
                nc.vector.tensor_tensor(row_c[0:TP, :].rearrange("p (h n) -> p h n", h=HEADS),
                                        bank(6)[0:TP, :].rearrange("p (h n) -> p h n", h=HEADS),
                                        rden_c[0:TP, :].unsqueeze(2).to_broadcast([TP, HEADS, DH]),
                                        ALU.mult).then_inc(b_row, 1)

            mask(0)
            for s in range(STEPS):
                t, h = divmod(s, HEADS)
                if s + 1 < STEPS:
                    mask(s + 1)
                if h == 1 and t >= 1:
                    finish(t - 1)
            finish(TILES - 1)
            leave_stage(dve, "DVE")

        def causal_act(act):
            act.wait_ge(s_zeroed, 2)

            def pad_q(t):
                if t >= 1:
                    act.wait_ge(b_s, before[HEADS * t])
                by_pair = qz_c.rearrange("p (j e) n -> p j e n", e=2)
                for e in range(2):
                    last = nc.scalar.activation(by_pair[64 * e:64 * e + 64, :, e, :],
                                                qT_f[64 * e:64 * e + 64, :, tok(t)], ACT.Copy)
                last.then_inc(b_qz, 1)

            def exps(s):
                t, h = divmod(s, HEADS)
                act.wait_ge(b_nm, s + 1)
                if h == 0 and t >= 2:
                    act.wait_ge(b_row, t - 1)
                b = S_c[s % 2][0:TP, 0:(t + 1) * TP]
                nc.scalar.activation(b, b, ACT.Exp, bias=nmx_c[s % 2][0:TP, :],
                                     accum_out=den_c[t % 2][0:TP, h:h + 1]).then_inc(b_e, 1)

            def row_T(t):
                act.wait_ge(b_tr, t + 1)
                nc.scalar.activation(aT_c, chunks(bank(7)[:, :], TP), ACT.Copy).then_inc(b_aT, 1)
                act.wait_ge(b_y, t + 1)
                nc.scalar.activation(yT[:, :, tok(t)], chunks(bank(7)[:, :], TP), ACT.Copy).then_inc(b_yT, 1)

            pad_q(0)
            exps(0)
            for s in range(STEPS):
                t, h = divmod(s, HEADS)
                if s + 1 < STEPS:
                    exps(s + 1)
                act.wait_ge(b_tp, s + 1)
                if s >= 1:
                    act.wait_ge(b_pv, s)
                for b0 in range(0, t + 1, 4):
                    n = min(4, t + 1 - b0)
                    last = nc.scalar.activation(
                        pTc_v[0:TP, b0:b0 + n, :], bank(3 + b0 // 4)[0:TP, 0:128 * n]
                        .rearrange("p (b n) -> p b n", n=128)[:, :, 0:TP], ACT.Copy)
                last.then_inc(b_pt, 1)
                if h == 5 and t + 1 < TILES:
                    pad_q(t + 1)
                if h == 2 and t >= 1:
                    row_T(t - 1)
            row_T(TILES - 1)
            leave_stage(act, "ACT")

        def causal_pe(pe):
            def scores(s):
                t, h = divmod(s, HEADS)
                if h == 0:
                    pe.wait_ge(b_qz, t + 1)
                for j, (c0, c1) in enumerate(parts[s]):
                    if before[s] + j >= 3:
                        pe.wait_ge(b_m, before[s] + j - 2)
                    nc.tensor.matmul(bank(score_bank(s, j))[0:TP, 0:c1 - c0], qz_c[:, h, :],
                                     kT_f[:, h // 2, c0:c1], start=True, stop=True).then_inc(b_s, 1)

            def turn(s):
                t = s // HEADS
                pe.wait_ge(b_e, s + 1)
                if s >= 1:
                    pe.wait_ge(b_pt, s)
                for b in range(t + 1):
                    last = nc.tensor.transpose(banks[0:TP, 3 * BANK + 128 * b:3 * BANK + 128 * b + TP],
                                               S_c[s % 2][0:TP, b * TP:(b + 1) * TP], ident[0:TP, 0:TP])
                last.then_inc(b_tp, 1)

            def values(s):
                t, h = divmod(s, HEADS)
                pe.wait_ge(b_pt, s + 1)
                if h == 0 and t >= 1:
                    pe.wait_ge(b_row, t)
                for b in range(t + 1):
                    last = nc.tensor.matmul(bank(6)[0:TP, h * DH:(h + 1) * DH], pTc_v[0:TP, b, :],
                                            V_f[0:TP, b, h * DH:(h + 1) * DH], start=(b == 0), stop=(b == t))
                last.then_inc(b_pv, 1)

            def turn_row(t):
                pe.wait_ge(b_row, t + 1)
                if t >= 1:
                    pe.wait_ge(b_yT, t)
                transpose_tile(chunks(bank(7)[:, :], TP), row_c[0:TP, :]).then_inc(b_tr, 1)

            def out(t):
                pe.wait_ge(b_aT, t + 1)
                for m in range(KC):
                    for k in range(KC):
                        last = nc.tensor.matmul(bank(7)[:, m * TP:(m + 1) * TP], wo_f[:, k, m * 128:(m + 1) * 128],
                                                aT_c[:, k, :], start=(k == 0), stop=(k == KC - 1))
                last.then_inc(b_y, 1)

            scores(0)
            scores(1)
            for s in range(STEPS):
                t, h = divmod(s, HEADS)
                if s + 2 < STEPS:
                    scores(s + 2)
                turn(s)
                if h == 1 and t >= 1:
                    turn_row(t - 1)
                if s >= 1:
                    values(s - 1)
                if h == 2 and t >= 1:
                    out(t - 1)
            values(STEPS - 1)
            turn_row(TILES - 1)
            out(TILES - 1)
            leave_stage(pe, "PE")

        NH = EXPERTS * FF // 128
        w1_e = [arena[:, at:at + KC * 4 * FF].rearrange("p (k n) -> p k n", k=KC) for at in (BIG + KC * NODES, 2 * SLOT)]
        w2_e = [arena[:, at:at + NH // 2 * C].rearrange("p (k n) -> p k n", k=NH // 2) for at in (SLOT, 5 * SLOT)]
        space = Space(BUF, TOP)
        gw_e = chunks(space.take(KC * EXPERTS), EXPERTS)
        gb_e = space.take(EXPERTS)
        b1_e = space.take(NH)
        b2_e = space.take(C)
        gate = space.take(TILES * EXPERTS)
        gsum = space.take(2 * TILES)
        gateT = space.take(TILES * 128)
        hT_e = [chunks(space.take(NH * TP), TP, NH) for _ in range(2)]
        s_we = sem("expert_weights_loaded")
        s_we2 = sem("expert_second_half_loaded")
        e_gl = sem("gate_logits_ready")
        e_gs = sem("gate_logits_shifted")
        e_ge = sem("gate_exponentials_ready")
        e_g = sem("gates_ready")
        e_gt = sem("gates_transposed")
        e_gT = sem("gatesT_copied")
        e_h = sem("expert_hidden_ready")
        e_a = sem("expert_gelu_ready")
        e_b = sem("expert_biases_ready")
        e_o = sem("expert_out_ready")
        e_x = sem("expert_added")

        w1_all = d["L0_ffn_W1"].rearrange("p (k n) -> p k n", k=KC)
        w2_all = d["L0_ffn_W2"].rearrange("p (k n) -> p k n", k=NH)

        def expert_sp(sp):
            sp.wait_ge(s_stage, 18)
            sp.dma_start(w1_e[0], w1_all[:, :, 0:4 * FF]).then_inc(s_we, 16)
            for i in range(2):
                sp.dma_start(w2_e[i], w2_all[:, NH // 2 * i:NH // 2 * (i + 1), :]).then_inc(s_we, 16)
            sp.wait_ge(s_stage, 21)
            load(sp, gw_e.rearrange("p k n -> p (k n)"), "L0_ffn_gate_W", s_we)
            for b, n in ((gb_e, "gate_b"), (b1_e, "b1")):
                load(sp, b, "L0_ffn_" + n, s_we)
            sp.dma_start(b2_e[0:EXPERTS, :], d["L0_ffn_b2"]).then_inc(s_we, 16)
            sp.dma_start(w1_e[1], w1_all[:, :, 4 * FF:8 * FF]).then_inc(s_we2, 16)

        def expert_dve(dve):
            g = gate[0:TP, :].rearrange("p (t e) -> p t e", e=EXPERTS)
            dve.wait_ge(s_we, 16 * 7)
            dve.wait_ge(e_gl, 1)
            link(dve, nc.vector.tensor_tensor(
                g, bank(0)[0:TP, 0:TILES * EXPERTS].rearrange("p (t e) -> p t e", e=EXPERTS),
                gb_e[0:TP, :].unsqueeze(1).to_broadcast([TP, TILES, EXPERTS]), ALU.add))
            link(dve, nc.vector.tensor_reduce(gsum[0:TP, 0:TILES], g, AX_X, ALU.max))
            nc.vector.tensor_tensor(g, g, gsum[0:TP, 0:TILES].unsqueeze(2).to_broadcast([TP, TILES, EXPERTS]),
                                    ALU.subtract).then_inc(e_gs, 1)
            dve.wait_ge(e_ge, 1)
            link(dve, nc.vector.tensor_reduce(gsum[0:TP, TILES:2 * TILES], g, AX_X, ALU.add))
            link(dve, nc.vector.reciprocal(gsum[0:TP, 0:TILES], gsum[0:TP, TILES:2 * TILES]))
            nc.vector.tensor_tensor(g, g, gsum[0:TP, 0:TILES].unsqueeze(2).to_broadcast([TP, TILES, EXPERTS]),
                                    ALU.mult).then_inc(e_g, 1)
            dve.wait_ge(e_g, 1)
            for t in range(TILES):
                x = X[0:TP, t, :]
                dve.wait_ge(e_b, t + 1)
                nc.vector.tensor_tensor(x, bank(1)[0:TP, :], x, ALU.add).then_inc(e_x, 1)
                for e in range(EXPERTS):
                    n = (EXPERTS + 1) * t + e + 1
                    dve.wait_ge(e_x, n)
                    dve.wait_ge(e_o, EXPERTS * t + e + 1)
                    nc.vector.scalar_tensor_tensor(
                        out=x, in0=bank(5 + (EXPERTS * t + e) % 3)[0:TP, :],
                        scalar=gate[0:TP, EXPERTS * t + e:EXPERTS * t + e + 1], in1=x,
                        op0=ALU.mult, op1=ALU.add).then_inc(e_x, 1)
                    if e == 0 and t >= 1:
                        dve.wait_ge(e_x, (EXPERTS + 1) * t)
                        gather_stats(X, t - 1)
            dve.wait_ge(e_x, (EXPERTS + 1) * TILES)
            leave_stage(dve, "DVE")

        def expert_act(act):
            act.wait_ge(s_we, 16 * 7)
            act.wait_ge(e_gs, 1)
            nc.scalar.activation(gate[0:TP, :], gate[0:TP, :], ACT.Exp).then_inc(e_ge, 1)
            act.wait_ge(e_gt, 1)
            for b in range(3):
                n = min(4, TILES - 4 * b) * 128
                last = nc.scalar.activation(
                    gateT[0:EXPERTS, 512 * b:512 * b + n].rearrange("p (b n) -> p b n", n=128)[:, :, 0:TP],
                    bank(5 + b)[0:EXPERTS, 0:n].rearrange("p (b n) -> p b n", n=128)[:, :, 0:TP], ACT.Copy)
            last.then_inc(e_gT, 1)
            for t in range(TILES):
                if t >= 2:
                    act.wait_ge(e_o, EXPERTS * (t - 1))
                for a in range(NH // 4):
                    n = NH // 4 * t + a
                    act.wait_ge(e_h, n + 1)
                    for m in range(4):
                        c = 4 * a + m
                        last = nc.scalar.activation(hT_e[t % 2][:, c, :], bank(2 + n % 3)[:, m * TP:(m + 1) * TP],
                                                    ACT.Gelu_apprx_tanh, bias=b1_e[:, c:c + 1])
                    last.then_inc(e_a, 1)
            leave_stage(act, "ACT")

        def expert_pe(pe):
            pe.wait_ge(s_we, 16 * 7)
            for t in range(TILES):
                for k in range(KC):
                    last = nc.tensor.matmul(bank(0)[0:TP, EXPERTS * t:EXPERTS * (t + 1)], yT[:, k, tok(t)],
                                            gw_e[:, k, :], start=(k == 0), stop=(k == KC - 1))
            last.then_inc(e_gl, 1)

            def hidden(t):
                for a in range(NH // 4):
                    n = NH // 4 * t + a
                    if n >= 3:
                        pe.wait_ge(e_a, n - 2)
                    if n == 2:
                        pe.wait_ge(s_we2, 16)
                    for m in range(4):
                        c = 4 * a + m
                        for k in range(KC):
                            last = nc.tensor.matmul(bank(2 + n % 3)[:, m * TP:(m + 1) * TP],
                                                    w1_e[a // 2][:, k, (c % 8) * 128:(c % 8 + 1) * 128], yT[:, k, tok(t)],
                                                    start=(k == 0), stop=(k == KC - 1))
                    last.then_inc(e_h, 1)

            pe.wait_ge(e_g, 1)
            for t in range(TILES):
                last = nc.tensor.transpose(banks[0:EXPERTS, 5 * BANK + 128 * t:5 * BANK + 128 * t + TP],
                                           gate[0:TP, EXPERTS * t:EXPERTS * (t + 1)], ident[0:TP, 0:TP])
            last.then_inc(e_gt, 1)
            hidden(0)
            pe.wait_ge(e_gT, 1)
            for t in range(TILES):
                if t >= 1:
                    pe.wait_ge(e_x, (EXPERTS + 1) * (t - 1) + 1)
                nc.tensor.matmul(bank(1)[0:TP, :], gateT[0:EXPERTS, 128 * t:128 * t + TP], b2_e[0:EXPERTS, :],
                                 start=True, stop=True).then_inc(e_b, 1)
                if t + 1 < TILES:
                    hidden(t + 1)
                for e in range(EXPERTS):
                    n = EXPERTS * t + e
                    pe.wait_ge(e_a, NH // 4 * t + e // 2 + 1)
                    if n >= 3:
                        u, f = divmod(n - 3, EXPERTS)
                        pe.wait_ge(e_x, (EXPERTS + 1) * u + f + 2)
                    for c in range(2):
                        last = nc.tensor.matmul(bank(5 + n % 3)[0:TP, :], hT_e[t % 2][:, 2 * e + c, :],
                                                w2_e[e // 4][:, 2 * (e % 4) + c, :], start=(c == 0), stop=(c == 1))
                    last.then_inc(e_o, 1)
            leave_stage(pe, "PE")

        L1_STAGE = 24
        W1AT = 3 * SLOT
        wgcn = chunks(arena[:, W1AT:W1AT + KC * C], C)
        wqkv = arena[:, W1AT + KC * C:W1AT + 4 * KC * C].rearrange("p (k n) -> p k n", k=KC)
        wdense = chunks(arena[:, W1AT + 4 * KC * C:W1AT + 5 * KC * C], C)
        H_n, Q_n = rows(slot[0]), rows(slot[3])
        K_n, V_n = (rows(arena[:, BIG + i * SLOT:BIG + (i + 1) * SLOT]) for i in range(2))
        adj = [arena[0:TP, SLOT + b * NODES:SLOT + (b + 1) * NODES] for b in range(4)] \
            + [arena[0:TP, W1AT + b * NODES:W1AT + (b + 1) * NODES] for b in range(TILES - 4)]
        wT_n = Space(BIG + 2 * SLOT, SMALL).take(NODES)
        wT_v = wT_n.rearrange("p (b n) -> p b n", b=TILES)
        space = Space(BUF, TOP)
        wproj = chunks(space.take(KC * C), C)
        bgcn, bdense, bproj, wq_bc, wk_bc = (space.take(C) for _ in range(5))
        zT_n = [chunks(space.take(C)) for _ in range(2)]
        prod = [space.take(C) for _ in range(2)]
        gspread = space.take(C)
        logit = space.take(TILES * HEADS)
        wtok = space.take(TILES * HEADS)
        st_n = space.take(8)
        gmask = space.take(C)
        s_wn = sem("l1_qkv_weights_loaded")
        s_wn2 = sem("l1_out_weights_loaded")
        s_an = sem("adjacency_loaded")
        n_tz = sem("l1_z_transposed")
        n_zT = sem("l1_zT_copied")
        n_proj = sem("l1_projected")
        n_ev = sem("l1_projection_read")
        o_pe = sem("global_step_of_pe")
        o_act = sem("global_step_of_act")
        o_dve = sem("global_step_of_dve")
        n_deg = sem("degrees_ready")
        n_hs = sem("h_scaled")
        n_agg = sem("neighbours_added")
        n_row = sem("l1_row_ready")
        n_tr = sem("l1_row_transposed")
        n_rT = sem("l1_rowT_copied")
        n_out = sem("l1_out_projected")
        n_x = sem("l1_out_added")

        def l1_sp(sp):
            sp.dma_start(wgcn.rearrange("p k n -> p (k n)"), d["L1_gnn_W_gcn"]).then_inc(s_wn, 16)
            sp.dma_start(wqkv.rearrange("p k n -> p (k n)"), d["L1_mix_w_qkv"]).then_inc(s_wn, 16)
            sp.dma_start(wdense.rearrange("p k n -> p (k n)"), d["L1_gnn_W_dense"]).then_inc(s_wn2, 16)
            sp.wait_ge(s_stage, L1_STAGE)
            for b, n in ((bdense, "gnn_b_dense"), (bproj, "mix_b_proj"), (wq_bc, "mix_w_q"), (bgcn, "gnn_b_gcn"),
                         (wk_bc, "mix_w_k")):
                load(sp, b, "L1_" + n, s_wn)
            sp.dma_start(wproj.rearrange("p k n -> p (k n)"), d["L1_mix_w_proj"]).then_inc(s_wn2, 16)
            sp.wait_ge(n_proj, 4 * TILES)
            for b in range(TILES):
                sp.dma_start(adj[b], d["adj"][tok(b), :]).then_inc(s_an, 16)

        def l1_dve(dve):
            ln_stats_dve(dve, X, 1e-5, gathered=True)
            for t in range(TILES):
                normalize(XN[0:TP, t, :], X[0:TP, t, :], t).then_inc(s_xn, 1)
            dve.wait_ge(s_wn, 16 * 7)
            link(dve, nc.vector.tensor_tensor(bproj[0:TP, :], bproj[0:TP, :], bdense[0:TP, :], ALU.add))

            def head_sums(t, row, by, dst):
                link(dve, nc.vector.tensor_tensor(prod[t % 2][0:TP, :], row, by[0:TP, :], ALU.mult))
                return nc.vector.tensor_reduce(dst[0:TP, t * HEADS:(t + 1) * HEADS],
                                               prod[t % 2][0:TP, :].rearrange("p (h n) -> p h n", h=HEADS),
                                               AX_X, ALU.add)

            for t in range(TILES):
                for j, m in enumerate((H_n, Q_n, K_n, V_n)):
                    dve.wait_ge(n_proj, 4 * t + j + 1)
                    nc.vector.tensor_copy(m[0:TP, t, :], bank(2 + j)[0:TP, :]).then_inc(n_ev, 1)
                dve.wait_ge(n_ev, 4 * t + 2)
                link(dve, head_sums(t, Q_n[0:TP, t, :], wq_bc, logit))
                link(dve, nc.vector.tensor_tensor(X[0:TP, t, :], X[0:TP, t, :], Q_n[0:TP, t, :], ALU.add))
                link(dve, nc.vector.tensor_tensor(X[0:TP, t, :], X[0:TP, t, :], bproj[0:TP, :], ALU.add))
            dve.wait_ge(n_ev, 4 * TILES)
            for r in range(2):
                if r == 1:
                    dve.wait_ge(o_pe, 4)
                    link(dve, nc.vector.tensor_tensor(gspread[0:TP, :], bank(5)[0:TP, :], wk_bc[0:TP, :], ALU.mult))
                    for t in range(TILES):
                        link(dve, head_sums(t, K_n[0:TP, t, :], gspread, logit))
                nc.vector.memset(st_n[0:8, 2:3], 0.0).then_inc(o_dve, 1)
                dve.wait_ge(o_act, 3 * r + 1)
                link(dve, nc.vector.tensor_reduce(st_n[0:8, 0:1], wT_n[0:8, :], AX_X, ALU.max))
                nc.vector.tensor_scalar(st_n[0:8, 1:2], st_n[0:8, 0:1], -(DH ** -0.5), None,
                                        ALU.mult).then_inc(o_dve, 1)
                dve.wait_ge(o_act, 3 * r + 2)
                link(dve, nc.vector.reciprocal(st_n[0:8, 3:4], st_n[0:8, 2:3]))
                nc.vector.tensor_scalar(wT_n[0:8, :], wT_n[0:8, :], st_n[0:8, 3:4], None,
                                        ALU.mult).then_inc(o_dve, 1)
                dve.wait_ge(o_pe, 4 * r + 3)
                nc.vector.tensor_tensor(gmask[0:8, :].rearrange("p (h n) -> p h n", h=HEADS),
                                        bank(4)[0:8, :].rearrange("p (h n) -> p h n", h=HEADS),
                                        ident[0:8, 0:8].unsqueeze(2).to_broadcast([8, HEADS, DH]),
                                        ALU.mult).then_inc(o_dve, 1)
            dve.wait_ge(o_pe, 8)
            link(dve, nc.vector.tensor_copy(gspread[0:TP, :], bank(5)[0:TP, :]))
            nc.vector.tensor_tensor(V_n[0:TP, :, :], V_n[0:TP, :, :],
                                    gspread[0:TP, :].unsqueeze(1).to_broadcast([TP, TILES, C]),
                                    ALU.mult).then_inc(o_dve, 1)
            dve.wait_ge(n_deg, 1)
            inverse_root_dve(dve, bank(6)[0:TP, 0:2 * TILES].rearrange("p (t n) -> p t n", n=2)[:, :, 0], 1.0)
            for t in range(TILES):
                nc.vector.tensor_scalar(H_n[0:TP, t, :], H_n[0:TP, t, :], rstd[0:TP, t:t + 1], None,
                                        ALU.mult).then_inc(n_hs, 1)
            dve.wait_ge(n_hs, TILES)

            def gcn_row(n):
                dve.wait_ge(n_agg, n + 1)
                if n >= 2:
                    dve.wait_ge(n_tr, n - 1)
                row = prod[n % 2][0:TP, :]
                link(dve, nc.vector.tensor_tensor(row, bank(n % 2)[0:TP, :], H_n[0:TP, n, :], ALU.add))
                nc.vector.scalar_tensor_tensor(out=row, in0=row, scalar=rstd[0:TP, n:n + 1], in1=bgcn[0:TP, :],
                                               op0=ALU.mult, op1=ALU.add).then_inc(n_row, 1)

            def add(n):
                t = n % TILES
                dve.wait_ge(n_out, n + 1)
                if n >= TILES:
                    dve.wait_ge(n_x, t + 1)
                nc.vector.tensor_tensor(X[0:TP, t, :], bank(4 + n % 2)[0:TP, :], X[0:TP, t, :],
                                        ALU.add).then_inc(n_x, 1)
                if n > TILES:
                    dve.wait_ge(n_x, n)
                    gather_stats(X, t - 1)

            gcn_row(0)
            gcn_row(1)
            for n in range(2 * TILES):
                if n + 2 < TILES:
                    gcn_row(n + 2)
                add(n)
            dve.wait_ge(n_x, 2 * TILES)
            leave_stage(dve, "DVE")

        def l1_act(act):
            ln_stats_act(act)
            for t in range(TILES):
                act.wait_ge(n_tz, t + 1)
                if t >= 2:
                    act.wait_ge(n_proj, 4 * t - 4)
                nc.scalar.activation(zT_n[t % 2], chunks(bank(t % 2)[:, :], TP), ACT.Copy).then_inc(n_zT, 1)
            for r in range(2):
                act.wait_ge(o_pe, 4 * r + 1)
                for b in range(3):
                    n = min(4, TILES - 4 * b)
                    last = nc.scalar.activation(
                        wT_v[0:8, 4 * b:4 * b + n, :],
                        bank(b)[0:8, 0:128 * n].rearrange("p (b n) -> p b n", n=128)[:, :, 0:TP], ACT.Copy)
                last.then_inc(o_act, 1)
                act.wait_ge(o_dve, 4 * r + 2)
                nc.scalar.activation(wT_n[0:8, :], wT_n[0:8, :], ACT.Exp, bias=st_n[0:8, 1:2], scale=DH ** -0.5,
                                     accum_out=st_n[0:8, 2:3]).then_inc(o_act, 1)
                act.wait_ge(o_pe, 4 * r + 2)
                nc.scalar.activation(wtok[0:TP, :], bank(3)[0:TP, 0:TILES * HEADS], ACT.Copy).then_inc(o_act, 1)
            ln_stats_act(act)
            for n in range(2 * TILES):
                act.wait_ge(n_tr, n + 1)
                if n >= 2:
                    act.wait_ge(n_out, n - 1)
                nc.scalar.activation(zT_n[n % 2], chunks(bank(2 + n % 2)[:, :], TP), ACT.Copy).then_inc(n_rT, 1)
            leave_stage(act, "ACT")

        def l1_pe(pe):
            pe.wait_ge(s_wn, 16 * 7)

            def turn_z(t):
                if t >= 2:
                    pe.wait_ge(n_zT, t - 1)
                pe.wait_ge(s_xn, TILES + t + 1)
                transpose_tile(chunks(bank(t % 2)[:, :], TP), XN[0:TP, t, :]).then_inc(n_tz, 1)

            turn_z(0)
            for t in range(TILES):
                if t + 1 < TILES:
                    turn_z(t + 1)
                pe.wait_ge(n_zT, t + 1)
                for j in range(4):
                    if t >= 1:
                        pe.wait_ge(n_ev, 4 * t - 3 + j)
                    w = wgcn if j == 0 else wqkv[:, :, (j - 1) * C:j * C]
                    project(bank(2 + j)[0:TP, :], zT_n[t % 2], w).then_inc(n_proj, 1)
            for r in range(2):
                pe.wait_ge(o_dve, 4 * r + 1)
                for t in range(TILES):
                    last = nc.tensor.transpose(banks[0:HEADS, 128 * t:128 * t + TP],
                                               logit[0:TP, HEADS * t:HEADS * (t + 1)], ident[0:TP, 0:TP])
                last.then_inc(o_pe, 1)
                pe.wait_ge(o_dve, 4 * r + 3)
                for t in range(TILES):
                    last = nc.tensor.transpose(bank(3)[0:TP, HEADS * t:HEADS * (t + 1)],
                                               wT_v[0:HEADS, t, :], ident[0:HEADS, 0:HEADS])
                last.then_inc(o_pe, 1)
                pe.wait_ge(o_act, 3 * r + 3)
                for t in range(TILES):
                    last = nc.tensor.matmul(bank(4)[0:HEADS, :], wtok[0:TP, HEADS * t:HEADS * (t + 1)],
                                            (Q_n, K_n)[r][0:TP, t, :], start=(t == 0), stop=(t == TILES - 1))
                last.then_inc(o_pe, 1)
                pe.wait_ge(o_dve, 4 * r + 4)
                nc.tensor.matmul(bank(5)[0:TP, :], ones[0:HEADS, 0:TP], gmask[0:HEADS, :],
                                 start=True, stop=True).then_inc(o_pe, 1)
            pe.wait_ge(s_an, 16 * TILES)
            pe.wait_ge(s_wn2, 16 * 2)
            for b in range(TILES):
                for t in range(TILES):
                    last = nc.tensor.matmul(bank(6)[0:TP, 2 * b:2 * b + 2], adj[t][:, tok(b)], ones[0:TP, 0:2],
                                            start=(t == 0), stop=(t == TILES - 1))
            last.then_inc(n_deg, 1)

            def aggregate(n):
                if n >= 2:
                    pe.wait_ge(n_row, n - 1)
                for t in range(TILES):
                    pe.wait_ge(n_hs, t + 1)
                    last = nc.tensor.matmul(bank(n % 2)[0:TP, :], adj[t][:, tok(n)], H_n[0:TP, t, :],
                                            start=(t == 0), stop=(t == TILES - 1))
                last.then_inc(n_agg, 1)

            def turn(n):
                if n < TILES:
                    pe.wait_ge(n_row, n + 1)
                else:
                    pe.wait_ge(o_dve, 9)
                if n >= 2:
                    pe.wait_ge(n_rT, n - 1)
                row = prod[n % 2][0:TP, :] if n < TILES else V_n[0:TP, n - TILES, :]
                transpose_tile(chunks(bank(2 + n % 2)[:, :], TP), row).then_inc(n_tr, 1)

            def out(n):
                pe.wait_ge(n_rT, n + 1)
                if n >= 2:
                    pe.wait_ge(n_x, n - 1)
                project(bank(4 + n % 2)[0:TP, :], zT_n[n % 2], wdense if n < TILES else wproj).then_inc(n_out, 1)

            aggregate(0)
            for n in range(2 * TILES):
                if n + 1 < TILES:
                    aggregate(n + 1)
                turn(n)
                if n >= 1:
                    out(n - 1)
            out(2 * TILES - 1)
            leave_stage(pe, "PE")

        PAIR_CELLS = TOPK * TOPK
        mem = Space(SLOT * 5, 7 * SLOT)
        wq_p, down_p = chunks(mem.take(KC * C), C), chunks(mem.take(KC * PAIR_CELLS), PAIR_CELLS)
        keys_p = [mem.take(4 * KEYS) for _ in range(2)]
        up_p = chunks(mem.take(2 * C), C, 2)
        mem = Space(SLOT * 2, 5 * SLOT)
        zT_p, qT_p = ([chunks(mem.take(KC * TP)) for _ in range(2)] for _ in range(2))
        R_p = mem.take(HEADS * KEYS)
        S_p = [mem.take(HEADS * PAIR_CELLS) for _ in range(2)]
        M_p = [mem.take(HEADS * PAIR_CELLS) for _ in range(2)]
        G_p = [mem.take(PAIR_CELLS) for _ in range(4)]
        gw_p = mem.take(PAIR_CELLS)
        gwT_p = chunks(mem.take(2 * TP), TP, 2)
        v0_p, i0_p, f0_p = ([mem.take(HEADS * TOPK) for _ in range(2)] for _ in range(3))
        top_p, shift_p = ([mem.take(HEADS * TOPK) for _ in range(2)] for _ in range(2))
        nmax_p, rsum_p = ([mem.take(HEADS) for _ in range(2)] for _ in range(2))
        s_wp = sem("peer_weights_loaded")
        p_q = sem("peer_q_ready")
        p_qT = sem("peer_qT_copied")
        p_h = sem("peer_hidden_ready")
        p_g = sem("peer_gelu_ready")
        p_s = sem("peer_similarities_ready")
        p_sr = sem("peer_similarities_read")
        p_top = sem("peer_tops_ready")
        p_e = sem("peer_exponentials_ready")
        p_f = sem("peer_keys_chosen")
        p_sp = sem("peer_pair_sums_ready")
        p_w = sem("peer_weights_masked")
        p_ws = sem("peer_weights_summed")
        p_gw = sem("peer_weighted_gelu_ready")
        s_out = sem("out_stored")
        Z0, R0 = TILES, 2 * TILES

        def peer_sp(sp):
            sp.wait_ge(o_dve, 9)
            for w, n in ((wq_p, "w_q"), (down_p, "down"), (up_p, "up")):
                sp.dma_start(w.rearrange("p k n -> p (k n)"), d["L1_ffn_" + n]).then_inc(s_wp, 16)
            sp.wait_ge(s_zeroed, 3)
            for h in range(HEADS):
                p = h % 4
                sp.dma_start(keys_p[h // 4][32 * p:32 * p + 32, KEYS * p:KEYS * (p + 1)],
                             d["L1_ffn_keys"][32 * h:32 * h + 32, :]).then_inc(s_wp, 16)
            for t in range(TILES):
                sp.wait_ge(n_x, R0 + t + 1)
                sp.dma_start(d["out"][tok(t), :], X[0:TP, t, :]).then_inc(s_out, 16)
            sp.wait_ge(s_out, 16 * TILES)

        def peer_pool(pool):
            pool.wait_ge(o_dve, 9)
            for w in keys_p:
                last = nc.gpsimd.memset(w, 0.0)
            last.then_inc(s_zeroed, 1)
            for t in range(TILES + 1):
                if t < TILES:
                    pool.wait_ge(p_f, t + 1)
                    if t >= 2:
                        pool.wait_ge(p_ws, t - 1)
                    nc.gpsimd.tensor_tensor(
                        S_p[t % 2][0:TP, :].rearrange("p (h a b) -> p h a b", h=HEADS, a=TOPK),
                        v0_p[t % 2][0:TP, :].rearrange("p (h a) -> p h a", a=TOPK).unsqueeze(3)
                        .to_broadcast([TP, HEADS, TOPK, TOPK]),
                        f0_p[t % 2][0:TP, :].rearrange("p (h b) -> p h b", b=TOPK).unsqueeze(2)
                        .to_broadcast([TP, HEADS, TOPK, TOPK]), ALU.add).then_inc(p_sp, 1)
                if t >= 1:
                    S, M = S_p[(t - 1) % 2][0:TP, :], M_p[(t - 1) % 2][0:TP, :]
                    pool.wait_ge(p_top, 2 * t - 1)
                    nc.gpsimd.tensor_scalar(M, M, LOWEST, None, ALU.is_equal).then_inc(p_w, 1)
                    pool.wait_ge(p_w, 2 * t - 1)
                    pool.wait_ge(p_e, 2 * t)
                    nc.gpsimd.tensor_tensor(S, S, M, ALU.mult).then_inc(p_w, 1)

        def peer_dve(dve):
            ln_stats_dve(dve, X, 1e-5, gathered=True)
            for t in range(TILES):
                normalize(XN[0:TP, t, :], X[0:TP, t, :], t).then_inc(s_xn, 1)
            hs = range(HEADS)

            def sims(h):
                return bank(4 + h // 2)[0:TP, KEYS * (h % 2):KEYS * (h % 2 + 1)]

            def cells(m, h):
                return m[0:TP, PAIR_CELLS * h:PAIR_CELLS * (h + 1)]

            def eight(m, h, a):
                return m[0:TP, TOPK * h + 8 * a:TOPK * h + 8 * a + 8]

            def by_head(m, n):
                return m[0:TP, :].rearrange("p (h n) -> p h n", n=n)

            def largest_keys(t):
                dve.wait_ge(p_s, t + 1)
                for h in hs:
                    last = nc.vector.max(eight(v0_p[t % 2], h, 0), sims(h))
                link(dve, last)

            def next_keys(t):
                for h in hs:
                    nc.vector.match_replace(cells(R_p, h), eight(v0_p[t % 2], h, 0), sims(h), LOWEST)
                    last = nc.vector.max_index(eight(i0_p[t % 2], h, 0).bitcast(U32), eight(v0_p[t % 2], h, 0), sims(h))
                last.then_inc(p_sr, 1)
                dve.wait_ge(p_sr, t + 1)
                for h in hs:
                    last = nc.vector.max(eight(v0_p[t % 2], h, 1), cells(R_p, h))
                link(dve, last)
                for h in hs:
                    last = nc.vector.max_index(eight(i0_p[t % 2], h, 1).bitcast(U32), eight(v0_p[t % 2], h, 1), cells(R_p, h))
                link(dve, last)
                nc.vector.tensor_copy(f0_p[t % 2][0:TP, :], i0_p[t % 2][0:TP, :].bitcast(U32)).then_inc(p_f, 1)

            def pairs(t):
                S, M, top = S_p[t % 2], M_p[t % 2], top_p[t % 2]
                dve.wait_ge(p_sp, t + 1)
                for h in hs:
                    last = nc.vector.max(eight(top, h, 0), cells(S, h))
                link(dve, last)
                for h in hs:
                    last = nc.vector.match_replace(cells(M, h), eight(top, h, 0), cells(S, h), LOWEST)
                link(dve, last)
                for h in hs:
                    last = nc.vector.max(eight(top, h, 1), cells(M, h))
                link(dve, last)
                for h in hs:
                    nc.vector.match_replace(cells(M, h), eight(top, h, 1), cells(M, h), LOWEST)
                largest = by_head(top, TOPK)[:, :, 0:1]
                nc.vector.tensor_scalar(nmax_p[t % 2][0:TP, :], largest[:, :, 0], -1.0, None, ALU.mult)
                nc.vector.tensor_tensor(by_head(shift_p[t % 2], TOPK), by_head(top, TOPK),
                                        largest.to_broadcast([TP, HEADS, TOPK]), ALU.subtract).then_inc(p_top, 1)

            def sums(t):
                dve.wait_ge(p_e, 2 * t + 1)
                link(dve, nc.vector.tensor_reduce(rsum_p[t % 2][0:TP, :], by_head(shift_p[t % 2], TOPK),
                                                  AX_X, ALU.add))
                nc.vector.reciprocal(rsum_p[t % 2][0:TP, :], rsum_p[t % 2][0:TP, :]).then_inc(p_top, 1)

            def weigh(t):
                dve.wait_ge(p_ws, t + 1)
                dve.wait_ge(p_g, t + 1)
                nc.vector.tensor_tensor(gw_p[0:TP, :], G_p[t % 4][0:TP, :], bank(3)[0:TP, 0:PAIR_CELLS],
                                        ALU.mult).then_inc(p_gw, 1)

            def add(t):
                dve.wait_ge(n_out, R0 + t + 1)
                nc.vector.tensor_tensor(X[0:TP, t, :], bank(3)[0:TP, :], X[0:TP, t, :], ALU.add).then_inc(n_x, 1)

            largest_keys(0)
            next_keys(0)
            for t in range(TILES):
                if t + 1 < TILES:
                    largest_keys(t + 1)
                pairs(t)
                if t >= 1:
                    weigh(t - 1)
                if t + 1 < TILES:
                    next_keys(t + 1)
                sums(t)
                if t >= 1:
                    add(t - 1)
            weigh(TILES - 1)
            add(TILES - 1)

        def peer_act(act):
            ln_stats_act(act)
            bn_scale = 1.0 / (1.0 + 1e-5) ** 0.5

            def prepare(t):
                act.wait_ge(n_tz, Z0 + t + 1)
                if t >= 2:
                    act.wait_ge(p_q, t - 1)
                nc.scalar.activation(zT_p[t % 2], chunks(bank(0)[:, :], TP), ACT.Copy).then_inc(n_zT, 1)
                act.wait_ge(p_q, t + 1)
                if t >= 2:
                    act.wait_ge(p_s, t - 1)
                nc.scalar.activation(qT_p[t % 2], chunks(bank(1)[:, :], TP), ACT.Copy,
                                     scale=bn_scale).then_inc(p_qT, 1)
                act.wait_ge(p_h, t + 1)
                if t >= 4:
                    act.wait_ge(p_gw, t - 3)
                nc.scalar.activation(G_p[t % 4][0:TP, :], bank(2)[0:TP, 0:PAIR_CELLS],
                                     ACT.Gelu_apprx_tanh).then_inc(p_g, 1)

            def turned(t):
                act.wait_ge(n_tr, R0 + t + 1)
                nc.scalar.activation(gwT_p, chunks(bank(3)[:, :], TP, 2), ACT.Copy).then_inc(n_rT, 1)

            prepare(0)
            prepare(1)
            for t in range(TILES):
                if t + 2 < TILES:
                    prepare(t + 2)
                S = S_p[t % 2]
                act.wait_ge(p_top, 2 * t + 1)
                nc.scalar.activation(shift_p[t % 2][0:TP, :], shift_p[t % 2][0:TP, :], ACT.Exp).then_inc(p_e, 1)
                for h in range(HEADS):
                    c = slice(PAIR_CELLS * h, PAIR_CELLS * (h + 1))
                    last = nc.scalar.activation(S[0:TP, c], S[0:TP, c], ACT.Exp, bias=nmax_p[t % 2][0:TP, h:h + 1])
                act_link(act, last)
                if t >= 1:
                    turned(t - 1)
                act.wait_ge(p_top, 2 * t + 2)
                for h in range(HEADS):
                    c = slice(PAIR_CELLS * h, PAIR_CELLS * (h + 1))
                    last = nc.scalar.activation(S[0:TP, c], S[0:TP, c], ACT.Copy, scale=rsum_p[t % 2][0:TP, h:h + 1])
                last.then_inc(p_e, 1)
            turned(TILES - 1)

        def peer_pe(pe):
            pe.wait_ge(s_wp, 16 * (3 + HEADS))

            def prepare(t):
                if t >= 1:
                    pe.wait_ge(n_zT, Z0 + t)
                pe.wait_ge(s_xn, 2 * TILES + t + 1)
                transpose_tile(chunks(bank(0)[:, :], TP), XN[0:TP, t, :]).then_inc(n_tz, 1)
                pe.wait_ge(n_zT, Z0 + t + 1)
                if t >= 1:
                    pe.wait_ge(p_qT, t)
                for m in range(KC):
                    for k in range(KC):
                        last = nc.tensor.matmul(bank(1)[:, m * TP:(m + 1) * TP], wq_p[:, k, m * 128:(m + 1) * 128],
                                                zT_p[t % 2][:, k, :], start=(k == 0), stop=(k == KC - 1))
                last.then_inc(p_q, 1)
                pe.wait_ge(p_qT, t + 1)
                if t >= 1:
                    pe.wait_ge(p_g, t)
                project(bank(2)[0:TP, 0:PAIR_CELLS], qT_p[t % 2], down_p, n=PAIR_CELLS).then_inc(p_h, 1)

            def similarities(t):
                pe.wait_ge(p_qT, t + 1)
                if t >= 1:
                    pe.wait_ge(p_sr, t)
                for b in range(HEADS // 2):
                    last = nc.tensor.matmul(bank(4 + b)[0:TP, :], qT_p[t % 2][:, b // 2, :],
                                            keys_p[b // 2][:, 2 * KEYS * (b % 2):2 * KEYS * (b % 2 + 1)],
                                            start=True, stop=True)
                last.then_inc(p_s, 1)

            def weights(t):
                pe.wait_ge(p_w, 2 * t + 2)
                if t >= 1:
                    pe.wait_ge(n_x, R0 + t)
                for h in range(HEADS):
                    last = nc.tensor.matmul(bank(3)[0:TP, 0:PAIR_CELLS], ident[0:TP, 0:TP],
                                            S_p[t % 2][0:TP, PAIR_CELLS * h:PAIR_CELLS * (h + 1)],
                                            start=(h == 0), stop=(h == HEADS - 1))
                last.then_inc(p_ws, 1)

            def out(t):
                pe.wait_ge(p_gw, t + 1)
                for k in range(2):
                    last = nc.tensor.transpose(bank(3)[:, k * TP:(k + 1) * TP], gw_p[0:TP, k * 128:(k + 1) * 128],
                                               ident[0:TP, 0:TP])
                last.then_inc(n_tr, 1)
                pe.wait_ge(n_rT, R0 + t + 1)
                project(bank(3)[0:TP, :], gwT_p, up_p, k=2).then_inc(n_out, 1)

            prepare(0)
            similarities(0)
            prepare(1)
            for t in range(TILES):
                if t + 1 < TILES:
                    similarities(t + 1)
                if t + 2 < TILES:
                    prepare(t + 2)
                if t >= 1:
                    weights(t - 1)
                    out(t - 1)
            weights(TILES - 1)
            out(TILES - 1)

        block = ctx.enter_context(nc.Block())

        @block.sync
        def _(sp):
            const_sp(sp)
            key_rows_sp(sp)
            gnn_w_sp(sp)
            zero_table(sp)
            mix_sp(sp)
            mix_bias_sp(sp)
            gnn_sp(sp)
            att_sp(sp)
            ff_sp(sp)
            ffn_sp(sp)
            expert_sp(sp)
            l1_sp(sp)
            peer_sp(sp)

        @block.gpsimd
        def _(pool):
            const_pool(pool)
            edges_pool(pool)
            causal_pool(pool)
            peer_pool(pool)

        @block.scalar
        def _(act):
            edges_act(act)
            mix_act(act)
            gnn_act(act)
            att_act(act)
            ff_act(act)
            ffn_act(act)
            causal_act(act)
            expert_act(act)
            l1_act(act)
            peer_act(act)

        @block.vector
        def _(dve):
            edges_dve(dve)
            mix_dve(dve)
            gnn_dve(dve)
            att_dve(dve)
            ff_dve(dve)
            ffn_dve(dve)
            causal_dve(dve)
            expert_dve(dve)
            l1_dve(dve)
            peer_dve(dve)

        @block.tensor
        def _(pe):
            edges_pe(pe)
            mix_pe(pe)
            gnn_pe(pe)
            att_pe(pe)
            ff_pe(pe)
            ffn_pe(pe)
            causal_pe(pe)
            expert_pe(pe)
            l1_pe(pe)
            peer_pe(pe)




def scratch(nc, d):
    d["table"] = nc.dram_tensor("edge_table", (TABLE_ROWS, ROW), F32).ap()
    d["key_rows"] = nc.dram_tensor("key_rows", (EC, TP), F32).ap()
    d["x_kept"] = nc.dram_tensor("x_kept", (NODES, C), F32).ap()
    d["adj"] = nc.dram_tensor("adjacency", (NODES, NODES), F32).ap()


def lay_out(a):
    import numpy as np

    def w4(w):
        k = w.shape[0] // 128
        return np.ascontiguousarray(w.reshape(k, 128, -1).transpose(1, 0, 2).reshape(128, -1))

    def row(v):
        return np.ascontiguousarray(v.reshape(1, -1))

    def col(v):
        return np.ascontiguousarray(v.reshape(-1, 128).T)

    a = {k: np.asarray(v) for k, v in a.items()}
    o = {"x": np.ascontiguousarray(a["x"]),
         "src": np.ascontiguousarray(a["src"].reshape(TP, EC)),
         "dst": np.ascontiguousarray(a["dst"].reshape(TP, EC)),
         "edge_attr_8": np.ascontiguousarray(a["edge_attr_8"].reshape(TP, EC * HEADS))}
    for n in ("Wq", "Wk", "Wv", "Wo", "W1", "W2"):
        o["L0_gnn_" + n] = w4(a["L0_gnn_" + n].T)
    for n in ("bq", "bk", "bv", "bo", "b2"):
        o["L0_gnn_" + n] = row(a["L0_gnn_" + n])
    for n in ("ln_att_g", "ln_att_b", "ln_ff_g", "ln_ff_b", "b1"):
        o["L0_gnn_" + n] = col(a["L0_gnn_" + n])
    for n in ("Wq", "Wk", "Wv", "Wo", "W1", "W2"):
        w = a["L0_mix_" + n]
        if n == "Wo":
            w = w.reshape(C, C)
        o["L0_mix_" + n] = w4(w.reshape(w.shape[0], -1))
    for n in ("bq", "bk", "bv", "bo", "ln1_scale", "ln1_bias", "b2", "ln2_scale", "ln2_bias"):
        o["L0_mix_" + n] = row(a["L0_mix_" + n])
    o["L0_mix_b1"] = col(a["L0_mix_b1"])
    for n in ("Wq", "Wk", "Wv", "Wo", "gate_W"):
        o["L0_ffn_" + n] = w4(a["L0_ffn_" + n])
    for n in ("ln_g", "ln_b"):
        o["L0_ffn_" + n] = col(a["L0_ffn_" + n])
    for n in ("qn_g", "kn_g"):
        o["L0_ffn_" + n] = np.ascontiguousarray(np.tile(a["L0_ffn_" + n], 2).reshape(128, 1))
    o["L0_ffn_gate_b"] = row(a["L0_ffn_gate_b"])
    o["L0_ffn_W1"] = w4(a["L0_ffn_W1"].transpose(1, 0, 2).reshape(C, EXPERTS * FF))
    o["L0_ffn_b1"] = col(a["L0_ffn_b1"])
    o["L0_ffn_W2"] = w4(a["L0_ffn_W2"].reshape(EXPERTS * FF, C))
    o["L0_ffn_b2"] = np.ascontiguousarray(a["L0_ffn_b2"])
    o["L1_gnn_W_gcn"], o["L1_gnn_W_dense"] = w4(a["L1_gnn_W_gcn"]), w4(a["L1_gnn_W_dense"])
    o["L1_gnn_b_gcn"], o["L1_gnn_b_dense"] = row(a["L1_gnn_b_gcn"]), row(a["L1_gnn_b_dense"])
    o["L1_mix_w_qkv"] = w4(a["L1_mix_w_qkv"].T)
    o["L1_mix_w_proj"] = w4(a["L1_mix_w_proj"].T)
    for n in ("b_proj", "w_q", "w_k"):
        o["L1_mix_" + n] = row(a["L1_mix_" + n])
    o["L1_ffn_w_q"] = w4(a["L1_ffn_w_q"])
    o["L1_ffn_keys"] = np.ascontiguousarray(a["L1_ffn_keys"][:, :, 0, :].transpose(0, 2, 1).reshape(HEADS * 32, KEYS))
    o["L1_ffn_down"] = w4(a["L1_ffn_weight_down_embed"][:TOPK * TOPK].T)
    o["L1_ffn_up"] = w4(a["L1_ffn_weight_up_embed"][:TOPK * TOPK])
    return o


def kernel(**inputs):
    import concourse.bacc as bacc
    from concourse import mybir as mb
    from concourse.bass_utils import run_bass_kernel_spmd

    arrays = lay_out(inputs)
    nc = bacc.Bacc("TRN2", target_bir_lowering=False, num_devices=1)
    d = {k: nc.dram_tensor(k, v.shape, mb.dt.from_np(v.dtype), kind="ExternalInput").ap()
         for k, v in arrays.items()}
    scratch(nc, d)
    d["out"] = nc.dram_tensor("out", (NODES, C), F32, kind="ExternalOutput").ap()
    gps_two_layers(nc, d)
    r = run_bass_kernel_spmd(nc, [arrays], core_ids=[0])
    return r.results[0]["out"]
```
